# Optimizing a Trainium2 kernel written in Bass

```python
import numpy as np
import jax
import jax.numpy as jnp

def _softmax(x, axis=-1):
    return jax.nn.softmax(x, axis=axis)

def _gelu(x):
    return jax.nn.gelu(x, approximate=True)

def _silu(x):
    return jax.nn.silu(x)

def _sigmoid(x):
    return jax.nn.sigmoid(x)

def _layernorm(x, axis=-1, eps=1e-05):
    m = jnp.mean(x, axis=axis, keepdims=True)
    v = jnp.var(x, axis=axis, keepdims=True)
    return (x - m) / jnp.sqrt(v + eps)

def _scatter_add(tgt, idx, src, axis=0):
    return tgt.at[idx].add(src)

def _segment_sum(src, seg, n):
    return jax.ops.segment_sum(src, seg, n)
kernel_name = 'mk_gnn_preln_d4_gnn_r64_ff1ae7'

def setup_inputs(seed: int=0):
    np.random.seed(seed)
    _w = jnp.asarray

    def _rec_inputs():
        import jax
        import jax.numpy as jnp
        _gk = jax.random.key(seed)
        x = -0.0008691 + 1 * jax.random.normal(jax.random.fold_in(_gk, 1), (50000, 128), jnp.float32)
        src = jax.random.randint(jax.random.fold_in(_gk, 2), (25000,), 0, 50000, jnp.int32)
        dst = jnp.minimum((50000 * jax.random.uniform(jax.random.fold_in(_gk, 3), (25000,)) ** 2.0).astype(jnp.int32), 49999)
        _o = jnp.argsort(dst, stable=True)
        src = src[_o]
        dst = dst[_o]
        edge_attr_16 = 0.000130101 + 1.00012 * jax.random.normal(jax.random.fold_in(_gk, 11), (25000, 16), jnp.float32)
        edge_type_2 = jax.random.randint(jax.random.fold_in(_gk, 13), (25000,), 0, 2, jnp.int32)
        edge_type_4 = jax.random.randint(jax.random.fold_in(_gk, 14), (25000,), 0, 4, jnp.int32)
        return (x, src, dst, edge_attr_16, edge_type_2, edge_type_4)
    x, src, dst, edge_attr_16, edge_type_2, edge_type_4 = _rec_inputs()

    def _L0_gnn_setup():
        import jax, jax.numpy as jnp
        import numpy as np
        HEADS = 2
        NEG_SLOPE = 0.2
        EPS = 1e-16

        def _gat_layer(x, src, dst, edge_attr_full, W, att, b, ew, eb):
            N, D = x.shape
            H = HEADS
            edge_emb = edge_attr_full @ ew.T + eb
            xw = x @ W
            xj = xw[src].reshape(-1, H, D) + edge_emb.reshape(-1, H, D)
            xi = xw[dst].reshape(-1, H, D)
            att_i, att_j = (att[:, :D], att[:, D:])
            alpha = jnp.einsum('ehd,hd->eh', xi, att_i) + jnp.einsum('ehd,hd->eh', xj, att_j)
            alpha = jax.nn.leaky_relu(alpha, NEG_SLOPE)
            amax = jax.ops.segment_max(alpha, dst, num_segments=N)
            ea = jnp.exp(alpha - amax[dst])
            denom = jax.ops.segment_sum(ea, dst, num_segments=N)
            alpha = ea / (denom[dst] + EPS)
            msg = xj * alpha[..., None]
            aggr = jax.ops.segment_sum(msg, dst, num_segments=N)
            return aggr.mean(axis=1) + b
        N, E, D, F = (10000, 5000, 128, 16)
        key = jax.random.key(seed)
        ks = jax.random.split(key, 8)
        return {'x': jax.random.normal(ks[0], (N, D), dtype=jnp.float32), 'edge_index': jax.random.randint(ks[1], (2, E), 0, N, dtype=jnp.int64), 'edge_attr': jax.random.normal(ks[2], (E, F), dtype=jnp.float32), 'weights': jax.random.normal(ks[3], (5, D, HEADS * D), dtype=jnp.float32) * 0.08, 'atts': jax.random.normal(ks[4], (5, HEADS, 2 * D), dtype=jnp.float32) * 0.08, 'biases': jnp.zeros((5, D), dtype=jnp.float32), 'edge_ws': jax.random.normal(ks[5], (5, HEADS * D, F), dtype=jnp.float32) * 0.2, 'edge_bs': jnp.zeros((5, HEADS * D), dtype=jnp.float32)}
    _L0_gnn_all = _L0_gnn_setup()
    _L0_gnn_in = {k: v for k, v in _L0_gnn_all.items() if k in ('weights', 'atts', 'biases', 'edge_ws', 'edge_bs')}
    del _L0_gnn_all

    def _L1_gnn_setup():
        import jax, jax.numpy as jnp
        import numpy as np
        N, E, C, H = (100000, 9375, 128, 8)
        D = C // H
        REL_EDGE_TYPE = (1, 0)
        key = jax.random.key(seed)
        ks = jax.random.split(key, 16)
        s = 1.0 / np.sqrt(C)
        sd = 1.0 / np.sqrt(D)
        return {'x': jax.random.normal(ks[0], (N, C), jnp.float32), 'edge_index': jax.random.randint(ks[1], (2, E), 0, N), 'edge_type': jax.random.randint(ks[2], (E,), 0, 2), 'Wk': jax.random.normal(ks[3], (C, C), jnp.float32) * s, 'bk': jnp.zeros((C,), jnp.float32), 'Wq': jax.random.normal(ks[4], (C, C), jnp.float32) * s, 'bq': jnp.zeros((C,), jnp.float32), 'Wv': jax.random.normal(ks[5], (C, C), jnp.float32) * s, 'bv': jnp.zeros((C,), jnp.float32), 'a_rel': jax.random.normal(ks[6], (2, H, D, D), jnp.float32) * sd, 'm_rel': jax.random.normal(ks[7], (2, H, D, D), jnp.float32) * sd, 'p_rel': jnp.ones((2, H), jnp.float32), 'Wa': jax.random.normal(ks[8], (C, C), jnp.float32) * s, 'ba': jnp.zeros((C,), jnp.float32), 'skip': jnp.zeros((), jnp.float32)}
    _L1_gnn_all = _L1_gnn_setup()
    _L1_gnn_in = {k: v for k, v in _L1_gnn_all.items() if k in ('Wk', 'bk', 'Wq', 'bq', 'Wv', 'bv', 'a_rel', 'm_rel', 'p_rel', 'Wa', 'ba', 'skip')}
    del _L1_gnn_all

    def _L2_gnn_setup():
        import jax, jax.numpy as jnp
        import numpy as np
        N_NODES = 50000
        N_EDGES = 12500
        IN_FEAT = 128
        OUT_FEAT = 128
        key = jax.random.key(seed)
        k1, k2, k3 = jax.random.split(key, 3)
        x = jax.random.normal(k1, (N_NODES, IN_FEAT), dtype=jnp.float32)
        edge_index = jax.random.randint(k2, (2, N_EDGES), 0, N_NODES, dtype=jnp.int32)
        limit = np.sqrt(6.0 / (IN_FEAT + OUT_FEAT)).astype(np.float32)
        W = jax.random.uniform(k3, (IN_FEAT, OUT_FEAT), minval=-limit, maxval=limit, dtype=jnp.float32)
        b = jnp.zeros((OUT_FEAT,), dtype=jnp.float32)
        return {'x': x, 'edge_index': edge_index, 'W': W, 'b': b}
    _L2_gnn_all = _L2_gnn_setup()
    _L2_gnn_in = {k: v for k, v in _L2_gnn_all.items() if k in ('W', 'b')}
    del _L2_gnn_all

    def _L3_gnn_setup():
        import jax, jax.numpy as jnp
        import numpy as np
        N_NODES = 50000
        N_EDGES = 12500
        IN_CH = 128
        OUT_CH = 32
        HEADS = 4
        N_TYPES = 4
        N_CONF = 5
        key = jax.random.key(seed)
        ks = jax.random.split(key, 8)
        x = jax.random.normal(ks[0], (N_NODES, IN_CH), dtype=jnp.float32)
        edge_index = jax.random.randint(ks[1], (2, N_EDGES), 0, N_NODES, dtype=jnp.int32)
        edge_types = jax.random.randint(ks[2], (N_EDGES,), 0, N_TYPES, dtype=jnp.int32)
        D = OUT_CH * HEADS
        W = jax.random.normal(ks[3], (N_TYPES, IN_CH, D), dtype=jnp.float32) * (1.0 / np.sqrt(IN_CH))
        att_vectors = jax.random.normal(ks[4], (N_CONF, HEADS, 2 * OUT_CH), dtype=jnp.float32) * 0.1
        confounder_probs = jax.random.uniform(ks[5], (N_CONF,), dtype=jnp.float32)
        edge_importance = jnp.array([2.0, 1.5, 1.0, 0.5], dtype=jnp.float32)
        bias = jnp.zeros((D,), dtype=jnp.float32)
        return {'x': x, 'edge_index': edge_index, 'edge_types': edge_types, 'W': W, 'att_vectors': att_vectors, 'confounder_probs': confounder_probs, 'edge_importance': edge_importance, 'bias': bias}
    _L3_gnn_all = _L3_gnn_setup()
    _L3_gnn_in = {k: v for k, v in _L3_gnn_all.items() if k in ('W', 'att_vectors', 'confounder_probs', 'edge_importance', 'bias')}
    del _L3_gnn_all
    return {'x': x, 'src': src, 'dst': dst, 'edge_attr_16': edge_attr_16, 'edge_type_2': edge_type_2, 'edge_type_4': edge_type_4, 'L0_gnn_weights': _L0_gnn_in['weights'], 'L0_gnn_atts': _L0_gnn_in['atts'], 'L0_gnn_biases': _L0_gnn_in['biases'], 'L0_gnn_edge_ws': _L0_gnn_in['edge_ws'], 'L0_gnn_edge_bs': _L0_gnn_in['edge_bs'], 'L1_gnn_Wk': _L1_gnn_in['Wk'], 'L1_gnn_bk': _L1_gnn_in['bk'], 'L1_gnn_Wq': _L1_gnn_in['Wq'], 'L1_gnn_bq': _L1_gnn_in['bq'], 'L1_gnn_Wv': _L1_gnn_in['Wv'], 'L1_gnn_bv': _L1_gnn_in['bv'], 'L1_gnn_a_rel': _L1_gnn_in['a_rel'], 'L1_gnn_m_rel': _L1_gnn_in['m_rel'], 'L1_gnn_p_rel': _L1_gnn_in['p_rel'], 'L1_gnn_Wa': _L1_gnn_in['Wa'], 'L1_gnn_ba': _L1_gnn_in['ba'], 'L1_gnn_skip': _L1_gnn_in['skip'], 'L2_gnn_W': _L2_gnn_in['W'], 'L2_gnn_b': _L2_gnn_in['b'], 'L3_gnn_W': _L3_gnn_in['W'], 'L3_gnn_att_vectors': _L3_gnn_in['att_vectors'], 'L3_gnn_confounder_probs': _L3_gnn_in['confounder_probs'], 'L3_gnn_edge_importance': _L3_gnn_in['edge_importance'], 'L3_gnn_bias': _L3_gnn_in['bias']}

def reference(x, src, dst, edge_attr_16, edge_type_2, edge_type_4, L0_gnn_weights, L0_gnn_atts, L0_gnn_biases, L0_gnn_edge_ws, L0_gnn_edge_bs, L1_gnn_Wk, L1_gnn_bk, L1_gnn_Wq, L1_gnn_bq, L1_gnn_Wv, L1_gnn_bv, L1_gnn_a_rel, L1_gnn_m_rel, L1_gnn_p_rel, L1_gnn_Wa, L1_gnn_ba, L1_gnn_skip, L2_gnn_W, L2_gnn_b, L3_gnn_W, L3_gnn_att_vectors, L3_gnn_confounder_probs, L3_gnn_edge_importance, L3_gnn_bias):
    import jax
    import jax.numpy as jnp

    def _L0_gnn_ref(x, edge_index, edge_attr, weights, atts, biases, edge_ws, edge_bs):
        import jax, jax.numpy as jnp
        import numpy as np
        HEADS = 2
        NEG_SLOPE = 0.2
        EPS = 1e-16

        def _gat_layer(x, src, dst, edge_attr_full, W, att, b, ew, eb):
            N, D = x.shape
            H = HEADS
            edge_emb = edge_attr_full @ ew.T + eb
            xw = x @ W
            xj = xw[src].reshape(-1, H, D) + edge_emb.reshape(-1, H, D)
            xi = xw[dst].reshape(-1, H, D)
            att_i, att_j = (att[:, :D], att[:, D:])
            alpha = jnp.einsum('ehd,hd->eh', xi, att_i) + jnp.einsum('ehd,hd->eh', xj, att_j)
            alpha = jax.nn.leaky_relu(alpha, NEG_SLOPE)
            amax = jax.ops.segment_max(alpha, dst, num_segments=N)
            ea = jnp.exp(alpha - amax[dst])
            denom = jax.ops.segment_sum(ea, dst, num_segments=N)
            alpha = ea / (denom[dst] + EPS)
            msg = xj * alpha[..., None]
            aggr = jax.ops.segment_sum(msg, dst, num_segments=N)
            return aggr.mean(axis=1) + b
        N = x.shape[0]
        E = edge_index.shape[1]
        F = edge_attr.shape[1]
        loop = jnp.arange(N, dtype=edge_index.dtype)
        src = jnp.concatenate([edge_index[0], loop])
        dst = jnp.concatenate([edge_index[1], loop])
        edge_attr_full = jnp.concatenate([edge_attr, jnp.zeros((N, F), dtype=edge_attr.dtype)], axis=0)
        h = x
        for l in range(5):
            h = _gat_layer(h, src, dst, edge_attr_full, weights[l], atts[l], biases[l], edge_ws[l], edge_bs[l])
            if l < 4:
                h = jax.nn.relu(h)
        return h

    def _L1_gnn_ref(x, edge_index, edge_type, Wk, bk, Wq, bq, Wv, bv, a_rel, m_rel, p_rel, Wa, ba, skip):
        import jax, jax.numpy as jnp
        import numpy as np
        N, E, C, H = (100000, 9375, 128, 8)
        D = C // H
        REL_EDGE_TYPE = (1, 0)
        n = x.shape[0]
        k = (x @ Wk + bk).reshape(n, H, D)
        q = (x @ Wq + bq).reshape(n, H, D)
        v = (x @ Wv + bv).reshape(n, H, D)
        src, dst = (edge_index[0], edge_index[1])
        q_dst = q[dst]
        scale = 1.0 / jnp.sqrt(jnp.asarray(D, x.dtype))
        out = jnp.zeros((n, H, D), x.dtype)
        for r in range(2):
            mask = edge_type == REL_EDGE_TYPE[r]
            k_r = jnp.einsum('nhd,hde->nhe', k, a_rel[r])
            v_r = jnp.einsum('nhd,hde->nhe', v, m_rel[r])
            score = jnp.sum(q_dst * k_r[src], axis=-1) * p_rel[r] * scale
            score = jnp.where(mask[:, None], score, -jnp.inf)
            m = jax.ops.segment_max(score, dst, num_segments=n)
            m = jnp.where(jnp.isfinite(m), m, 0.0)
            e = jnp.where(mask[:, None], jnp.exp(score - m[dst]), 0.0)
            den = jax.ops.segment_sum(e, dst, num_segments=n)
            alpha = e / jnp.where(den[dst] > 0, den[dst], 1.0)
            msg = v_r[src] * alpha[..., None]
            out = out + jax.ops.segment_sum(msg, dst, num_segments=n)
        out = out.reshape(n, C)
        out = jax.nn.gelu(out, approximate=False) @ Wa + ba
        a = jax.nn.sigmoid(skip)
        return a * out + (1.0 - a) * x

    def _L2_gnn_ref(x, edge_index, W, b):
        import jax, jax.numpy as jnp
        import numpy as np
        N_NODES = 50000
        N_EDGES = 12500
        IN_FEAT = 128
        OUT_FEAT = 128
        n = x.shape[0]
        loops = jnp.arange(n, dtype=edge_index.dtype)
        src = jnp.concatenate([edge_index[0], loops])
        dst = jnpp_concat = jnp.concatenate([edge_index[1], loops])
        deg = jax.ops.segment_sum(jnp.ones_like(dst, dtype=x.dtype), dst, num_segments=n)
        dinv = jnp.where(deg > 0, jax.lax.rsqrt(deg), 0.0)
        norm = dinv[src] * dinv[dst]
        h = x @ W
        msgs = h[src] * norm[:, None]
        out = jax.ops.segment_sum(msgs, dst, num_segments=n) + b
        return jax.nn.gelu(out, approximate=False)

    def _L3_gnn_ref(x, edge_index, edge_types, W, att_vectors, confounder_probs, edge_importance, bias):
        import jax, jax.numpy as jnp
        import numpy as np
        N_NODES = 50000
        N_EDGES = 12500
        IN_CH = 128
        OUT_CH = 32
        HEADS = 4
        N_TYPES = 4
        N_CONF = 5
        N = x.shape[0]
        T = W.shape[0]
        K, H, C2 = att_vectors.shape
        C = C2 // 2
        src = edge_index[0]
        dst = edge_index[1]
        et = edge_types.astype(jnp.int32)
        xt = jnp.einsum('ni,tio->tno', x, W)
        xj = xt[et, src].reshape(-1, H, C)
        xi = xt[et, dst].reshape(-1, H, C)
        x_cat = jnp.concatenate([xi, xj], axis=-1)
        scores = jnp.einsum('ehd,khd->ehk', x_cat, att_vectors)
        scores = jax.nn.leaky_relu(scores, negative_slope=0.2)
        pk = jax.nn.softmax(confounder_probs)
        alpha = jnp.einsum('ehk,k->eh', scores, pk)
        seg = et * N + dst
        n_seg = T * N
        m = jax.ops.segment_max(alpha, seg, num_segments=n_seg)
        a = jnp.exp(alpha - m[seg])
        denom = jax.ops.segment_sum(a, seg, num_segments=n_seg)
        alpha_n = a / denom[seg]
        msg = (xj * alpha_n[..., None]).reshape(-1, H * C)
        msg = msg * edge_importance[et][:, None]
        out = jax.ops.segment_sum(msg, dst, num_segments=N)
        out = out + x @ W[0] + bias
        return out
    edge_index = jnp.stack([src, dst])
    h = jnp.maximum(_layernorm(x, axis=-1), 0.0)
    x = x + _L0_gnn_ref(h, edge_index, edge_attr_16, L0_gnn_weights, L0_gnn_atts, L0_gnn_biases, L0_gnn_edge_ws, L0_gnn_edge_bs)
    h = jnp.maximum(_layernorm(x, axis=-1), 0.0)
    x = x + _L1_gnn_ref(h, edge_index, edge_type_2, L1_gnn_Wk, L1_gnn_bk, L1_gnn_Wq, L1_gnn_bq, L1_gnn_Wv, L1_gnn_bv, L1_gnn_a_rel, L1_gnn_m_rel, L1_gnn_p_rel, L1_gnn_Wa, L1_gnn_ba, L1_gnn_skip)
    h = jnp.maximum(_layernorm(x, axis=-1), 0.0)
    x = x + _L2_gnn_ref(h, edge_index, L2_gnn_W, L2_gnn_b)
    h = jnp.maximum(_layernorm(x, axis=-1), 0.0)
    x = x + _L3_gnn_ref(h, edge_index, edge_type_4, L3_gnn_W, L3_gnn_att_vectors, L3_gnn_confounder_probs, L3_gnn_edge_importance, L3_gnn_bias)
    return x

_drawn_inputs = setup_inputs


def setup_inputs(seed=0):
    import zlib

    import numpy as np

    out = dict(_drawn_inputs(seed))
    spreads = {'L0_gnn_biases': (0.0, 0.1),
     'L0_gnn_edge_bs': (0.0, 0.1),
     'L1_gnn_bk': (0.0, 0.8),
     'L1_gnn_bq': (0.0, 0.8),
     'L1_gnn_bv': (0.0, 0.554),
     'L1_gnn_p_rel': (1.0, 0.6),
     'L1_gnn_ba': (0.0, 0.1),
     'L2_gnn_b': (0.0, 0.1),
     'L3_gnn_bias': (0.0, 0.1)}
    factors = {'L1_gnn_Wk': 8.0,
     'L1_gnn_Wq': 8.0,
     'L1_gnn_a_rel': 8.0,
     'L3_gnn_att_vectors': 8.0,
     'L3_gnn_confounder_probs': 8.0}
    for name, (base, spread) in spreads.items():
        noise = np.random.default_rng([zlib.crc32(name.encode()), seed]).standard_normal(out[name].shape)
        drawn = base * np.exp(spread * noise) if base else spread * noise
        out[name] = jnp.asarray(drawn.astype(out[name].dtype))
    for name, factor in factors.items():
        out[name] = (out[name] * factor).astype(out[name].dtype)
    return out
```

```python
from collections import namedtuple
from contextlib import ExitStack

import concourse.bass as bass
from concourse import mybir

F32 = mybir.dt.float32
I32 = mybir.dt.int32
ALU = mybir.AluOpType
ACT = mybir.ActivationFunctionType
AX = mybir.AxisListType

P = 128
D = 128
TILES = 4
GROUP = TILES * P
ROWW = D + 4
GAT_HEADS = 2
GAT_LAYERS = 5
EDGE_F = 16
HGT_HEADS, HGT_RELS = 8, 2
CAT_HEADS, CAT_TYPES, CAT_CONF = 4, 4, 5
CAT_S = CAT_CONF * CAT_HEADS
LN_EPS = 1e-5
FAR = -3.0e38
NOWHERE = 1 << 20


class Order:

    def __init__(self, eng, sem):
        self.eng, self.sem, self.n = eng, sem, 0

    def __call__(self, instruction):
        instruction.then_inc(self.sem, 1)
        self.n += 1
        self.eng.wait_ge(self.sem, self.n)


def batch(i, n, extra):
    if isinstance(i, int):
        return [(g, g % 2) for g in (2 * i, 2 * i + 1) if g < n + extra]
    return [(i * 2, 0), (i * 2 + 1, 1)]


def batches(eng, n, extra=0):
    full = n // 2
    if full:
        with eng.Fori(0, full) as i:
            yield i, batch(i, n, extra)
    if batch(full, n, extra):
        yield full, batch(full, n, extra)


def batches_ahead(eng, n, extra=0):
    full = n // 2
    if full > 1:
        with eng.Fori(0, full - 1) as i:
            yield i, batch(i, n, extra), i + 1, batch(i + 1, n, extra)
    for i in range(max(full - 1, 0), full + 1):
        if batch(i, n, extra):
            yield i, batch(i, n, extra), i + 1, batch(i + 1, n, extra)


def tiles_of(g, n):
    return 1 if isinstance(g, int) and g == n else TILES



class LoopOrder:

    def __init__(self, eng, sem, per, i, before=0):
        self.eng, self.sem, self.per, self.i, self.before, self.n = eng, sem, per, i, before, 0

    def __call__(self, instruction):
        instruction.then_inc(self.sem, 1)
        self.n += 1
        self.eng.wait_ge(self.sem, self.i * self.per + self.before + self.n)

    def end(self):
        assert self.n == self.per, (self.n, self.per)


def done(g):
    return g + 3


def freed(g):
    return g + 1


def broadcast(ap, n):
    return bass.AP(tensor=ap.tensor, offset=ap.offset, ap=list(ap.ap) + [[0, n]])


def spread(ap, axis, n):
    wide = ap.unsqueeze(axis)
    shape = list(wide.shape)
    shape[axis] = n
    return wide.broadcast_to(shape)


def named(items):
    return namedtuple("Named", items.keys())(*items.values())


class Buffers:

    def __init__(self, nc, ctx, tag):
        self.nc, self.ctx, self.tag, self.taken = nc, ctx, tag, []
        ctx.callback(self.give_back)

    def sb(self, name, shape, dt=F32):
        return self.ctx.enter_context(self.nc.sbuf_tensor(f"{self.tag}_{name}", shape, dt))

    def ps(self, name, shape):
        return self.ctx.enter_context(self.nc.psum_tensor(f"{self.tag}_{name}", shape, F32))

    def sem(self, name):
        self.taken.append(self.nc.alloc_semaphore(f"{self.tag}_{name}"))
        return self.taken[-1]

    def sems(self, names):
        return named({name: self.sem(name) for name in names})

    def give_back(self):
        if self.taken:
            self.nc.clear_and_free_semaphores(self.taken)
            self.nc.all_engine_barrier()


class Kept:

    def __init__(self, rows, cols):
        self.rows, self.cols, self.slots = rows, cols, P * cols + P



def prepare_weights(nc, K, I):
    with ExitStack() as ctx:
        A = Buffers(nc, ctx, "weights")
        L, H = GAT_LAYERS, GAT_HEADS
        n_att = L * H * 2
        n_rows = n_att + L * H + L + 2
        eb_at, b_at, bk_at, bv_at = n_att, n_att + L * H, n_att + L * H + L, n_att + L * H + L + 1
        w_raw = A.sb("w_raw", [P, L, H, D])
        rows = A.sb("rows", [n_rows, P])
        ew_raw = A.sb("ew_raw", [P, L, H, EDGE_F])
        hgt_raw = A.sb("hgt_raw", [P, 2, D])
        wa_raw = A.sb("wa_raw", [P, D])
        rel_raw = A.sb("rel_raw", [P, HGT_RELS, 2, D])
        p_col = A.sb("p_col", [P, HGT_RELS])
        p_scaled = A.sb("p_scaled", [P, HGT_RELS])
        skip_rep = A.sb("skip_rep", [P, 1])
        att_blk = A.sb("att_blk", [P, 2, CAT_S])
        conf = A.sb("conf", [P, CAT_CONF])
        conf_max = A.sb("conf_max", [P, 1])
        conf_sum = A.sb("conf_sum", [P, 1])
        wT = A.sb("wT", [P, L * H + 2 + CAT_TYPES, D])
        cols = A.sb("cols", [P, n_rows])
        rep = A.sb("rep", [P, L * H + L + 2, D])
        n_t = L * H + 2 + CAT_TYPES
        ps = [A.ps(f"ps_w{b}", [P, 512]) for b in range(8)]
        loaded, made, turned, copied, mixed = (A.sem(s) for s in ("loaded", "made", "turned", "copied", "mixed"))
        scores_act, conf_ready, dve_step = A.sem("scores_act"), A.sem("conf_ready"), A.sem("dve_step")
        n_loads = (4 + L + 2 + 4 + 3 * HGT_RELS * HGT_HEADS + 1 + 2 * CAT_HEADS * CAT_CONF + 2 + CAT_TYPES + 1 + 4 + 1)

        with nc.Block() as block:
            @block.gpsimd
            def _(eng):
                eng.memset(rel_raw[:, :, :, :], 0.0).then_inc(made, 1)
                eng.memset(att_blk[:, :, :], 0.0).then_inc(made, 1)
                eng.memset(K.ones[:, :], 1.0).then_inc(made, 1)
                eng.memset(K.minus_half[:, :], -0.5)
                eng.wait_ge(made, 3)
                for out, base, step, mult, cmp in ((K.ident, 0, -1, 1, ALU.is_equal), (K.from_prev, 1, -1, 1, ALU.is_equal),
                                                   (K.from_next, -1, -1, 1, ALU.is_equal), (K.upper, -1, 1, -1, ALU.is_ge)):
                    eng.affine_select(out[:, :], K.ones[:, :], pattern=[[step, P]], compare_op=cmp, fill=0.0,
                                      base=base, channel_multiplier=mult).then_inc(made, 1)

            @block.sync
            def _(eng):
                def load(out, in_):
                    eng.dma_start(out, in_).then_inc(loaded, 16)
                with nc.allow_non_contiguous_dma(reason="small weights"):
                    load(w_raw[:, :, :, :].rearrange("i l h o -> i l (h o)"), I.gat_w.rearrange("l i o -> i l o"))
                    load(rows[0:n_att, :], I.gat_att.rearrange("l h (j d) -> (l h j) d", j=2))
                    load(rows[eb_at:eb_at + L * H, :], I.gat_eb.rearrange("l (h o) -> (l h) o", h=H))
                    load(rows[b_at:b_at + L, :], I.gat_b)
                    for l in range(L):
                        load(ew_raw[:, l, :, :], I.gat_ew[l, :, :].rearrange("(h o) f -> o h f", h=H))
                    load(rows[bk_at:bk_at + 1, :], I.hgt_bk.unsqueeze(0))
                    load(rows[bv_at:bv_at + 1, :], I.hgt_bv.unsqueeze(0))
                    load(hgt_raw[:, 0, :], I.hgt_wk)
                    load(hgt_raw[:, 1, :], I.hgt_wv)
                    load(K.hgt_wq[:, :], I.hgt_wq)
                    load(wa_raw[:, :], I.hgt_wa)
                    eng.wait_ge(made, 2)
                    d = D // HGT_HEADS
                    for r in range(HGT_RELS):
                        for h in range(HGT_HEADS):
                            at = slice(h * d, (h + 1) * d)
                            load(rel_raw[at, r, 0, at], I.hgt_a[r, h, :, :])
                            load(rel_raw[at, r, 1, at], I.hgt_m[r, h, :, :])
                            load(p_col[at, r:r + 1], I.hgt_p[r:r + 1, h:h + 1].broadcast_to([d, 1]))
                    load(skip_rep[:, :], I.hgt_skip.broadcast_to([P, 1]))
                    c = D // CAT_HEADS
                    for h in range(CAT_HEADS):
                        for k in range(CAT_CONF):
                            for j in range(2):
                                s = k * CAT_HEADS + h
                                load(att_blk[h * c:(h + 1) * c, j, s:s + 1],
                                     I.cat_att[k, h, j * c:(j + 1) * c].unsqueeze(1))
                    load(conf[:, :], I.cat_conf.unsqueeze(0).broadcast_to([P, CAT_CONF]))
                    load(K.cat_imp[:, :], I.cat_imp.unsqueeze(0).broadcast_to([P, CAT_TYPES]))
                    for t in range(CAT_TYPES):
                        load(K.cat_wu[:, t, 0:D], I.cat_w[t, :, :])
                    load(K.gcn_w[:, :], I.gcn_w)
                    for n, b in enumerate((I.hgt_bq, I.gcn_b, I.cat_b, I.hgt_ba)):
                        load(K.bias_rows[0:1, n, :], b.unsqueeze(0))
                    load(K.hgt_ba[:, :], I.hgt_ba.unsqueeze(0).broadcast_to([P, D]))

            @block.tensor
            def _(eng):
                eng.wait_ge(made, 4)
                eng.wait_ge(loaded, 16 * n_loads)
                src = [w_raw[:, l, h, :] for l in range(L) for h in range(H)] + [hgt_raw[:, 0, :], hgt_raw[:, 1, :]]
                src += [K.cat_wu[:, t, 0:D] for t in range(CAT_TYPES)]
                for n, m in enumerate(src):
                    eng.transpose(ps[n // 4][:, n % 4 * D:n % 4 * D + D], m, K.ident[:, :])
                eng.transpose(ps[4][:, 0:n_rows], rows[:, :], K.ident[0:n_rows, 0:n_rows])
                for l in range(L):
                    b, o = 5 + l // 4, l % 4 * D
                    mm = eng.transpose(ps[b][0:H * EDGE_F, o:o + D], ew_raw[:, l, :, :].rearrange("o h f -> o (h f)"),
                                       K.ident[:, :])
                mm.then_inc(turned, 1)
                eng.wait_ge(copied, 1)
                for l in range(L):
                    for h in range(H):
                        for j in range(2):
                            col = (l * H + h) * 2 + (1 - j)
                            at = l * 4 + j * 2 + h
                            eng.matmul(ps[7][:, at:at + 1], wT[:, l * H + h, :], cols[:, col:col + 1],
                                       start=True, stop=True)
                        at = 32 + (l * H + h) * 20
                        eng.matmul(ps[7][:, at:at + EDGE_F], rep[:, l * H + h, :], ew_raw[:, l, h, :], start=True, stop=True)
                        eng.matmul(ps[7][:, at + EDGE_F:at + EDGE_F + 1], rep[:, l * H + h, :],
                                   cols[:, eb_at + l * H + h:eb_at + l * H + h + 1], start=True, stop=True)
                    eng.matmul(ps[l // 4][:, l % 4 * D:l % 4 * D + D], rep[:, L * H + l, :], K.ident[:, :],
                               start=True, stop=True)
                for r in range(HGT_RELS):
                    for j in range(2):
                        o = (r * 2 + j) * D
                        eng.matmul(ps[2][:, o:o + D], wT[:, L * H + j, :], rel_raw[:, r, j, :], start=True, stop=True)
                        eng.matmul(ps[3][:, o:o + D], rep[:, L * H + L + j, :], rel_raw[:, r, j, :], start=True, stop=True)
                for t in range(CAT_TYPES):
                    for j in range(2):
                        o = (t * 2 + j) * CAT_S
                        mm = eng.matmul(ps[4][:, o:o + CAT_S], wT[:, L * H + 2 + t, :], att_blk[:, j, :],
                                        start=True, stop=True)
                mm.then_inc(mixed, 1)

            @block.scalar
            def _(eng):
                eng.wait_ge(loaded, 16 * n_loads)
                eng.activation(K.hgt_gate[:, 1:2], skip_rep[:, :], ACT.Exp, scale=-1.0).then_inc(scores_act, 1)
                eng.wait_ge(conf_ready, 1)
                eng.activation(K.cat_pk[:, :], conf[:, :], ACT.Exp).then_inc(scores_act, 1)

            @block.vector
            def _(eng):
                step = Order(eng, dve_step)
                eng.wait_ge(loaded, 16 * n_loads)
                eng.wait_ge(made, 7)
                step(eng.tensor_reduce(conf_max[:, :], conf[:, :], AX.X, ALU.max))
                eng.tensor_scalar(conf[:, :], conf[:, :], conf_max[:, 0:1], None, ALU.subtract).then_inc(conf_ready, 1)
                step(eng.tensor_scalar(p_scaled[:, :], p_col[:, :], float(D // HGT_HEADS) ** -0.5, None, ALU.mult))
                for r in range(HGT_RELS):
                    step(eng.tensor_scalar(rel_raw[:, r, 0, :], rel_raw[:, r, 0, :], p_scaled[:, r:r + 1], None, ALU.mult))
                step(eng.tensor_scalar(K.gat_wh[:, :, :, :], w_raw[:, :, :, :], 1.0 / H, None, ALU.mult))
                step(eng.tensor_tensor(K.gat_wm[:, :, :], K.gat_wh[:, :, 0, :], K.gat_wh[:, :, 1, :], ALU.add))
                eng.wait_ge(turned, 1)
                for b in range(n_t // 4):
                    step(eng.tensor_copy(wT[:, 4 * b:4 * b + 4, :].rearrange("p a d -> p (a d)"), ps[b][:, :]))
                step(eng.tensor_copy(cols[:, :], ps[4][:, 0:n_rows]))
                for l in range(L):
                    b, o = 5 + l // 4, l % 4 * D
                    step(eng.tensor_scalar(K.gat_ewT[:, l, :], ps[b][0:H * EDGE_F, o:o + D], 1.0 / H, None, ALU.mult))
                    e0 = eb_at + l * H
                    step(eng.tensor_tensor(K.gat_bias[:, l:l + 1], cols[:, e0:e0 + 1], cols[:, e0 + 1:e0 + 2], ALU.add))
                    step(eng.scalar_tensor_tensor(K.gat_bias[:, l:l + 1], K.gat_bias[:, l:l + 1], 1.0 / H,
                                                  cols[:, b_at + l:b_at + l + 1], ALU.mult, ALU.add))
                    for h in range(H):
                        col = (l * H + h) * 2 + 1
                        step(eng.tensor_scalar(rep[:, l * H + h, :], K.ones[:, :], cols[:, col:col + 1], None, ALU.mult))
                    step(eng.tensor_scalar(rep[:, L * H + l, :], K.ones[:, :], K.gat_bias[:, l:l + 1], None, ALU.mult))
                step(eng.tensor_scalar(rep[:, L * H + L, :], K.ones[:, :], cols[:, bk_at:bk_at + 1], None, ALU.mult))
                eng.tensor_scalar(rep[:, L * H + L + 1, :], K.ones[:, :], cols[:, bv_at:bv_at + 1], None,
                                  ALU.mult).then_inc(copied, 1)
                eng.wait_ge(scores_act, 2)
                step(eng.tensor_scalar(K.hgt_gate[:, 1:2], K.hgt_gate[:, 1:2], 1.0, None, ALU.add))
                step(eng.reciprocal(K.hgt_gate[:, 0:1], K.hgt_gate[:, 1:2]))
                step(eng.tensor_scalar(K.hgt_gate[:, 1:2], K.hgt_gate[:, 0:1], -1.0, 1.0, ALU.mult, ALU.add))
                step(eng.tensor_scalar(K.hgt_wa[:, :], wa_raw[:, :], K.hgt_gate[:, 0:1], None, ALU.mult))
                step(eng.tensor_scalar(K.bias_rows[0:1, 3, :], K.bias_rows[0:1, 3, :], K.hgt_gate[0:1, 0:1], None, ALU.mult))
                step(eng.tensor_scalar(K.hgt_ba[:, :], K.hgt_ba[:, :], K.hgt_gate[:, 0:1], None, ALU.mult))
                step(eng.tensor_reduce(conf_sum[:, :], K.cat_pk[:, :], AX.X, ALU.add))
                step(eng.reciprocal(conf_sum[:, :], conf_sum[:, :]))
                step(eng.tensor_scalar(K.cat_pk[:, :], K.cat_pk[:, :], conf_sum[:, 0:1], None, ALU.mult))
                eng.wait_ge(mixed, 1)
                step(eng.tensor_copy(K.gat_v[:, :, :].rearrange("p l s -> p (l s)"), ps[7][:, 0:4 * L]))
                step(eng.tensor_copy(K.gat_u[:, :, :],
                                     ps[7][:, 32:32 + 20 * L * H].rearrange("p (a f) -> p a f", f=20)[:, :, 0:EDGE_F + 1]))
                for l in range(L):
                    step(eng.tensor_copy(K.gat_bias_rep[:, l, :], ps[l // 4][:, l % 4 * D:l % 4 * D + D]))
                step(eng.tensor_copy(K.hgt_kv[:, :, :].rearrange("p r o -> p (r o)"), ps[2][:, :]))
                step(eng.tensor_copy(K.hgt_kvb[:, :, :].rearrange("p r o -> p (r o)"), ps[3][:, :]))
                u = ps[4][:, 0:2 * CAT_TYPES * CAT_S].rearrange("p (t j s) -> p t j s", t=CAT_TYPES, j=2)
                step(eng.tensor_copy(K.cat_ui[:, :, :], u[:, :, 0, :]))
                step(eng.tensor_copy(K.cat_wu[:, :, D:D + CAT_S], u[:, :, 1, :]))



def describe_slots(nc, K, I):
    C = K.cols
    with ExitStack() as ctx:
        A = Buffers(nc, ctx, "slots")
        raw = A.sb("dst_raw", [P, C], I32)
        src_raw = A.sb("src_raw", [P, C], I32)
        typ2, typ4 = A.sb("typ2", [P, C], I32), A.sb("typ4", [P, C], I32)
        number = A.sb("number", [P, C + 1], I32)
        node_rows = A.sb("node_rows", [P, K.rows // P], I32)
        d1 = A.sb("d1", [P, C])
        diag = A.sb("diag", [P, 2, P])
        around = A.sb("around", [P, 4])
        a_end, head, t0 = A.sb("a_end", [P, C]), A.sb("head", [P, C]), A.sb("t0", [P, C + 1])
        seq = A.sb("seq", [16, P, 2])
        typ4f = A.sb("typ4f", [P, C])
        small = A.sb("small", [P, 8])
        ps = [A.ps(f"ps_s{b}", [P, 512]) for b in range(2)]
        loaded, iotas, diags, turned, step_sem, rows_out = (
            A.sem(s) for s in ("loaded", "iotas", "diags", "turned", "step", "rows_out"))

        with nc.Block() as block:
            @block.sync
            def _(eng):
                eng.dma_start(raw[:, :], I.dst).then_inc(loaded, 16)
                eng.dma_start(src_raw[:, :], I.src).then_inc(loaded, 16)
                eng.dma_start(typ2[:, :], I.type2).then_inc(loaded, 16)
                eng.dma_start(typ4[:, :], I.type4).then_inc(loaded, 16)
                eng.wait_ge(iotas, 3)
                eng.dma_start(K.row_of.rearrange("(p n) one -> p (n one)", p=P), node_rows[:, :]).then_inc(rows_out, 16)
                eng.wait_ge(rows_out, 16)

            @block.gpsimd
            def _(eng):
                eng.iota(number[:, 0:C], [[1, C]], base=0, channel_multiplier=C).then_inc(iotas, 1)
                eng.iota(number[:, C:C + 1], [[0, 1]], base=P * C, channel_multiplier=1).then_inc(iotas, 1)
                eng.iota(node_rows[:, :], [[1, K.rows // P]], base=0, channel_multiplier=K.rows // P).then_inc(iotas, 1)

            @block.tensor
            def _(eng):
                eng.wait_ge(diags, 1)
                eng.matmul(ps[0][:, 0:1], K.from_prev[:, :], d1[:, C - 1:C], start=True, stop=True)
                eng.matmul(ps[0][:, 1:2], K.from_next[:, :], d1[:, 0:1], start=True, stop=True)
                eng.matmul(ps[1][:, 0:P], K.ones[:, :], diag[:, 0, :], start=True, stop=True)
                eng.matmul(ps[1][:, P:2 * P], K.ones[:, :], diag[:, 1, :], start=True, stop=True).then_inc(turned, 1)

            @block.vector
            def _(eng):
                step = Order(eng, step_sem)
                eng.wait_ge(loaded, 16 * 4)
                eng.wait_ge(iotas, 3)
                step(eng.tensor_copy(d1[:, :], raw[:, :]))
                step(eng.tensor_scalar(d1[:, :], d1[:, :], 1.0, None, ALU.add))
                first, last = d1[:, 0:1], d1[:, C - 1:C]
                step(eng.tensor_scalar(diag[:, 0, :], K.ident[:, :], first, None, ALU.mult))
                eng.tensor_scalar(diag[:, 1, :], K.ident[:, :], last, None, ALU.mult).then_inc(diags, 1)
                step(eng.tensor_copy(K.slot_no[:, :], number[:, :]))
                step(eng.tensor_copy(K.gather_dst[:, 0:C], raw[:, :]))
                step(eng.tensor_copy(K.gather_dst[:, C:C + 1], raw[:, 0:1]))
                step(eng.tensor_copy(K.src_node[:, :], src_raw[:, :]))
                step(eng.memset(K.cont[:, 0:1], 0.0))
                step(eng.tensor_tensor(K.cont[:, 1:C], d1[:, 1:C], d1[:, 0:C - 1], ALU.is_equal))
                step(eng.memset(K.goes_on[:, C - 1:C], 0.0))
                step(eng.tensor_copy(K.goes_on[:, 0:C - 1], K.cont[:, 1:C]))
                step(eng.tensor_scalar(K.ends[:, :], K.goes_on[:, :], -1.0, 1.0, ALU.mult, ALU.add))
                step(eng.tensor_scalar(K.restart[:, :], K.cont[:, :], 1.0, -FAR, ALU.subtract, ALU.mult))
                eng.wait_ge(turned, 1)
                step(eng.tensor_tensor(around[:, 0:1], first, ps[0][:, 0:1], ALU.is_equal))
                step(eng.tensor_tensor(around[:, 1:2], last, ps[0][:, 1:2], ALU.is_equal))
                step(eng.tensor_tensor(around[:, 2:3], first, last, ALU.is_equal))
                step(eng.tensor_scalar(K.many[:, :], around[:, 2:3], -1.0, 1.0, ALU.mult, ALU.add))
                step(eng.tensor_scalar(K.carry[:, :], ps[1][:, 0:P], last, None, ALU.is_equal))
                step(eng.tensor_tensor(K.carry[:, :], K.carry[:, :], K.upper[:, :], ALU.mult))
                step(eng.tensor_scalar(head[:, :], d1[:, :], first, None, ALU.is_equal))
                step(eng.tensor_copy(K.in_head[:, :], head[:, :]))
                step(eng.tensor_scalar(K.in_tail[:, :], d1[:, :], last, None, ALU.is_equal))
                step(eng.tensor_tensor(t0[:, 0:C], K.in_tail[:, :], head[:, :], ALU.mult))
                step(eng.tensor_tensor(K.in_tail[:, :], K.in_tail[:, :], t0[:, 0:C], ALU.subtract))
                step(eng.tensor_tensor(t0[:, 0:C], K.in_tail[:, :], head[:, :], ALU.add))
                step(eng.tensor_scalar(K.inner[:, :], t0[:, 0:C], -1.0, 1.0, ALU.mult, ALU.add))
                step(eng.tensor_copy(a_end[:, :], K.ends[:, :]))
                step(eng.tensor_scalar(a_end[:, C - 1:C], around[:, 1:2], -1.0, 1.0, ALU.mult, ALU.add))
                step(eng.tensor_scalar(t0[:, 0:C], head[:, :], around[:, 0:1], None, ALU.mult))
                step(eng.tensor_tensor(t0[:, 0:C], t0[:, 0:C], a_end[:, :], ALU.mult))
                step(eng.tensor_tensor(K.own[:, 0:C], a_end[:, :], t0[:, 0:C], ALU.subtract))
                step(eng.tensor_reduce(K.own[:, C:C + 1], t0[:, 0:C], AX.X, ALU.add))
                step(eng.tensor_scalar(head[:, :], K.slot_no[:, 0:C], K.slot_no[:, 0:1], None, ALU.subtract))
                step(eng.tensor_tensor(head[:, :], head[:, :], t0[:, 0:C], ALU.mult))
                step(eng.tensor_reduce(small[:, 0:1], head[:, :], AX.X, ALU.add))
                step(eng.tensor_tensor(small[:, 0:1], small[:, 0:1], K.slot_no[:, 0:1], ALU.add))
                step(eng.tensor_copy(K.part_slot[:, :], small[:, 0:1]))
                step(eng.tensor_scalar(small[:, 1:2], small[:, 0:1], float(K.rows), None, ALU.add))
                step(eng.tensor_copy(K.part_row[:, :], small[:, 1:2]))
                step(eng.tensor_scalar(t0[:, 0:C], d1[:, :], -1.0 - NOWHERE, None, ALU.add))
                step(eng.tensor_copy(t0[:, C:C + 1], t0[:, 0:1]))
                step(eng.tensor_tensor(t0[:, :], t0[:, :], K.own[:, :], ALU.mult))
                step(eng.tensor_scalar(t0[:, :], t0[:, :], float(NOWHERE), None, ALU.add))
                step(eng.tensor_copy(K.node_of[:, :], t0[:, :]))
                step(eng.tensor_scalar(t0[:, :], K.slot_no[:, :], float(K.rows), None, ALU.add))
                step(eng.tensor_copy(K.slot_row[:, :], t0[:, :]))
                step(eng.tensor_copy(seq[:, :, 0], ps[1][0:16, 0:P]))
                step(eng.tensor_copy(seq[:, :, 1], ps[1][0:16, P:2 * P]))
                flat = seq[:, :, :].rearrange("c p e -> c (p e)")
                step(eng.memset(K.seq_cont[:, 0:1], 0.0))
                step(eng.tensor_tensor(K.seq_cont[:, 1:2 * P], flat[:, 1:2 * P], flat[:, 0:2 * P - 1], ALU.is_equal))
                step(eng.memset(K.seq_goes_on[:, 2 * P - 1:2 * P], 0.0))
                step(eng.tensor_copy(K.seq_goes_on[:, 0:2 * P - 1], K.seq_cont[:, 1:2 * P]))
                step(eng.tensor_scalar(K.seq_ends[:, :], K.seq_goes_on[:, :], -1.0, 1.0, ALU.mult, ALU.add))
                step(eng.tensor_scalar(K.seq_restart[:, :], K.seq_cont[:, :], 1.0, -FAR, ALU.subtract, ALU.mult))
                step(eng.tensor_copy(K.rel_mask[:, 0, :], typ2[:, :]))
                step(eng.tensor_copy(typ4f[:, :], typ4[:, :]))
                step(eng.tensor_scalar(K.rel_mask[:, 1, :], K.rel_mask[:, 0, :], 0.0, None, ALU.is_equal))
                step(eng.tensor_scalar(K.rel_mask[:, 0, :], K.rel_mask[:, 0, :], 1.0, None, ALU.is_equal))
                for t in range(CAT_TYPES):
                    step(eng.tensor_scalar(K.type_mask[:, t, :], typ4f[:, :], float(t), None, ALU.is_equal))


class RunTotals:

    def __init__(self, K, A, channels):
        self.K, self.n = K, channels
        self.edge = A.sb("rt_edge", [P, 2, channels])
        self.seq = A.sb("rt_seq", [channels, P, 2])
        self.back = A.sb("rt_back", [P, 2, channels])
        self.ps_seq, self.ps_back = A.ps("rt_ps_seq", [channels, 2 * P]), A.ps("rt_ps_back", [P, 2 * channels])
        self.edges_ready, self.seq_turned = A.sem("edges_ready"), A.sem("seq_turned")
        self.vector_calls = self.tensor_calls = 0

    def on_vector(self, eng, step, val, op, n, extra=None):
        K, C, k = self.K, self.K.cols, self.vector_calls
        self.vector_calls += 1
        keep, how = (K.cont, ALU.mult) if op is ALU.add else (K.restart, ALU.add)
        for c in range(n):
            v = val[:, c, :]
            step(eng.tensor_tensor_scan(v, keep[:, :], v, 0.0, how, op))
        step(eng.tensor_tensor(val[:, 0:n, :], val[:, 0:n, :], spread(K.ends[:, :], 1, n), ALU.mult))
        for c in range(n):
            v = val[:, c, ::-1]
            step(eng.tensor_tensor_scan(v, K.goes_on[:, ::-1], v, 0.0, ALU.mult, ALU.add))
        head, tail = self.edge[:, 0, 0:n], self.edge[:, 1, 0:n]
        if op is ALU.add:
            step(eng.tensor_scalar(head, val[:, 0:n, 0], K.many[:, 0:1], None, ALU.mult))
        else:
            step(eng.tensor_copy(head, val[:, 0:n, 0]))
        if extra is not None:
            step(eng.tensor_tensor(head, head, extra, ALU.add))
        step(eng.tensor_copy(tail, val[:, 0:n, C - 1]))
        eng.sem_inc(self.edges_ready, 1)
        eng.wait_ge(self.seq_turned, 2 * k + 1)
        seq = self.seq[0:n, :, :].rearrange("c p e -> c (p e)")
        step(eng.tensor_copy(self.seq[0:n, :, 0], self.ps_seq[0:n, 0:P]))
        step(eng.tensor_copy(self.seq[0:n, :, 1], self.ps_seq[0:n, P:2 * P]))
        keep = K.seq_cont if op is ALU.add else K.seq_restart
        step(eng.tensor_tensor_scan(seq, keep[0:n, :], seq, 0.0, how, op))
        step(eng.tensor_tensor(seq, seq, K.seq_ends[0:n, :], ALU.mult))
        step(eng.tensor_tensor_scan(seq[:, ::-1], K.seq_goes_on[0:n, ::-1], seq[:, ::-1], 0.0, ALU.mult, ALU.add))
        eng.sem_inc(self.edges_ready, 1)
        eng.wait_ge(self.seq_turned, 2 * k + 2)
        back = self.back[:, :, 0:n]
        step(eng.tensor_copy(back, self.ps_back[:, 0:2 * n].rearrange("p (e c) -> p e c", e=2)))
        step(eng.tensor_tensor(val[:, 0:n, :], val[:, 0:n, :], spread(K.inner[:, :], 1, n), ALU.mult))
        for c in range(n):
            for e, mask in enumerate((K.in_head, K.in_tail)):
                step(eng.scalar_tensor_tensor(val[:, c, :], mask[:, :], self.back[:, e, c:c + 1], val[:, c, :],
                                              ALU.mult, ALU.add))

    def on_tensor(self, eng, n):
        K, k = self.K, self.tensor_calls
        self.tensor_calls += 1
        eng.wait_ge(self.edges_ready, 2 * k + 1)
        for e in range(2):
            mm = eng.transpose(self.ps_seq[0:n, e * P:(e + 1) * P], self.edge[:, e, 0:n], K.ident[:, :])
        mm.then_inc(self.seq_turned, 1)
        eng.wait_ge(self.edges_ready, 2 * k + 2)
        for e in range(2):
            mm = eng.transpose(self.ps_back[:, e * n:(e + 1) * n], self.seq[0:n, :, e], K.ident[0:n, 0:n])
        mm.then_inc(self.seq_turned, 1)


def map_rows(nc, K):
    C = K.cols
    with ExitStack() as ctx:
        A = Buffers(nc, ctx, "map")
        R = RunTotals(K, A, 2)
        val = A.sb("val", [P, 2, C])
        extra = A.sb("extra", [P, 2])
        deg = A.sb("deg", [P, C + 1])
        power = A.sb("power", [P, C + 1])
        at = A.sb("at", [P, 2, TILES], I32)
        what = A.sb("what", [P, 2, TILES], I32)
        got = A.sb("got", [P, 2, TILES], I32)
        s = A.sems((
            "step", "deg_ready", "dinv_ready", "copied", "wrote0", "wrote1", "got0", "got1", "taken", "gate"))
        n = C // TILES
        with nc.Block() as block:
            @block.gpsimd
            def _(eng):
                with eng.Fori(0, n) as g:
                    eng.tensor_copy(at[:, 0, :], K.node_of[:, bass.ts(g, TILES)])
                    eng.tensor_copy(what[:, 0, :], K.slot_row[:, bass.ts(g, TILES)]).then_inc(s.copied, 1)
                    eng.wait_ge(s.copied, g + 1)
                    eng.sem_inc(s.gate, 1)
                    for t in range(TILES):
                        eng.indirect_dma_start(K.row_of, bass.IndirectOffsetOnAxis(ap=at[:, 0, t:t + 1], axis=0),
                                               what[:, 0, t:t + 1], None, bounds_check=K.rows - 1,
                                               oob_is_err=False).then_inc(s.wrote0, 16)
                    eng.wait_ge(s.wrote0, g * 16 * TILES + 16 * TILES)
                    eng.sem_inc(s.gate, 1)
                eng.tensor_copy(at[:, 1, 0:1], K.node_of[:, C:C + 1])
                eng.tensor_copy(what[:, 1, 0:1], K.slot_row[:, C:C + 1]).then_inc(s.copied, 1)
                eng.wait_ge(s.copied, n + 1)
                eng.indirect_dma_start(K.row_of, bass.IndirectOffsetOnAxis(ap=at[:, 1, 0:1], axis=0),
                                       what[:, 1, 0:1], None, bounds_check=K.rows - 1,
                                       oob_is_err=False).then_inc(s.wrote1, 16)
                eng.wait_ge(s.wrote1, 16)
                eng.sem_inc(s.taken, 2)
                for i, both in batches(eng, n):
                    for g, u in both:
                        eng.wait_ge(s.taken, freed(g))
                        eng.sem_inc(s.gate, 1)
                        eng.tensor_copy(at[:, u, :], K.src_node[:, bass.ts(g, TILES)]).then_inc(s.copied, 1)
                        eng.wait_ge(s.copied, n + 2 + g)
                        eng.sem_inc(s.gate, 1)
                        for t in range(TILES):
                            eng.indirect_dma_start(got[:, u, t:t + 1], None, K.row_of,
                                                   bass.IndirectOffsetOnAxis(ap=at[:, u, t:t + 1], axis=0)
                                                   ).then_inc((s.got0, s.got1)[u], 16)
                eng.wait_ge(s.deg_ready, 1)
                eng.tensor_tensor(K.dinv[:, :], deg[:, :], power[:, :], ALU.pow).then_inc(s.dinv_ready, 1)

            @block.tensor
            def _(eng):
                R.on_tensor(eng, 1)
                R.on_tensor(eng, 1)

            @block.vector
            def _(eng):
                step = Order(eng, s.step)
                step(eng.tensor_tensor(val[:, 0, :], K.slot_no[:, 0:C], K.own[:, 0:C], ALU.mult))
                step(eng.tensor_tensor(extra[:, 0:1], K.slot_no[:, C:C + 1], K.own[:, C:C + 1], ALU.mult))
                R.on_vector(eng, step, val, ALU.add, 1, extra[:, 0:1])
                step(eng.tensor_copy(K.dst_slot[:, :], val[:, 0, :]))
                step(eng.memset(val[:, 1, :], 1.0))
                R.on_vector(eng, step, val[:, 1:2, :], ALU.add, 1)
                step(eng.tensor_scalar(deg[:, 0:C], val[:, 1, :], 1.0, None, ALU.add))
                step(eng.memset(power[:, :], -0.5))
                eng.tensor_copy(deg[:, C:C + 1], deg[:, 0:1]).then_inc(s.deg_ready, 1)
                for i, both in batches(eng, n):
                    for g, u in both:
                        eng.wait_ge((s.got0, s.got1)[u], (i + 1) * 16 * TILES)
                        eng.tensor_scalar(K.src_row[:, bass.ts(g, TILES)], got[:, u, :], 0.0, None,
                                          ALU.add).then_inc(s.taken, 1)
                eng.wait_ge(s.dinv_ready, 1)



def stats_of(eng, step, gate, x, st, mv, n):
    for t in range(n):
        ins = eng.bn_stats(st[:, t, :], x[:, t, :])
    step(ins)
    eng.sem_inc(gate, 1)
    for t in range(n):
        ins = eng.bn_aggr(mv[:, t, :], st[:, t, :])
    step(ins)
    return eng.tensor_scalar(mv[:, 0:n, 1], mv[:, 0:n, 1], LN_EPS, None, ALU.add)


def normalised(eng, step, x, mv, rstd, out, n):
    for t in range(n):
        ins = eng.tensor_scalar(out[:, t, 0:D], x[:, t, :], mv[:, t, 0:1], rstd[:, t:t + 1], ALU.subtract, ALU.mult)
    step(ins)
    return eng.tensor_scalar(out[:, 0:n, 0:D], out[:, 0:n, 0:D], 0.0, None, ALU.max)


def node_pass(nc, K, I, out):
    n_pairs = K.rows // GROUP // 2
    L = GAT_LAYERS
    LN = 4
    with ExitStack() as ctx:
        A = Buffers(nc, ctx, "nodes")
        x_in = A.sb("x_in", [P, 2, TILES, D])
        xs = A.sb("xs", [P, 2, TILES, D])
        rows = A.sb("rows", [P, 2, 2, TILES, ROWW])
        h_rows = A.sb("h_rows", [P, 2, 3, TILES, D])
        x_out = A.sb("x_out", [P, 2, TILES, D])
        hT = A.sb("hT", [P, 2, 2, GROUP])
        gelu = A.sb("gelu", [P, 2, TILES, D])
        st = A.sb("st", [P, 2, TILES, 6])
        mv = A.sb("mv", [P, 2, LN, TILES, 2])
        rstd = A.sb("rstd", [P, 2, LN, TILES])
        psT = [A.ps(f"psT{u}", [P, GROUP]) for u in range(2)]
        psZ = [A.ps(f"psZ{u}", [P, GROUP]) for u in range(2)]
        psR = [A.ps(f"psR{u}", [P, GROUP]) for u in range(2)]
        psS = [A.ps(f"psS{u}", [P, 4 * TILES]) for u in range(2)]
        s = A.sems((
            "x0_in", "x1_in", "stats", "rstd_ready", "normed", "rows_done", "x1_done", "finished", "turned", "mixed",
            "rows_ready", "last_turned", "wide", "copiedT", "hT_ready", "gelu_done", "step", "rows_free", "out_free",
            "stored", "stored_h", "x2_done", "x3_done", "gate"))

        def node_view(table, i, u, w):
            at = (i * 2 + u) * GROUP
            return table[bass.ds(at, GROUP), 0:w].rearrange("(p t) w -> p t w", t=TILES)

        with nc.Block() as block:
            @block.sync
            def _(eng):
                def load(i):
                    for u in range(2):
                        eng.dma_start(x_in[:, u, :, :], node_view(I.x, i, u, D)).then_inc((s.x0_in, s.x1_in)[u], 16)

                def stores(i, more):
                    for l in range(L):
                        for u in range(2):
                            eng.wait_ge(s.rows_done, i * 2 * L + 2 * l + u + 1)
                            eng.dma_start(node_view(K.tables[l], i, u, ROWW), rows[:, u, l % 2, :, :]).then_inc(s.stored, 16)
                        eng.wait_ge(s.stored, i * 32 * L + 32 * (l + 1))
                        eng.sem_inc(s.rows_free, 1)
                    if more:
                        eng.wait_ge(s.x1_done, 2 * i + 2)
                        load(i + 1)
                    for n in range(3):
                        for u in range(2):
                            eng.wait_ge(s.normed, i * 2 * LN + 2 * (n + 1) + u + 1)
                            eng.dma_start(node_view(K.tables[L + n], i, u, D), h_rows[:, u, n, :, :]).then_inc(s.stored_h, 16)
                    for u in range(2):
                        eng.wait_ge(s.finished, 2 * i + u + 1)
                        eng.dma_start(node_view(out, i, u, D), x_out[:, u, :, :]).then_inc(s.stored_h, 16)
                    eng.wait_ge(s.stored_h, i * 128 + 128)
                    eng.sem_inc(s.out_free, 1)

                eng.sem_inc(s.rows_free, 2)
                eng.sem_inc(s.out_free, 1)
                load(0)
                with eng.Fori(0, n_pairs - 1) as i:
                    stores(i, True)
                stores(n_pairs - 1, False)

            @block.gpsimd
            def _(eng):
                with eng.Fori(0, n_pairs) as i:
                    for n in range(LN):
                        for u in range(2):
                            eng.wait_ge(s.stats, i * 2 * LN + 2 * n + u + 1)
                            eng.tensor_tensor(rstd[:, u, n, :], mv[:, u, n, :, 1], K.minus_half[:, :], ALU.pow
                                              ).then_inc(s.rstd_ready, 1)

            @block.vector
            def _(eng):
                with eng.Fori(0, n_pairs) as i:
                    step = LoopOrder(eng, s.step, 2 * (3 * LN + 1), i)

                    def layer_norm_stats(n, x):
                        for u in range(2):
                            stats_of(eng, step, s.gate, x[:, u, :, :], st[:, u, :, :], mv[:, u, n, :, :], TILES).then_inc(s.stats, 1)

                    def layer_norm(n, x, to):
                        for u in range(2):
                            eng.wait_ge(s.rstd_ready, i * 2 * LN + 2 * n + u + 1)
                            normalised(eng, step, x[:, u, :, :], mv[:, u, n, :, :], rstd[:, u, n, :], to(u), TILES
                                       ).then_inc(s.normed, 1)

                    for u in range(2):
                        eng.wait_ge((s.x0_in, s.x1_in)[u], 16 * (i + 1))
                    layer_norm_stats(0, x_in)
                    eng.wait_ge(s.rows_free, i * L + 2)
                    layer_norm(0, x_in, lambda u: rows[:, u, 0, :, :])
                    for l in range(L):
                        eng.wait_ge(s.rows_free, i * L + l + 1)
                        for u in range(2):
                            eng.wait_ge(s.rows_ready, i * 2 * L + 2 * l + u + 1)
                            to = rows[:, u, l % 2, :, :]
                            if l > 0:
                                eng.tensor_copy(to[:, :, 0:D], psR[u][:, :].rearrange("p (t d) -> p t d", d=D))
                            eng.tensor_copy(to[:, :, D:ROWW], psS[u][:, :].rearrange("p (t c) -> p t c", c=4)
                                            ).then_inc(s.rows_done, 1)
                    for u in range(2):
                        eng.wait_ge(s.last_turned, 2 * i + u + 1)
                        eng.tensor_tensor(xs[:, u, :, :], x_in[:, u, :, :],
                                          psR[u][:, :].rearrange("p (t d) -> p t d", d=D), ALU.add).then_inc(s.x1_done, 1)
                    eng.wait_ge(s.x1_done, 2 * i + 2)
                    layer_norm_stats(1, xs)
                    eng.wait_ge(s.out_free, i + 1)
                    layer_norm(1, xs, lambda u: h_rows[:, u, 0, :, :])
                    eng.wait_ge(s.normed, i * 2 * LN + 4)
                    for u in range(2):
                        step(eng.scalar_tensor_tensor(xs[:, u, :, :], h_rows[:, u, 0, :, :], K.hgt_gate[:, 1:2],
                                                      xs[:, u, :, :], ALU.mult, ALU.add))
                        if u == 0:
                            eng.tensor_tensor(xs[:, u, :, :], xs[:, u, :, :], spread(K.hgt_ba[:, :], 1, TILES), ALU.add)
                        else:
                            eng.tensor_tensor(xs[:, u, :, :], xs[:, u, :, :], spread(K.hgt_ba[:, :], 1, TILES),
                                              ALU.add).then_inc(s.x2_done, 1)
                    eng.wait_ge(s.x2_done, i + 1)
                    layer_norm_stats(2, xs)
                    layer_norm(2, xs, lambda u: h_rows[:, u, 1, :, :])
                    for u in range(2):
                        eng.wait_ge(s.gelu_done, 2 * i + u + 1)
                        eng.tensor_tensor(xs[:, u, :, :], xs[:, u, :, :], gelu[:, u, :, :], ALU.add).then_inc(s.x3_done, 1)
                    eng.wait_ge(s.x3_done, 2 * i + 2)
                    layer_norm_stats(3, xs)
                    layer_norm(3, xs, lambda u: h_rows[:, u, 2, :, :])
                    for u in range(2):
                        eng.wait_ge(s.wide, 4 * i + 2 + u + 1)
                        eng.tensor_tensor(x_out[:, u, :, :], xs[:, u, :, :],
                                          psZ[u][:, :].rearrange("p (t d) -> p t d", d=D), ALU.add).then_inc(s.finished, 1)
                    step.end()

            @block.tensor
            def _(eng):
                with eng.Fori(0, n_pairs) as i:
                    def turn_rows(n, ln, h):
                        for u in range(2):
                            eng.wait_ge(s.normed, i * 2 * LN + 2 * ln + u + 1)
                            for t in range(TILES):
                                mm = eng.transpose(psT[u][:, t * P:(t + 1) * P], h(u)[:, t, 0:D], K.ident[:, :])
                            mm.then_inc(s.turned, 1)

                    turn_rows(0, 0, lambda u: rows[:, u, 0, :, :])
                    for l in range(L):
                        for u in range(2):
                            if l == 0:
                                eng.wait_ge(s.copiedT, 6 * i + u + 1)
                            else:
                                eng.wait_ge(s.hT_ready, i * 2 * L + 2 * (l - 1) + u + 1)
                            eng.matmul(psZ[u][:, :], K.gat_wm[:, l, :], hT[:, u, l % 2, :], start=True, stop=True
                                       ).then_inc(s.mixed, 1)
                        for u in range(2):
                            if l > 0:
                                eng.wait_ge(s.rows_done, i * 2 * L + 2 * (l - 1) + u + 1)
                            for t in range(TILES):
                                if l > 0:
                                    eng.transpose(psR[u][:, t * P:(t + 1) * P], hT[:, u, l % 2, t * P:(t + 1) * P],
                                                  K.ident[:, :])
                                mm = eng.matmul(psS[u][:, 4 * t:4 * t + 4], hT[:, u, l % 2, t * P:(t + 1) * P],
                                                K.gat_v[:, l, :], start=True, stop=True)
                            mm.then_inc(s.rows_ready, 1)
                    for u in range(2):
                        eng.wait_ge(s.hT_ready, i * 2 * L + 2 * (L - 1) + u + 1)
                        eng.wait_ge(s.rows_done, i * 2 * L + 2 * (L - 1) + u + 1)
                        for t in range(TILES):
                            mm = eng.transpose(psR[u][:, t * P:(t + 1) * P], hT[:, u, L % 2, t * P:(t + 1) * P], K.ident[:, :])
                        mm.then_inc(s.last_turned, 1)
                    for n, (w, bias) in enumerate(((K.gcn_w[:, :], K.bias_rows[0:1, 1, :]),
                                                   (K.cat_wu[:, 0, 0:D], K.bias_rows[0:1, 2, :]))):
                        turn_rows(1 + n, 2 + n, lambda u: h_rows[:, u, 1 + n, :, :])
                        for u in range(2):
                            eng.wait_ge(s.copiedT, 6 * i + 2 * (n + 1) + u + 1)
                            for t in range(TILES):
                                o = psZ[u][:, t * P:(t + 1) * P]
                                eng.matmul(o, K.ones[0:1, :], bias, start=True, stop=False)
                                mm = eng.matmul(o, hT[:, u, n, t * P:(t + 1) * P], w, start=False, stop=True)
                            mm.then_inc(s.wide, 1)

            @block.scalar
            def _(eng):
                eng.preload_act_table(ACT.Gelu)
                with eng.Fori(0, n_pairs) as i:
                    def copy_turned(n, buf):
                        for u in range(2):
                            eng.wait_ge(s.turned, 6 * i + 2 * n + u + 1)
                            eng.activation(hT[:, u, buf, :], psT[u][:, :], ACT.Copy).then_inc(s.copiedT, 1)

                    copy_turned(0, 0)
                    for l in range(L):
                        for u in range(2):
                            eng.wait_ge(s.mixed, i * 2 * L + 2 * l + u + 1)
                            eng.activation(hT[:, u, (l + 1) % 2, :], psZ[u][:, :],
                                           ACT.Relu if l < L - 1 else ACT.Identity,
                                           bias=K.gat_bias[:, l:l + 1]).then_inc(s.hT_ready, 1)
                    copy_turned(1, 0)
                    for u in range(2):
                        eng.wait_ge(s.wide, 4 * i + u + 1)
                        eng.activation(gelu[:, u, :, :].rearrange("p t d -> p (t d)"), psZ[u][:, :], ACT.Gelu
                                       ).then_inc(s.gelu_done, 1)
                    copy_turned(2, 1)




def column(tile, c):
    w = tile.shape[2]
    return tile[:, :, :].rearrange("p c w -> p (c w)")[:, bass.ds(c * w, w)]


def slot_cols(g, n):
    return slice(TILES * g, TILES * g + 1) if tiles_of(g, n) == 1 else bass.ts(g, TILES)


def slot_rows(K, table, first, g, w=None):
    C, w = K.cols, w or table.shape[1]
    if tiles_of(g, C // TILES) == 1:
        return table[first + P * C:first + P * C + P, 0:w].unsqueeze(1)
    return table[first:first + P * C, 0:w].rearrange("(p c) w -> p c w", p=P)[:, bass.ts(g, TILES), :]


def gather(eng, table, index, to, sem):
    eng.indirect_dma_start(to, None, table, bass.IndirectOffsetOnAxis(ap=index, axis=0)).then_inc(sem, 16)


def turn_tiles(eng, K, ps, h, tiles):
    for t in range(tiles):
        mm = eng.transpose(ps[:, t * P:(t + 1) * P], h[:, t, 0:D], K.ident[:, :])
    return mm


def by_tile(ps, tiles, w=D):
    return ps[:, 0:tiles * w].rearrange("p (t w) -> p t w", w=w)


def enter_slots(nc, K, I):
    C = K.cols
    n = C // TILES
    with ExitStack() as ctx:
        A = Buffers(nc, ctx, "enter")
        at = A.sb("at", [P, 2, TILES], I32)
        x_in = A.sb("x_in", [P, 2, TILES, D])
        rows = A.sb("rows", [P, 2, TILES, ROWW])
        hT = A.sb("hT", [P, 2, GROUP])
        st, mv, rstd = A.sb("st", [P, 2, TILES, 6]), A.sb("mv", [P, 2, TILES, 2]), A.sb("rstd", [P, 2, TILES])
        psT = [A.ps(f"psT{u}", [P, GROUP]) for u in range(2)]
        psS = [A.ps(f"psS{u}", [P, 4 * TILES]) for u in range(2)]
        s = A.sems((
            "indexed", "x0_in", "x1_in", "stats", "rstd_ready", "normed", "turned", "copiedT", "scored", "rows_done",
            "stored", "free", "step", "gate"))
        with nc.Block() as block:
            @block.gpsimd
            def _(eng):
                for i, both in batches(eng, n, 1):
                    for g, u in both:
                        eng.wait_ge(s.free, freed(g))
                        eng.sem_inc(s.gate, 1)
                        m = tiles_of(g, n)
                        eng.tensor_copy(at[:, u, 0:m], K.gather_dst[:, slot_cols(g, n)]).then_inc(s.indexed, 1)
                        eng.wait_ge(s.indexed, g + 1)
                        eng.sem_inc(s.gate, 1)
                        for t in range(m):
                            gather(eng, I.x, at[:, u, t:t + 1], x_in[:, u, t, :], (s.x0_in, s.x1_in)[u])
                    for g, u in both:
                        eng.wait_ge(s.stats, g + 1)
                        eng.tensor_tensor(rstd[:, u, :], mv[:, u, :, 1], K.minus_half[:, :], ALU.pow
                                          ).then_inc(s.rstd_ready, 1)

            @block.vector
            def _(eng):
                eng.memset(mv[:, :, :, :], 1.0).then_inc(s.step, 1)
                eng.wait_ge(s.step, 1)
                for i, both in batches(eng, n, 1):
                    step = LoopOrder(eng, s.step, 6, i, 1)
                    for g, u in both:
                        m = tiles_of(g, n)
                        eng.wait_ge((s.x0_in, s.x1_in)[u], i * 16 * TILES + 16 * m)
                        stats_of(eng, step, s.gate, x_in[:, u, :, :], st[:, u, :, :], mv[:, u, :, :], m).then_inc(s.stats, 1)
                    for g, u in both:
                        eng.wait_ge(s.rstd_ready, g + 1)
                        normalised(eng, step, x_in[:, u, :, :], mv[:, u, :, :], rstd[:, u, :], rows[:, u, :, :],
                                   tiles_of(g, n)).then_inc(s.normed, 1)
                    for g, u in both:
                        m = tiles_of(g, n)
                        eng.wait_ge(s.scored, g + 1)
                        eng.tensor_scalar(K.sc[:, :, slot_cols(g, n)], psS[u][:, 0:4 * m].rearrange("p (t c) -> p c t", c=4),
                                          0.0, None, ALU.add)
                        eng.tensor_copy(rows[:, u, 0:m, D:ROWW], by_tile(psS[u], m, 4)).then_inc(s.rows_done, 1)

            @block.tensor
            def _(eng):
                for i, both in batches(eng, n, 1):
                    for g, u in both:
                        eng.wait_ge(s.normed, g + 1)
                        turn_tiles(eng, K, psT[u], rows[:, u, :, :], tiles_of(g, n)).then_inc(s.turned, 1)
                    for g, u in both:
                        eng.wait_ge(s.copiedT, g + 1)
                        for t in range(tiles_of(g, n)):
                            mm = eng.matmul(psS[u][:, 4 * t:4 * t + 4], hT[:, u, t * P:(t + 1) * P], K.gat_v[:, 0, :],
                                            start=True, stop=True)
                        mm.then_inc(s.scored, 1)

            @block.scalar
            def _(eng):
                eng.preload_act_table(ACT.Copy)
                for i, both in batches(eng, n, 1):
                    for g, u in both:
                        w = tiles_of(g, n) * P
                        eng.wait_ge(s.turned, g + 1)
                        eng.activation(hT[:, u, 0:w], psT[u][:, 0:w], ACT.Copy).then_inc(s.copiedT, 1)

            @block.sync
            def _(eng):
                eng.sem_inc(s.free, 2)
                for i, both in batches(eng, n, 1):
                    for g, u in both:
                        m = tiles_of(g, n)
                        eng.wait_ge(s.rows_done, g + 1)
                        eng.dma_start(slot_rows(K, K.tables[0], K.rows, g), rows[:, u, 0:m, :]).then_inc(s.stored, 16)
                        eng.dma_start(slot_rows(K, K.resid, 0, g), x_in[:, u, 0:m, :]).then_inc(s.stored, 16)
                    eng.wait_ge(s.stored, i * 64 + 32 * len(both))
                    eng.sem_inc(s.free, 2)



def gather_rows(nc, K, l, table, w, to, scores=None):
    n = K.cols // TILES
    with ExitStack() as ctx:
        A = Buffers(nc, ctx, f"gather{l}")
        at = A.sb("at", [P, 2, TILES], I32)
        ring = A.sb("ring", [P, 2, TILES, w])
        s = A.sems(("indexed", "r0_in", "r1_in", "taken", "gate"))
        with nc.Block() as block:
            @block.gpsimd
            def _(eng):
                eng.sem_inc(s.taken, 2)
                for i, both in batches(eng, n):
                    for g, u in both:
                        eng.wait_ge(s.taken, freed(g))
                        eng.sem_inc(s.gate, 1)
                        eng.tensor_copy(at[:, u, :], K.src_row[:, bass.ts(g, TILES)]).then_inc(s.indexed, 1)
                        eng.wait_ge(s.indexed, g + 1)
                        eng.sem_inc(s.gate, 1)
                        for t in range(TILES):
                            gather(eng, table, at[:, u, t:t + 1], ring[:, u, t, :], (s.r0_in, s.r1_in)[u])

            @block.vector
            def _(eng):
                for i, both in batches(eng, n):
                    for g, u in both:
                        eng.wait_ge((s.r0_in, s.r1_in)[u], (i + 1) * 16 * TILES)
                        if scores is not None:
                            eng.tensor_scalar(scores[:, :, bass.ts(g, TILES)],
                                              ring[:, u, :, D:D + GAT_HEADS].rearrange("p t h -> p h t"), 0.0, None, ALU.add)
                        eng.tensor_scalar(to[:, bass.ds(g * TILES + 1, TILES), :], ring[:, u, :, 0:D], 0.0, None, ALU.max
                                          ).then_inc(s.taken, 1)


def gat_weights(nc, K, I, l, src_score, alpha, alpha_self):
    C, H = K.cols, GAT_HEADS
    with ExitStack() as ctx:
        A = Buffers(nc, ctx, f"attend{l}")
        R = RunTotals(K, A, 4)
        node = A.sb("node", [P, 4, C])
        extra = A.sb("extra", [P, 4])
        part = C // 4
        edge_x = A.sb("edge_x", [P, C, EDGE_F])
        prod = A.sb("prod", [P, part, EDGE_F])
        edge, top = A.sb("edge", [P, H, C]), A.sb("top", [P, H, C])
        loop = A.sb("loop", [P, H, C])
        step_sem, to_exp, from_exp, x_in = A.sem("step"), A.sem("to_exp"), A.sem("from_exp"), A.sem("x_in")
        with nc.Block() as block:
            @block.sync
            def _(eng):
                eng.dma_start(edge_x[:, :, :], I.edge_x).then_inc(x_in, 16)

            @block.vector
            def _(eng):
                step = Order(eng, step_sem)
                step(eng.tensor_tensor(node[:, :, :], K.sc[:, :, 0:C], spread(K.own[:, 0:C], 1, 4), ALU.mult))
                step(eng.tensor_scalar(extra[:, :], K.sc[:, :, C], K.own[:, C:C + 1], None, ALU.mult))
                R.on_vector(eng, step, node, ALU.add, 4, extra[:, :])
                eng.wait_ge(x_in, 16)
                for h in range(H):
                    u = K.gat_u[:, l * H + h, :]
                    for c in range(0, C, part):
                        step(eng.tensor_tensor(prod[:, :, :], edge_x[:, c:c + part, :], spread(u[:, 0:EDGE_F], 1, part), ALU.mult))
                        step(eng.tensor_reduce(edge[:, h, c:c + part], prod[:, :, :], AX.X, ALU.add))
                    step(eng.tensor_scalar(node[:, 2 + h, :], node[:, 2 + h, :], u[:, EDGE_F:EDGE_F + 1], None, ALU.add))
                step(eng.tensor_tensor(edge[:, :, :], edge[:, :, :], node[:, 2:4, :], ALU.add))
                step(eng.tensor_tensor(edge[:, :, :], edge[:, :, :], src_score[:, :, :], ALU.add))
                step(eng.scalar_tensor_tensor(edge[:, :, :], edge[:, :, :], 0.2, edge[:, :, :], ALU.mult, ALU.max))
                step(eng.tensor_tensor(loop[:, :, :], node[:, 0:2, :], node[:, 2:4, :], ALU.add))
                step(eng.scalar_tensor_tensor(loop[:, :, :], loop[:, :, :], 0.2, loop[:, :, :], ALU.mult, ALU.max))
                step(eng.tensor_copy(top[:, :, :], edge[:, :, :]))
                R.on_vector(eng, step, top, ALU.max, H)
                step(eng.tensor_tensor(top[:, :, :], top[:, :, :], loop[:, :, :], ALU.max))
                step(eng.tensor_tensor(edge[:, :, :], edge[:, :, :], top[:, :, :], ALU.subtract))
                step(eng.tensor_tensor(loop[:, :, :], loop[:, :, :], top[:, :, :], ALU.subtract))
                eng.sem_inc(to_exp, 1)
                eng.wait_ge(from_exp, 2)
                step(eng.tensor_copy(top[:, :, :], edge[:, :, :]))
                R.on_vector(eng, step, top, ALU.add, H)
                step(eng.tensor_tensor(top[:, :, :], top[:, :, :], loop[:, :, :], ALU.add))
                step(eng.reciprocal(top[:, :, :], top[:, :, :]))
                step(eng.tensor_tensor(alpha[:, :, :], edge[:, :, :], top[:, :, :], ALU.mult))
                step(eng.tensor_tensor(loop[:, :, :], loop[:, :, :], top[:, :, :], ALU.mult))
                step(eng.tensor_tensor(alpha_self[:, :, 0:C], loop[:, :, :], spread(K.own[:, 0:C], 1, H), ALU.mult))
                step(eng.tensor_copy(alpha_self[:, :, C], loop[:, :, 0]))

            @block.tensor
            def _(eng):
                R.on_tensor(eng, 4)
                R.on_tensor(eng, H)
                R.on_tensor(eng, H)

            @block.scalar
            def _(eng):
                eng.preload_act_table(ACT.Exp)
                eng.wait_ge(to_exp, 1)
                eng.activation(edge[:, :, :], edge[:, :, :], ACT.Exp).then_inc(from_exp, 1)
                eng.activation(loop[:, :, :], loop[:, :, :], ACT.Exp).then_inc(from_exp, 1)


def gat_slots(nc, K, I, l, G, alpha, alpha_self):
    C, H = K.cols, GAT_HEADS
    n = C // TILES
    E2 = H * EDGE_F
    last = l == GAT_LAYERS - 1
    table = K.gat_out if last else K.tables[l + 1]
    first, w = (0, D) if last else (K.rows, ROWW)
    with ExitStack() as ctx:
        A = Buffers(nc, ctx, f"gat{l}")
        own = A.sb("own", [P, 2, TILES, ROWW])
        part = A.sb("part", [P, 2, H * D])
        edge_x, part_e = A.sb("edge_x", [P, 2, TILES, EDGE_F]), A.sb("part_e", [P, 2, TILES, E2])
        run, run_e = A.sb("run", [P, 2, TILES, H * D]), A.sb("run_e", [P, 2, TILES, E2])
        loop = A.sb("loop", [P, 2, TILES, H, D])
        aggT = A.sb("aggT", [P, 2, H, GROUP])
        edgeT = A.sb("edgeT", [E2, 2, GROUP])
        zT, hT = A.sb("zT", [P, 2, GROUP]), A.sb("hT", [P, 2, GROUP])
        rows = A.sb("rows", [P, 2, TILES, ROWW])
        psA = [[A.ps(f"psA{u}{h}", [P, GROUP]) for h in range(H)] for u in range(2)]
        psE, psZ, psR, psS = (A.ps(m, [P, GROUP]) for m in ("psE", "psZ", "psR", "psS"))
        s = A.sems((
            "own0_in", "own1_in", "x0_in", "x1_in", "part_ready", "run_ready", "looped", "agg_turned", "aggT0", "aggT1", "edgeT_ready",
            "mixed", "zT_ready", "hT_ready", "rows_ready", "rows_done", "stored", "free", "gate", "zeroed"))
        with nc.Block() as block:
            @block.sync
            def _(eng):
                def load(both):
                    for g, u in both:
                        eng.wait_ge(s.looped, freed(g))
                        eng.dma_start(own[:, u, :, :], slot_rows(K, K.tables[l], K.rows, g)).then_inc((s.own0_in, s.own1_in)[u], 16)
                        eng.wait_ge(s.agg_turned, freed(g))
                        eng.dma_start(edge_x[:, u, :, :], I.edge_x[:, bass.ts(g, TILES), :]).then_inc((s.x0_in, s.x1_in)[u], 16)

                eng.sem_inc(s.free, 2)
                load(batch(0, n, 0))
                for i, both, j, ahead in batches_ahead(eng, n):
                    load(ahead)
                    for g, u in both:
                        eng.wait_ge(s.rows_done, g + 2)
                        eng.dma_start(slot_rows(K, table, first, g), rows[:, u, :, 0:w]).then_inc(s.stored, 16)
                    eng.wait_ge(s.stored, i * 32 + 16 * len(both))
                    eng.sem_inc(s.free, len(both))

            @block.vector
            def _(eng):
                eng.memset(run[:, 1, TILES - 1, :], 0.0).then_inc(s.run_ready, 1)
                eng.memset(run_e[:, 1, TILES - 1, :], 0.0).then_inc(s.run_ready, 1)
                eng.sem_inc(s.rows_done, 1)
                for i, both in batches(eng, n):
                    for g, u in both:
                        def weigh(t):
                            for h in range(H):
                                ins = eng.tensor_scalar(part[:, t % 2, h * D:(h + 1) * D], column(G, g * TILES + t + 1),
                                                        alpha[:, h, bass.ds(g * TILES + t, 1)], None, ALU.mult)
                            ins.then_inc(s.part_ready, 1)
                        eng.wait_ge((s.x0_in, s.x1_in)[u], (i + 1) * 16)
                        for h in range(H):
                            eng.tensor_tensor(part_e[:, u, :, h * EDGE_F:(h + 1) * EDGE_F], edge_x[:, u, :, :],
                                              spread(alpha[:, h, bass.ts(g, TILES)], 2, EDGE_F), ALU.mult)
                        weigh(0)
                        eng.wait_ge(s.agg_turned, freed(g))
                        for t in range(TILES):
                            c = g * TILES + t
                            eng.wait_ge(s.run_ready, c + 2)
                            if t + 1 < TILES:
                                weigh(t + 1)
                            before = (u, t - 1) if t else (1 - u, TILES - 1)
                            eng.wait_ge(s.part_ready, c + 1)
                            eng.scalar_tensor_tensor(run_e[:, u, t, :], run_e[:, before[0], before[1], :],
                                                     K.cont[:, bass.ds(c, 1)], part_e[:, u, t, :], ALU.mult, ALU.add)
                            eng.scalar_tensor_tensor(run[:, u, t, :], run[:, before[0], before[1], :],
                                                     K.cont[:, bass.ds(c, 1)], part[:, t % 2, :], ALU.mult, ALU.add
                                                     ).then_inc(s.run_ready, 1)
                    for g, u in both:
                        eng.wait_ge(s.agg_turned, done(g))
                        eng.tensor_copy(aggT[:, u, 0, :], psA[u][0][:, :]).then_inc(s.aggT0, 1)
                    for g, u in both:
                        eng.wait_ge(s.zT_ready, g + 2)
                        eng.tensor_scalar(hT[:, u, :], zT[:, u, :], 0.0, None, ALU.max).then_inc(s.hT_ready, 1)
                    for g, u in both:
                        eng.wait_ge(s.rows_ready, g + 1)
                        eng.wait_ge(s.free, freed(g))
                        if not last:
                            eng.tensor_scalar(K.sc_next[:, :, bass.ts(g, TILES)],
                                              psS[:, 16 * u:16 * u + 16].rearrange("p (t c) -> p c t", c=4), 0.0, None, ALU.add)
                            eng.tensor_copy(rows[:, u, :, D:ROWW], psS[:, 16 * u:16 * u + 16].rearrange("p (t c) -> p t c", c=4))
                        eng.tensor_copy(rows[:, u, :, 0:D], by_tile(psR, TILES)).then_inc(s.rows_done, 1)

            @block.scalar
            def _(eng):
                eng.preload_act_table(ACT.Relu)
                eng.sem_inc(s.looped, 2)
                eng.sem_inc(s.edgeT_ready, 1)
                eng.sem_inc(s.zT_ready, 1)
                for i, both in batches(eng, n):
                    for g, u in both:
                        eng.wait_ge((s.own0_in, s.own1_in)[u], (i + 1) * 16)
                        eng.wait_ge(s.agg_turned, freed(g))
                        eng.sem_inc(s.gate, 1)
                        for t in range(TILES):
                            for h in range(H):
                                ins = eng.activation(loop[:, u, t, h, :], own[:, u, t, 0:D], ACT.Relu,
                                                     scale=alpha_self[:, h, bass.ds(g * TILES + t, 1)])
                        ins.then_inc(s.looped, 1)
                    for g, u in both:
                        eng.wait_ge(s.agg_turned, done(g))
                        eng.activation(aggT[:, u, 1, :], psA[u][1][:, :], ACT.Copy).then_inc(s.aggT1, 1)
                        eng.activation(edgeT[:, u, :], psE[0:E2, :], ACT.Copy).then_inc(s.edgeT_ready, 1)
                    for g, u in both:
                        eng.wait_ge(s.mixed, g + 1)
                        eng.activation(zT[:, u, :], psZ[:, :], ACT.Identity, bias=K.gat_bias[:, l:l + 1]
                                       ).then_inc(s.zT_ready, 1)

            @block.tensor
            def _(eng):
                eng.sem_inc(s.agg_turned, 2)
                for i, both in batches(eng, n):
                    for g, u in both:
                        eng.wait_ge(s.run_ready, g * TILES + 2 + TILES)
                        eng.wait_ge(s.looped, done(g))
                        for t in range(TILES):
                            for h in range(H):
                                o = psA[u][h][:, t * P:(t + 1) * P]
                                eng.matmul(o, run[:, u, t, h * D:(h + 1) * D], K.ident[:, :], is_transpose=True,
                                           start=True, stop=False)
                                eng.matmul(o, loop[:, u, t, h, :], K.ident[:, :], is_transpose=True, start=False, stop=True)
                        eng.wait_ge(s.edgeT_ready, g + 1)
                        for t in range(TILES):
                            mm = eng.transpose(psE[0:E2, t * P:(t + 1) * P], run_e[:, u, t, :], K.ident[:, :])
                        mm.then_inc(s.agg_turned, 1)
                    for g, u in both:
                        eng.wait_ge(s.aggT0, g + 1)
                        eng.wait_ge(s.aggT1, g + 1)
                        eng.wait_ge(s.edgeT_ready, g + 2)
                        eng.wait_ge(s.zT_ready, g + 1)
                        for h in range(H):
                            eng.matmul(psZ[:, :], K.gat_wh[:, l, h, :], aggT[:, u, h, :], start=(h == 0), stop=False)
                        eng.matmul(psZ[:, :], K.gat_ewT[:, l, :], edgeT[:, u, :], start=False, stop=True).then_inc(s.mixed, 1)
                    for g, u in both:
                        eng.wait_ge(s.hT_ready, g + 1)
                        eng.wait_ge(s.rows_done, g + 1)
                        for t in range(TILES):
                            mm = eng.transpose(psR[:, t * P:(t + 1) * P], zT[:, u, t * P:(t + 1) * P], K.ident[:, :])
                            if not last:
                                mm = eng.matmul(psS[:, 16 * u + 4 * t:16 * u + 4 * t + 4], hT[:, u, t * P:(t + 1) * P],
                                                K.gat_v[:, l + 1, :], start=True, stop=True)
                        mm.then_inc(s.rows_ready, 1)


def gat_extra(nc, K, l, alpha_self):
    C, H = K.cols, GAT_HEADS
    last = l == GAT_LAYERS - 1
    table = K.gat_out if last else K.tables[l + 1]
    first, w = (0, D) if last else (K.rows, ROWW)
    with ExitStack() as ctx:
        A = Buffers(nc, ctx, f"gatx{l}")
        own, rows = A.sb("own", [P, ROWW]), A.sb("rows", [P, ROWW])
        piece, ends = A.sb("piece", [P, w]), A.sb("ends", [P, D])
        loop, loopT = A.sb("loop", [P, H, D]), A.sb("loopT", [P, H * D])
        zT, hT = A.sb("zT", [P, P]), A.sb("hT", [P, P])
        psA, psZ, psR = A.ps("psA", [P, H * D]), A.ps("psZ", [P, P]), A.ps("psR", [P, ROWW])
        s = A.sems((
            "own_in", "piece_in", "ends_in", "ends_ready", "looped", "turned", "loopT_ready", "mixed", "zT_ready",
            "hT_ready", "rows_ready", "rows_done", "stored"))
        with nc.Block() as block:
            @block.sync
            def _(eng):
                eng.dma_start(own[:, :], slot_rows(K, K.tables[l], K.rows, C // TILES)[:, 0, :]).then_inc(s.own_in, 16)
                ends_of = table[first:first + P * C, 0:D].rearrange("(p c) w -> p c w", p=P)
                eng.dma_start(ends[:, :], ends_of[:, C - 1, :]).then_inc(s.ends_in, 16)
                eng.wait_ge(s.rows_done, 1)
                eng.dma_start(slot_rows(K, table, first, C // TILES)[:, 0, :], rows[:, 0:w]).then_inc(s.stored, 16)
                eng.wait_ge(s.stored, 16)

            @block.gpsimd
            def _(eng):
                gather(eng, table[0:first + P * C, :], (K.part_slot if last else K.part_row)[:, :], piece[:, :], s.piece_in)

            @block.vector
            def _(eng):
                eng.wait_ge(s.ends_in, 16)
                eng.tensor_tensor(ends[:, :], ends[:, :], K.gat_bias_rep[:, l, :], ALU.subtract).then_inc(s.ends_ready, 1)
                eng.wait_ge(s.turned, 1)
                eng.tensor_copy(loopT[:, :], psA[:, :]).then_inc(s.loopT_ready, 1)
                eng.wait_ge(s.mixed, 1)
                eng.tensor_copy(zT[:, :], psZ[:, :]).then_inc(s.zT_ready, 1)
                eng.tensor_scalar(hT[:, :], psZ[:, :], 0.0, None, ALU.max).then_inc(s.hT_ready, 1)
                eng.wait_ge(s.rows_ready, 1)
                if not last:
                    eng.tensor_copy(K.sc_next[:, :, C], psR[:, D:ROWW])
                eng.tensor_copy(rows[:, 0:w], psR[:, 0:w]).then_inc(s.rows_done, 1)

            @block.scalar
            def _(eng):
                eng.wait_ge(s.own_in, 16)
                for h in range(H):
                    eng.activation(loop[:, h, :], own[:, 0:D], ACT.Relu, scale=alpha_self[:, h, C:C + 1]).then_inc(s.looped, 1)

            @block.tensor
            def _(eng):
                eng.wait_ge(s.looped, H)
                for h in range(H):
                    mm = eng.transpose(psA[:, h * D:(h + 1) * D], loop[:, h, :], K.ident[:, :])
                mm.then_inc(s.turned, 1)
                eng.wait_ge(s.piece_in, 16)
                eng.wait_ge(s.ends_ready, 1)
                eng.wait_ge(s.loopT_ready, 1)
                for h in range(H):
                    eng.matmul(psZ[:, :], K.gat_wh[:, l, h, :], loopT[:, h * D:(h + 1) * D], start=(h == 0), stop=False)
                eng.matmul(psZ[:, :], piece[:, 0:D], K.ident[:, :], start=False, stop=False)
                eng.matmul(psZ[:, :], ends[:, :], K.carry[:, :], start=False, stop=True).then_inc(s.mixed, 1)
                eng.wait_ge(s.zT_ready, 1)
                eng.wait_ge(s.hT_ready, 1)
                mm = eng.transpose(psR[:, 0:D], zT[:, :], K.ident[:, :])
                if not last:
                    mm = eng.matmul(psR[:, D:ROWW], hT[:, :], K.gat_v[:, l + 1, :], start=True, stop=True)
                mm.then_inc(s.rows_ready, 1)


def gat_to_hgt(nc, K):
    C = K.cols
    n = C // TILES
    with ExitStack() as ctx:
        A = Buffers(nc, ctx, "to_hgt")
        z, x = A.sb("z", [P, 2, TILES, D]), A.sb("x", [P, 2, TILES, D])
        x1, rows, q = (A.sb(m, [P, 2, TILES, D]) for m in ("x1", "rows", "q"))
        hT = A.sb("hT", [P, 2, GROUP])
        st, mv, rstd = A.sb("st", [P, 2, TILES, 6]), A.sb("mv", [P, 2, TILES, 2]), A.sb("rstd", [P, 2, TILES])
        psT = [A.ps(f"psT{u}", [P, GROUP]) for u in range(2)]
        psQ = [A.ps(f"psQ{u}", [P, GROUP]) for u in range(2)]
        s = A.sems((
            "in0", "in1", "summed", "stats", "rstd_ready", "normed", "turned", "copiedT", "projected", "q_done",
            "stored", "free", "step", "gate"))
        with nc.Block() as block:
            @block.sync
            def _(eng):
                def load(both):
                    for g, u in both:
                        m = tiles_of(g, n)
                        eng.wait_ge(s.summed, freed(g))
                        eng.dma_start(z[:, u, 0:m, :], slot_rows(K, K.gat_out, 0, g)).then_inc((s.in0, s.in1)[u], 16)
                        eng.dma_start(x[:, u, 0:m, :], slot_rows(K, K.resid, 0, g)).then_inc((s.in0, s.in1)[u], 16)

                eng.sem_inc(s.free, 2)
                load(batch(0, n, 1))
                for i, both, j, ahead in batches_ahead(eng, n, 1):
                    load(ahead)
                    for g, u in both:
                        m = tiles_of(g, n)
                        eng.wait_ge(s.q_done, g + 1)
                        eng.dma_start(slot_rows(K, K.tables[5], K.rows, g), rows[:, u, 0:m, :]).then_inc(s.stored, 16)
                        eng.dma_start(slot_rows(K, K.resid, 0, g), x1[:, u, 0:m, :]).then_inc(s.stored, 16)
                        eng.dma_start(slot_rows(K, K.hgt_q, 0, g), q[:, u, 0:m, :]).then_inc(s.stored, 16)
                    eng.wait_ge(s.stored, i * 96 + 48 * len(both))
                    eng.sem_inc(s.free, 2)

            @block.gpsimd
            def _(eng):
                for i, both in batches(eng, n, 1):
                    for g, u in both:
                        eng.wait_ge(s.stats, g + 1)
                        eng.tensor_tensor(rstd[:, u, :], mv[:, u, :, 1], K.minus_half[:, :], ALU.pow
                                          ).then_inc(s.rstd_ready, 1)

            @block.vector
            def _(eng):
                eng.memset(mv[:, :, :, :], 1.0).then_inc(s.step, 1)
                eng.wait_ge(s.step, 1)
                eng.sem_inc(s.summed, 2)
                for i, both in batches(eng, n, 1):
                    step = LoopOrder(eng, s.step, 6, i, 1)
                    for g, u in both:
                        m = tiles_of(g, n)
                        eng.wait_ge((s.in0, s.in1)[u], (i + 1) * 32)
                        eng.wait_ge(s.free, freed(g))
                        eng.tensor_tensor(x1[:, u, 0:m, :], z[:, u, 0:m, :], x[:, u, 0:m, :], ALU.add).then_inc(s.summed, 1)
                    for g, u in both:
                        eng.wait_ge(s.summed, done(g))
                        stats_of(eng, step, s.gate, x1[:, u, :, :], st[:, u, :, :], mv[:, u, :, :], tiles_of(g, n)
                                 ).then_inc(s.stats, 1)
                    for g, u in both:
                        eng.wait_ge(s.rstd_ready, g + 1)
                        normalised(eng, step, x1[:, u, :, :], mv[:, u, :, :], rstd[:, u, :], rows[:, u, :, :],
                                   tiles_of(g, n)).then_inc(s.normed, 1)
                    for g, u in both:
                        m = tiles_of(g, n)
                        eng.wait_ge(s.projected, g + 1)
                        eng.tensor_copy(q[:, u, 0:m, :], by_tile(psQ[u], m)).then_inc(s.q_done, 1)

            @block.tensor
            def _(eng):
                for i, both in batches(eng, n, 1):
                    for g, u in both:
                        eng.wait_ge(s.normed, g + 1)
                        turn_tiles(eng, K, psT[u], rows[:, u, :, :], tiles_of(g, n)).then_inc(s.turned, 1)
                    for g, u in both:
                        eng.wait_ge(s.copiedT, g + 1)
                        for t in range(tiles_of(g, n)):
                            o = psQ[u][:, t * P:(t + 1) * P]
                            eng.matmul(o, K.ones[0:1, :], K.bias_rows[0:1, 0, :], start=True, stop=False)
                            mm = eng.matmul(o, hT[:, u, t * P:(t + 1) * P], K.hgt_wq[:, :], start=False, stop=True)
                        mm.then_inc(s.projected, 1)

            @block.scalar
            def _(eng):
                eng.preload_act_table(ACT.Copy)
                for i, both in batches(eng, n, 1):
                    for g, u in both:
                        w = tiles_of(g, n) * P
                        eng.wait_ge(s.turned, g + 1)
                        eng.activation(hT[:, u, 0:w], psT[u][:, 0:w], ACT.Copy).then_inc(s.copiedT, 1)



def typed_edges(nc, K, kind, V, score):
    C = K.cols
    n = C // TILES
    hgt = kind == "hgt"
    types = HGT_RELS if hgt else CAT_TYPES
    mask = K.rel_mask if hgt else K.type_mask
    src_table, dst_table = (K.tables[5], K.hgt_q) if hgt else (K.tables[7], K.cat_si)
    wd = dst_table.shape[1]
    wo = 2 * D if hgt else D + CAT_S
    heads = HGT_HEADS if hgt else CAT_HEADS
    with ExitStack() as ctx:
        A = Buffers(nc, ctx, kind)
        at, at_d = A.sb("at", [P, 2, TILES], I32), A.sb("at_d", [P, 2, TILES], I32)
        src, dst = A.sb("src", [P, 2, TILES, D]), A.sb("dst", [P, 2, TILES, wd])
        diag = A.sb("diag", [P, 2, TILES, types, P])
        hT = A.sb("hT", [P, 2, TILES, types * P])
        prod = A.sb("prod", [P, TILES, wd])
        part = A.sb("part", [P, TILES, CAT_S])
        psT = [A.ps(f"psT{t}", [P, types * P]) for t in range(TILES)]
        psO = [A.ps(f"psO{t}", [P, wo]) for t in range(TILES)]
        s = A.sems((
            "indexed", "e0_in", "e1_in", "diag_ready", "turned", "copiedT", "made", "taken", "step", "gate"))
        with nc.Block() as block:
            @block.gpsimd
            def _(eng):
                eng.sem_inc(s.taken, 2)
                for i, both in batches(eng, n):
                    for g, u in both:
                        eng.wait_ge(s.taken, freed(g))
                        eng.sem_inc(s.gate, 1)
                        eng.tensor_copy(at[:, u, :], K.src_row[:, bass.ts(g, TILES)])
                        eng.tensor_copy(at_d[:, u, :], K.dst_slot[:, bass.ts(g, TILES)]).then_inc(s.indexed, 1)
                        eng.wait_ge(s.indexed, g + 1)
                        eng.sem_inc(s.gate, 1)
                        for t in range(TILES):
                            gather(eng, src_table, at[:, u, t:t + 1], src[:, u, t, :], (s.e0_in, s.e1_in)[u])
                            gather(eng, dst_table, at_d[:, u, t:t + 1], dst[:, u, t, :], (s.e0_in, s.e1_in)[u])

            @block.tensor
            def _(eng):
                for i, both in batches(eng, n):
                    for g, u in both:
                        eng.wait_ge((s.e0_in, s.e1_in)[u], (i + 1) * 32 * TILES)
                        eng.wait_ge(s.diag_ready, g + 1)
                        for t in range(TILES):
                            mm = eng.matmul(psT[t][:, :], src[:, u, t, :], diag[:, u, t, :, :].rearrange("p r q -> p (r q)"),
                                            start=True, stop=True)
                            mm.then_inc(s.turned, 1)
                        eng.wait_ge(s.taken, g + 2)
                        for t in range(TILES):
                            eng.wait_ge(s.copiedT, g * TILES + t + 1)
                            for r in range(types):
                                w = (K.hgt_kv if hgt else K.cat_wu)[:, r, :]
                                mm = eng.matmul(psO[t][:, :], hT[:, u, t, r * P:(r + 1) * P], w, start=(r == 0),
                                                stop=(not hgt and r == types - 1))
                            if hgt:
                                for r in range(types):
                                    mm = eng.matmul(psO[t][:, :], diag[:, u, t, r, :], K.hgt_kvb[:, r, :], start=False,
                                                    stop=(r == types - 1))
                        mm.then_inc(s.made, 1)

            @block.scalar
            def _(eng):
                eng.preload_act_table(ACT.Copy)
                for i, both in batches(eng, n):
                    for g, u in both:
                        for t in range(TILES):
                            eng.wait_ge(s.turned, g * TILES + t + 1)
                            eng.activation(hT[:, u, t, :], psT[t][:, :], ACT.Copy).then_inc(s.copiedT, 1)

            @block.vector
            def _(eng):
                for i, both in batches(eng, n):
                    step = LoopOrder(eng, s.step, 2 * (1 if hgt else 5), i)

                    def masked_identities(g, u):
                        eng.wait_ge(s.taken, freed(g))
                        for t in range(TILES):
                            for r in range(types):
                                ins = eng.tensor_scalar(diag[:, u, t, r, :], K.ident[:, :],
                                                        mask[:, r, bass.ds(g * TILES + t, 1)], None, ALU.mult)
                        ins.then_inc(s.diag_ready, 1)

                    for g, u in both:
                        masked_identities(g, u)
                    for g, u in both:
                        eng.wait_ge(s.made, g + 1)
                        to = V[:, bass.ds(g * TILES + 1, TILES), :]
                        for t in range(TILES):
                            o = psO[t][:, D:2 * D] if hgt else psO[t][:, 0:D]
                            eng.tensor_scalar(column(V, g * TILES + t + 1), o, 0.0, None, ALU.add)
                            if hgt:
                                ins = eng.tensor_tensor(prod[:, t, :], psO[t][:, 0:D], dst[:, u, t, :], ALU.mult)
                            else:
                                m = spread(mask[:, :, bass.ds(g * TILES + t, 1)].rearrange("p r one -> p (r one)"), 2, CAT_S)
                                ins = eng.tensor_tensor(prod[:, t, :].rearrange("p (r s) -> p r s", r=types),
                                                        dst[:, u, t, :].rearrange("p (r s) -> p r s", r=types), m, ALU.mult)
                        step(ins)
                        if hgt:
                            for t in range(TILES):
                                ins = eng.tensor_reduce(score[:, :, bass.ds(g * TILES + t, 1)],
                                                        prod[:, t, :].rearrange("p (h d) -> p h d", h=heads), AX.X, ALU.add)
                        else:
                            for t in range(TILES):
                                ins = eng.tensor_reduce(part[:, t, :], prod[:, t, :].rearrange("p (r s) -> p s r", r=types),
                                                        AX.X, ALU.add)
                            step(ins)
                            for t in range(TILES):
                                ins = eng.tensor_tensor(part[:, t, :], part[:, t, :], psO[t][:, D:D + CAT_S], ALU.add)
                            step(ins)
                            step(eng.scalar_tensor_tensor(part[:, :, :], part[:, :, :], 0.2, part[:, :, :], ALU.mult, ALU.max))
                            for t in range(TILES):
                                pk = spread(K.cat_pk[:, :], 2, CAT_HEADS)
                                ins = eng.tensor_tensor(part[:, t, :].rearrange("p (k h) -> p k h", k=CAT_CONF),
                                                        part[:, t, :].rearrange("p (k h) -> p k h", k=CAT_CONF), pk, ALU.mult)
                            step(ins)
                            for t in range(TILES):
                                ins = eng.tensor_reduce(score[:, :, bass.ds(g * TILES + t, 1)],
                                                        part[:, t, :].rearrange("p (k h) -> p h k", k=CAT_CONF), AX.X, ALU.add)
                        ins.then_inc(s.taken, 1)


def typed_weights(nc, K, kind, score):
    C = K.cols
    hgt = kind == "hgt"
    types, heads = (HGT_RELS, HGT_HEADS) if hgt else (CAT_TYPES, CAT_HEADS)
    mask = K.rel_mask if hgt else K.type_mask
    with ExitStack() as ctx:
        A = Buffers(nc, ctx, kind + "_attend")
        R = RunTotals(K, A, types * heads)
        val = A.sb("val", [P, types * heads, C])
        top = A.sb("top", [P, heads, C])
        away = A.sb("away", [P, types, C])
        imp = A.sb("imp", [P, C])
        step_sem, to_exp, from_exp = A.sem("step"), A.sem("to_exp"), A.sem("from_exp")
        with nc.Block() as block:
            @block.vector
            def _(eng):
                step = Order(eng, step_sem)

                def of_type(r):
                    return val[:, r * heads:(r + 1) * heads, :]

                def own_type():
                    for r in range(types):
                        step(eng.tensor_tensor(of_type(r), of_type(r), spread(mask[:, r, :], 1, heads), ALU.mult))
                    step(eng.tensor_tensor(top[:, :, :], of_type(0), of_type(1), ALU.add))
                    for r in range(2, types):
                        step(eng.tensor_tensor(top[:, :, :], top[:, :, :], of_type(r), ALU.add))

                step(eng.tensor_scalar(away[:, :, :], mask[:, :, :], 1.0, -FAR, ALU.subtract, ALU.mult))
                for r in range(types):
                    step(eng.tensor_tensor(of_type(r), score[:, :, :], spread(mask[:, r, :], 1, heads), ALU.mult))
                    step(eng.tensor_tensor(of_type(r), of_type(r), spread(away[:, r, :], 1, heads), ALU.add))
                R.on_vector(eng, step, val, ALU.max, types * heads)
                own_type()
                step(eng.tensor_tensor(score[:, :, :], score[:, :, :], top[:, :, :], ALU.subtract))
                eng.sem_inc(to_exp, 1)
                eng.wait_ge(from_exp, 1)
                for r in range(types):
                    step(eng.tensor_tensor(of_type(r), score[:, :, :], spread(mask[:, r, :], 1, heads), ALU.mult))
                R.on_vector(eng, step, val, ALU.add, types * heads)
                own_type()
                step(eng.reciprocal(top[:, :, :], top[:, :, :]))
                step(eng.tensor_tensor(score[:, :, :], score[:, :, :], top[:, :, :], ALU.mult))
                if not hgt:
                    step(eng.tensor_scalar(imp[:, :], mask[:, 0, :], K.cat_imp[:, 0:1], None, ALU.mult))
                    for r in range(1, types):
                        step(eng.scalar_tensor_tensor(imp[:, :], mask[:, r, :], K.cat_imp[:, r:r + 1], imp[:, :],
                                                      ALU.mult, ALU.add))
                    step(eng.tensor_tensor(score[:, :, :], score[:, :, :], spread(imp[:, :], 1, heads), ALU.mult))

            @block.tensor
            def _(eng):
                R.on_tensor(eng, types * heads)
                R.on_tensor(eng, types * heads)

            @block.scalar
            def _(eng):
                eng.preload_act_table(ACT.Exp)
                eng.wait_ge(to_exp, 1)
                eng.activation(score[:, :, :], score[:, :, :], ACT.Exp).then_inc(from_exp, 1)


def run_sums(nc, K, tag, V, weight, heads):
    C = K.cols
    n = C // TILES
    with ExitStack() as ctx:
        A = Buffers(nc, ctx, tag)
        piece, rows = A.sb("piece", [P, D]), A.sb("rows", [P, D])
        psX = A.ps("psX", [P, D])
        s = A.sems(("weighed", "summed", "stored", "piece_in", "mixed", "rows_done",
                                                     "out", "gate"))
        with nc.Block() as block:
            @block.vector
            def _(eng):
                eng.memset(V[:, 0, :], 0.0).then_inc(s.summed, 1)
                for i, both in batches(eng, n):
                    for g, u in both:
                        to = V[:, bass.ds(g * TILES + 1, TILES), :]
                        if weight is not None:
                            to = to.rearrange("p t (h d) -> p t h d", h=heads)
                            w = weight[:, :, bass.ts(g, TILES)].rearrange("p h t -> p t h")
                            eng.tensor_tensor(to, to, spread(w, 3, D // heads), ALU.mult).then_inc(s.weighed, 1)
                            eng.wait_ge(s.weighed, g + 1)
                        for t in range(TILES):
                            c = g * TILES + t
                            eng.wait_ge(s.summed, c + 1)
                            eng.scalar_tensor_tensor(column(V, c + 1), column(V, c), K.cont[:, bass.ds(c, 1)], column(V, c + 1),
                                                     ALU.mult, ALU.add).then_inc(s.summed, 1)
                eng.wait_ge(s.mixed, 1)
                eng.wait_ge(s.piece_in, 16)
                eng.tensor_tensor(rows[:, :], piece[:, :], psX[:, :], ALU.add).then_inc(s.rows_done, 1)

            @block.tensor
            def _(eng):
                eng.wait_ge(s.summed, C + 1)
                eng.matmul(psX[:, :], K.carry[:, :], V[:, C, :], start=True, stop=True).then_inc(s.mixed, 1)

            @block.sync
            def _(eng):
                for i, both in batches(eng, n):
                    for g, u in both:
                        eng.wait_ge(s.summed, g * TILES + TILES + 1)
                        eng.dma_start(slot_rows(K, K.sums, 0, g), V[:, bass.ds(g * TILES + 1, TILES), :]).then_inc(s.stored, 16)
                eng.wait_ge(s.stored, 16 * n)
                eng.sem_inc(s.out, 1)
                eng.wait_ge(s.rows_done, 1)
                eng.dma_start(slot_rows(K, K.sums, 0, n)[:, 0, :], rows[:, :]).then_inc(s.stored, 16)
                eng.wait_ge(s.stored, 16 * n + 16)

            @block.gpsimd
            def _(eng):
                eng.wait_ge(s.out, 1)
                gather(eng, K.sums[0:P * C, :], K.part_slot[:, :], piece[:, :], s.piece_in)


def hgt_to_gcn(nc, K):
    C = K.cols
    n = C // TILES
    with ExitStack() as ctx:
        A = Buffers(nc, ctx, "to_gcn")
        sums, x, h, x2, rows = (A.sb(m, [P, 2, TILES, D]) for m in ("sums", "x", "h", "x2", "rows"))
        hT = A.sb("hT", [P, 2, GROUP])
        st, mv, rstd = A.sb("st", [P, 2, TILES, 6]), A.sb("mv", [P, 2, TILES, 2]), A.sb("rstd", [P, 2, TILES])
        psT = [A.ps(f"psT{u}", [P, GROUP]) for u in range(2)]
        psO = [A.ps(f"psO{u}", [P, GROUP]) for u in range(2)]
        s = A.sems((
            "in0", "in1", "turned", "gelu_done", "projected", "summed", "stats", "rstd_ready", "rows_done", "stored",
            "free", "step", "gate"))
        with nc.Block() as block:
            @block.sync
            def _(eng):
                def load(both):
                    for g, u in both:
                        m = tiles_of(g, n)
                        eng.wait_ge(s.summed, freed(g))
                        for to, of, first in ((sums, K.sums, 0), (x, K.resid, 0), (h, K.tables[5], K.rows)):
                            eng.dma_start(to[:, u, 0:m, :], slot_rows(K, of, first, g)).then_inc((s.in0, s.in1)[u], 16)

                eng.sem_inc(s.free, 2)
                load(batch(0, n, 1))
                for i, both, j, ahead in batches_ahead(eng, n, 1):
                    load(ahead)
                    for g, u in both:
                        m = tiles_of(g, n)
                        eng.wait_ge(s.rows_done, g + 1)
                        eng.dma_start(slot_rows(K, K.tables[6], K.rows, g), rows[:, u, 0:m, :]).then_inc(s.stored, 16)
                        eng.dma_start(slot_rows(K, K.resid, 0, g), x2[:, u, 0:m, :]).then_inc(s.stored, 16)
                    eng.wait_ge(s.stored, i * 64 + 32 * len(both))
                    eng.sem_inc(s.free, 2)

            @block.tensor
            def _(eng):
                for i, both in batches(eng, n, 1):
                    for g, u in both:
                        eng.wait_ge((s.in0, s.in1)[u], (i + 1) * 48)
                        turn_tiles(eng, K, psT[u], sums[:, u, :, :], tiles_of(g, n)).then_inc(s.turned, 1)
                    for g, u in both:
                        eng.wait_ge(s.gelu_done, g + 1)
                        eng.wait_ge(s.summed, freed(g))
                        for t in range(tiles_of(g, n)):
                            o = psO[u][:, t * P:(t + 1) * P]
                            eng.matmul(o, K.ones[0:1, :], K.bias_rows[0:1, 3, :], start=True, stop=False)
                            mm = eng.matmul(o, hT[:, u, t * P:(t + 1) * P], K.hgt_wa[:, :], start=False, stop=True)
                        mm.then_inc(s.projected, 1)

            @block.scalar
            def _(eng):
                eng.preload_act_table(ACT.Gelu)
                for i, both in batches(eng, n, 1):
                    for g, u in both:
                        w = tiles_of(g, n) * P
                        eng.wait_ge(s.turned, g + 1)
                        eng.activation(hT[:, u, 0:w], psT[u][:, 0:w], ACT.Gelu).then_inc(s.gelu_done, 1)

            @block.gpsimd
            def _(eng):
                for i, both in batches(eng, n, 1):
                    for g, u in both:
                        eng.wait_ge(s.stats, g + 1)
                        eng.tensor_tensor(rstd[:, u, :], mv[:, u, :, 1], K.minus_half[:, :], ALU.pow
                                          ).then_inc(s.rstd_ready, 1)

            @block.vector
            def _(eng):
                eng.memset(mv[:, :, :, :], 1.0).then_inc(s.step, 1)
                eng.wait_ge(s.step, 1)
                eng.sem_inc(s.summed, 2)
                for i, both in batches(eng, n, 1):
                    step = LoopOrder(eng, s.step, 10, i, 1)
                    for g, u in both:
                        m = tiles_of(g, n)
                        eng.wait_ge(s.projected, g + 1)
                        eng.wait_ge(s.free, freed(g))
                        eng.wait_ge((s.in0, s.in1)[u], (i + 1) * 48)
                        step(eng.scalar_tensor_tensor(x2[:, u, 0:m, :], h[:, u, 0:m, :], K.hgt_gate[:, 1:2], x[:, u, 0:m, :],
                                                      ALU.mult, ALU.add))
                        eng.tensor_tensor(x2[:, u, 0:m, :], x2[:, u, 0:m, :], by_tile(psO[u], m), ALU.add).then_inc(s.summed, 1)
                    for g, u in both:
                        eng.wait_ge(s.summed, done(g))
                        stats_of(eng, step, s.gate, x2[:, u, :, :], st[:, u, :, :], mv[:, u, :, :], tiles_of(g, n)
                                 ).then_inc(s.stats, 1)
                    for g, u in both:
                        m = tiles_of(g, n)
                        eng.wait_ge(s.rstd_ready, g + 1)
                        step(normalised(eng, step, x2[:, u, :, :], mv[:, u, :, :], rstd[:, u, :], rows[:, u, :, :], m))
                        eng.tensor_tensor(rows[:, u, 0:m, :], rows[:, u, 0:m, :], spread(K.dinv[:, slot_cols(g, n)], 2, D),
                                          ALU.mult).then_inc(s.rows_done, 1)


def gcn_to_cat(nc, K):
    C = K.cols
    n = C // TILES
    SI = CAT_TYPES * CAT_S
    with ExitStack() as ctx:
        A = Buffers(nc, ctx, "to_cat")
        sums, x, own, x3, rows, gelu, out = (A.sb(m, [P, 2, TILES, D]) for m in ("sums", "x", "own", "x3", "rows", "gelu", "out"))
        si = A.sb("si", [P, 2, TILES, SI])
        hT, h7T = A.sb("hT", [P, 2, GROUP]), A.sb("h7T", [P, 2, GROUP])
        st, mv, rstd = A.sb("st", [P, 2, TILES, 6]), A.sb("mv", [P, 2, TILES, 2]), A.sb("rstd", [P, 2, TILES])
        psT = [A.ps(f"psT{u}", [P, GROUP]) for u in range(2)]
        psO = [A.ps(f"psO{u}", [P, GROUP]) for u in range(2)]
        psI = [A.ps(f"psI{u}", [P, TILES * SI]) for u in range(2)]
        s = A.sems((
            "in0", "in1", "scaled", "turned", "copiedT", "projected", "gelu_done", "x3_done", "stats", "rstd_ready",
            "normed", "turned7", "copied7", "projected7", "rows_done", "stored", "free", "step", "gate"))
        with nc.Block() as block:
            @block.sync
            def _(eng):
                def load(both):
                    for g, u in both:
                        m = tiles_of(g, n)
                        eng.wait_ge(s.x3_done, freed(g))
                        for to, of, first in ((sums, K.sums, 0), (x, K.resid, 0), (own, K.tables[6], K.rows)):
                            eng.dma_start(to[:, u, 0:m, :], slot_rows(K, of, first, g)).then_inc((s.in0, s.in1)[u], 16)

                eng.sem_inc(s.free, 2)
                load(batch(0, n, 1))
                for i, both, j, ahead in batches_ahead(eng, n, 1):
                    load(ahead)
                    for g, u in both:
                        m = tiles_of(g, n)
                        eng.wait_ge(s.rows_done, g + 1)
                        eng.dma_start(slot_rows(K, K.tables[7], K.rows, g), rows[:, u, 0:m, :]).then_inc(s.stored, 16)
                        eng.dma_start(slot_rows(K, K.resid, 0, g), out[:, u, 0:m, :]).then_inc(s.stored, 16)
                        eng.dma_start(slot_rows(K, K.cat_si, 0, g), si[:, u, 0:m, :]).then_inc(s.stored, 16)
                    eng.wait_ge(s.stored, i * 96 + 48 * len(both))
                    eng.sem_inc(s.free, 2)

            @block.tensor
            def _(eng):
                for i, both in batches(eng, n, 1):
                    for g, u in both:
                        eng.wait_ge(s.scaled, g + 1)
                        turn_tiles(eng, K, psT[u], sums[:, u, :, :], tiles_of(g, n)).then_inc(s.turned, 1)
                    for g, u in both:
                        eng.wait_ge(s.copiedT, g + 1)
                        for t in range(tiles_of(g, n)):
                            o = psO[u][:, t * P:(t + 1) * P]
                            eng.matmul(o, K.ones[0:1, :], K.bias_rows[0:1, 1, :], start=True, stop=False)
                            mm = eng.matmul(o, hT[:, u, t * P:(t + 1) * P], K.gcn_w[:, :], start=False, stop=True)
                        mm.then_inc(s.projected, 1)
                    for g, u in both:
                        eng.wait_ge(s.normed, g + 1)
                        turn_tiles(eng, K, psT[u], rows[:, u, :, :], tiles_of(g, n)).then_inc(s.turned7, 1)
                    for g, u in both:
                        eng.wait_ge(s.copied7, g + 1)
                        for t in range(tiles_of(g, n)):
                            o, h = psO[u][:, t * P:(t + 1) * P], h7T[:, u, t * P:(t + 1) * P]
                            eng.matmul(o, K.ones[0:1, :], K.bias_rows[0:1, 2, :], start=True, stop=False)
                            eng.matmul(o, h, K.cat_wu[:, 0, 0:D], start=False, stop=True)
                            mm = eng.matmul(psI[u][:, t * SI:(t + 1) * SI], h, K.cat_ui[:, :, :].rearrange("p t s -> p (t s)"),
                                            start=True, stop=True)
                        mm.then_inc(s.projected7, 1)

            @block.scalar
            def _(eng):
                eng.preload_act_table(ACT.Gelu)
                for i, both in batches(eng, n, 1):
                    for g, u in both:
                        w = tiles_of(g, n) * P
                        eng.wait_ge(s.turned, g + 1)
                        eng.activation(hT[:, u, 0:w], psT[u][:, 0:w], ACT.Copy).then_inc(s.copiedT, 1)
                    for g, u in both:
                        m = tiles_of(g, n)
                        eng.wait_ge(s.projected, g + 1)
                        eng.activation(gelu[:, u, 0:m, :], by_tile(psO[u], m), ACT.Gelu).then_inc(s.gelu_done, 1)
                    for g, u in both:
                        w = tiles_of(g, n) * P
                        eng.wait_ge(s.turned7, g + 1)
                        eng.activation(h7T[:, u, 0:w], psT[u][:, 0:w], ACT.Copy).then_inc(s.copied7, 1)

            @block.gpsimd
            def _(eng):
                for i, both in batches(eng, n, 1):
                    for g, u in both:
                        eng.wait_ge(s.stats, g + 1)
                        eng.tensor_tensor(rstd[:, u, :], mv[:, u, :, 1], K.minus_half[:, :], ALU.pow
                                          ).then_inc(s.rstd_ready, 1)

            @block.vector
            def _(eng):
                eng.memset(mv[:, :, :, :], 1.0).then_inc(s.step, 1)
                eng.wait_ge(s.step, 1)
                eng.sem_inc(s.x3_done, 2)
                for i, both in batches(eng, n, 1):
                    step = LoopOrder(eng, s.step, 8, i, 1)
                    for g, u in both:
                        m = tiles_of(g, n)
                        eng.wait_ge((s.in0, s.in1)[u], (i + 1) * 48)
                        step(eng.tensor_tensor(sums[:, u, 0:m, :], sums[:, u, 0:m, :], own[:, u, 0:m, :], ALU.add))
                        eng.tensor_tensor(sums[:, u, 0:m, :], sums[:, u, 0:m, :], spread(K.dinv[:, slot_cols(g, n)], 2, D),
                                          ALU.mult).then_inc(s.scaled, 1)
                    for g, u in both:
                        m = tiles_of(g, n)
                        eng.wait_ge(s.gelu_done, g + 1)
                        eng.wait_ge(s.free, freed(g))
                        eng.tensor_tensor(x3[:, u, 0:m, :], gelu[:, u, 0:m, :], x[:, u, 0:m, :], ALU.add).then_inc(s.x3_done, 1)
                    for g, u in both:
                        eng.wait_ge(s.x3_done, done(g))
                        stats_of(eng, step, s.gate, x3[:, u, :, :], st[:, u, :, :], mv[:, u, :, :], tiles_of(g, n)
                                 ).then_inc(s.stats, 1)
                    for g, u in both:
                        eng.wait_ge(s.rstd_ready, g + 1)
                        normalised(eng, step, x3[:, u, :, :], mv[:, u, :, :], rstd[:, u, :], rows[:, u, :, :],
                                   tiles_of(g, n)).then_inc(s.normed, 1)
                    for g, u in both:
                        m = tiles_of(g, n)
                        eng.wait_ge(s.projected7, g + 1)
                        eng.tensor_tensor(out[:, u, 0:m, :], by_tile(psO[u], m), x3[:, u, 0:m, :], ALU.add)
                        eng.tensor_copy(si[:, u, 0:m, :], by_tile(psI[u], m, SI)).then_inc(s.rows_done, 1)


def leave_slots(nc, K, out):
    C = K.cols
    n = C // TILES
    with ExitStack() as ctx:
        A = Buffers(nc, ctx, "leave")
        at = A.sb("at", [P, 2, TILES], I32)
        sums, x, rows = (A.sb(m, [P, 2, TILES, D]) for m in ("sums", "x", "rows"))
        s = A.sems(("in0", "in1", "added", "indexed", "stored", "free", "gate"))
        with nc.Block() as block:
            @block.sync
            def _(eng):
                for i, both in batches(eng, n, 1):
                    for g, u in both:
                        m = tiles_of(g, n)
                        eng.wait_ge(s.added, freed(g))
                        eng.dma_start(sums[:, u, 0:m, :], slot_rows(K, K.sums, 0, g)).then_inc((s.in0, s.in1)[u], 16)
                        eng.dma_start(x[:, u, 0:m, :], slot_rows(K, K.resid, 0, g)).then_inc((s.in0, s.in1)[u], 16)

            @block.vector
            def _(eng):
                eng.sem_inc(s.added, 2)
                for i, both in batches(eng, n, 1):
                    for g, u in both:
                        m = tiles_of(g, n)
                        eng.wait_ge((s.in0, s.in1)[u], (i + 1) * 32)
                        eng.wait_ge(s.free, freed(g))
                        eng.tensor_tensor(rows[:, u, 0:m, :], sums[:, u, 0:m, :], x[:, u, 0:m, :], ALU.add).then_inc(s.added, 1)

            @block.gpsimd
            def _(eng):
                eng.sem_inc(s.free, 2)
                for i, both in batches(eng, n, 1):
                    for g, u in both:
                        m = tiles_of(g, n)
                        eng.wait_ge(s.free, freed(g))
                        eng.sem_inc(s.gate, 1)
                        eng.tensor_copy(at[:, u, 0:m], K.node_of[:, slot_cols(g, n)]).then_inc(s.indexed, 1)
                        eng.wait_ge(s.indexed, g + 1)
                        eng.wait_ge(s.added, done(g))
                        eng.sem_inc(s.gate, 1)
                        for t in range(m):
                            eng.indirect_dma_start(out, bass.IndirectOffsetOnAxis(ap=at[:, u, t:t + 1], axis=0),
                                                   rows[:, u, t, :], None, bounds_check=K.rows - 1,
                                                   oob_is_err=False).then_inc(s.stored, 16)
                    eng.wait_ge(s.stored, i * 32 * TILES + 16 * sum(tiles_of(g, n) for g, u in both))
                    eng.sem_inc(s.free, 2)


def gnn_stack(nc, I, out, rows, cols):
    L, C = GAT_LAYERS, cols
    with ExitStack() as ctx:
        A = Buffers(nc, ctx, "k")
        K = Kept(rows, cols)

        def dram(name, shape, dt=F32):
            return nc.dram_tensor(name, shape, dt, kind="Internal").ap()

        K.tables = [dram(f"table{l}", (rows + K.slots, ROWW if l < L else D)) for l in range(L + 3)]
        K.gat_out = dram("gat_out", (K.slots, D))
        K.hgt_q = dram("hgt_q", (K.slots, D))
        K.cat_si = dram("cat_si", (K.slots, CAT_TYPES * CAT_S))
        K.resid = dram("resid", (K.slots, D))
        K.sums = dram("sums", (K.slots, D))
        K.row_of = dram("row_of", (rows, 1), I32)

        sb = A.sb
        K.ones, K.ident, K.carry = (sb(n, [P, P]) for n in ("ones", "ident", "carry"))
        K.gat_wh = sb("gat_wh", [P, L, GAT_HEADS, D])
        K.gat_v, K.gat_u = sb("gat_v", [P, L, 4]), sb("gat_u", [P, L * GAT_HEADS, EDGE_F + 1])
        K.gat_bias, K.gat_bias_rep = sb("gat_bias", [P, L]), sb("gat_bias_rep", [P, L, D])
        K.gat_ewT = sb("gat_ewT", [GAT_HEADS * EDGE_F, L, D])
        K.hgt_wq, K.hgt_wa, K.hgt_ba = sb("hgt_wq", [P, D]), sb("hgt_wa", [P, D]), sb("hgt_ba", [P, D])
        K.hgt_gate = sb("hgt_gate", [P, 2])
        K.hgt_kv, K.hgt_kvb = sb("hgt_kv", [P, HGT_RELS, 2 * D]), sb("hgt_kvb", [P, HGT_RELS, 2 * D])
        K.gcn_w = sb("gcn_w", [P, D])
        K.cat_wu, K.cat_ui = sb("cat_wu", [P, CAT_TYPES, D + CAT_S]), sb("cat_ui", [P, CAT_TYPES, CAT_S])
        K.cat_imp, K.cat_pk = sb("cat_imp", [P, CAT_TYPES]), sb("cat_pk", [P, CAT_CONF])
        K.bias_rows = sb("bias_rows", [1, 4, D])
        K.minus_half = sb("minus_half", [P, TILES])
        K.slot_no, K.own, K.dinv = sb("slot_no", [P, C + 1]), sb("own", [P, C + 1]), sb("dinv", [P, C + 1])
        K.cont, K.goes_on, K.ends, K.restart, K.in_head, K.in_tail, K.inner = (
            sb(n, [P, C]) for n in ("cont", "goes_on", "ends", "restart", "in_head", "in_tail", "inner"))
        K.many = sb("many", [P, 1])
        K.seq_cont, K.seq_goes_on, K.seq_ends, K.seq_restart = (
            sb(n, [16, 2 * P]) for n in ("seq_cont", "seq_goes_on", "seq_ends", "seq_restart"))
        K.rel_mask, K.type_mask = sb("rel_mask", [P, HGT_RELS, C]), sb("type_mask", [P, CAT_TYPES, C])
        K.node_of = sb("node_of", [P, C + 1], I32)
        K.src_row, K.dst_slot = (sb(n, [P, C], I32) for n in ("src_row", "dst_slot"))
        K.part_slot, K.part_row = sb("part_slot", [P, 1], I32), sb("part_row", [P, 1], I32)
        K.sc, K.sc_next = sb("sc_a", [P, 4, C + 1]), sb("sc_b", [P, 4, C + 1])
        with ExitStack() as first_ctx:
            F = Buffers(nc, first_ctx, "first")
            K.from_prev, K.from_next, K.upper = (F.sb(n, [P, P]) for n in ("from_prev", "from_next", "upper"))
            K.gat_wm = F.sb("gat_wm", [P, L, D])
            K.gather_dst, K.slot_row = (F.sb(n, [P, C + 1], I32) for n in ("gather_dst", "slot_row"))
            K.src_node = F.sb("src_node", [P, C], I32)
            prepare_weights(nc, K, I)
            describe_slots(nc, K, I)
            map_rows(nc, K)
            node_pass(nc, K, I, out)
            enter_slots(nc, K, I)
        with ExitStack() as rows_ctx:
            G = rows_ctx.enter_context(nc.sbuf_tensor("source_rows", [P, C + 1, D], F32))
            with ExitStack() as gat_ctx:
                B = Buffers(nc, gat_ctx, "gat")
                src_score, alpha = B.sb("src_score", [P, GAT_HEADS, C]), B.sb("alpha", [P, GAT_HEADS, C])
                alpha_self = B.sb("alpha_self", [P, GAT_HEADS, C + 1])
                for l in range(L):
                    gather_rows(nc, K, l, K.tables[l], ROWW, G, src_score)
                    gat_weights(nc, K, I, l, src_score, alpha, alpha_self)
                    gat_slots(nc, K, I, l, G, alpha, alpha_self)
                    gat_extra(nc, K, l, alpha_self)
                    K.sc, K.sc_next = K.sc_next, K.sc
            gat_to_hgt(nc, K)
            with ExitStack() as hgt_ctx:
                score = Buffers(nc, hgt_ctx, "hgt_s").sb("score", [P, HGT_HEADS, C])
                typed_edges(nc, K, "hgt", G, score)
                typed_weights(nc, K, "hgt", score)
                run_sums(nc, K, "hgt_sums", G, score, HGT_HEADS)
            hgt_to_gcn(nc, K)
            gather_rows(nc, K, 6, K.tables[6], D, G)
            run_sums(nc, K, "gcn_sums", G, None, 1)
            gcn_to_cat(nc, K)
            with ExitStack() as cat_ctx:
                score = Buffers(nc, cat_ctx, "cat_s").sb("score", [P, CAT_HEADS, C])
                typed_edges(nc, K, "cat", G, score)
                typed_weights(nc, K, "cat", score)
                run_sums(nc, K, "cat_sums", G, score, CAT_HEADS)
        leave_slots(nc, K, out)


_NAMES = dict(
    x="x", gat_w="L0_gnn_weights", gat_att="L0_gnn_atts", gat_b="L0_gnn_biases", gat_ew="L0_gnn_edge_ws",
    gat_eb="L0_gnn_edge_bs", hgt_wk="L1_gnn_Wk", hgt_bk="L1_gnn_bk", hgt_wq="L1_gnn_Wq", hgt_bq="L1_gnn_bq",
    hgt_wv="L1_gnn_Wv", hgt_bv="L1_gnn_bv", hgt_a="L1_gnn_a_rel", hgt_m="L1_gnn_m_rel", hgt_p="L1_gnn_p_rel",
    hgt_wa="L1_gnn_Wa", hgt_ba="L1_gnn_ba", hgt_skip="L1_gnn_skip", gcn_w="L2_gnn_W", gcn_b="L2_gnn_b",
    cat_w="L3_gnn_W", cat_att="L3_gnn_att_vectors", cat_conf="L3_gnn_confounder_probs",
    cat_imp="L3_gnn_edge_importance", cat_b="L3_gnn_bias")


def kernel(**inputs):
    import numpy as np
    import concourse.bacc as bacc
    from concourse.bass_utils import run_bass_kernel_spmd as run

    n_nodes, n_edges = inputs["x"].shape[0], inputs["src"].shape[0]
    block = 2 * GROUP
    rows = (n_nodes + 1 + block - 1) // block * block
    cols = (n_edges + P * TILES - 1) // (P * TILES) * TILES
    fill = P * cols - n_edges

    def edges(a, value=0):
        a = np.asarray(a)
        tail = np.full((fill,) + a.shape[1:], value, a.dtype)
        return np.concatenate([a, tail]).reshape((P, cols) + a.shape[1:])

    arrays = {k: np.ascontiguousarray(np.asarray(inputs[v])) for k, v in _NAMES.items()}
    arrays["x"] = np.concatenate([arrays["x"], np.zeros((rows - n_nodes, D), arrays["x"].dtype)])
    arrays["hgt_skip"] = arrays["hgt_skip"].reshape(1, 1)
    arrays["src"], arrays["dst"] = edges(inputs["src"]), edges(inputs["dst"], n_nodes)
    arrays["type2"], arrays["type4"] = edges(inputs["edge_type_2"]), edges(inputs["edge_type_4"])
    arrays["edge_x"] = edges(inputs["edge_attr_16"])

    nc = bacc.Bacc("TRN2", target_bir_lowering=False, num_devices=1)
    I = named({k: nc.dram_tensor(f"in_{k}", a.shape, mybir.dt.from_np(a.dtype), kind="ExternalInput").ap()
                           for k, a in arrays.items()})
    out = nc.dram_tensor("out", (rows, D), F32, kind="ExternalOutput").ap()
    gnn_stack(nc, I, out, rows, cols)
    got = run(nc, [{f"in_{k}": a for k, a in arrays.items()}], core_ids=[0])
    return got.results[0]["out"][:n_nodes]
```

```python
from collections import namedtuple
from contextlib import ExitStack

import concourse.bass as bass
from concourse import mybir

F32 = mybir.dt.float32
I32 = mybir.dt.int32
ALU = mybir.AluOpType
ACT = mybir.ActivationFunctionType
AX = mybir.AxisListType

P = 128
D = 128
TILES = 4
GROUP = TILES * P
BLOCKS, BLOCK = 4, 3 * P
ROWW = D + 4
GAT_HEADS = 2
GAT_LAYERS = 5
EDGE_F = 16
HGT_HEADS, HGT_RELS = 8, 2
CAT_HEADS, CAT_TYPES, CAT_CONF = 4, 4, 5
CAT_S = CAT_CONF * CAT_HEADS
LN_EPS = 1e-5
FAR = -3.0e38
NOWHERE = 1 << 20


class Order:

    def __init__(self, eng, sem):
        self.eng, self.sem, self.n = eng, sem, 0

    def __call__(self, instruction):
        instruction.then_inc(self.sem, 1)
        self.n += 1
        self.eng.wait_ge(self.sem, self.n)


def batch(i, n, extra):
    if isinstance(i, int):
        return [(g, g % 2) for g in (2 * i, 2 * i + 1) if g < n + extra]
    return [(i * 2, 0), (i * 2 + 1, 1)]


def batches(eng, n, extra=0):
    full = n // 2
    if full:
        with eng.Fori(0, full) as i:
            yield i, batch(i, n, extra)
    if batch(full, n, extra):
        yield full, batch(full, n, extra)


def batches_ahead(eng, n, extra=0):
    full = n // 2
    if full > 1:
        with eng.Fori(0, full - 1) as i:
            yield i, batch(i, n, extra), i + 1, batch(i + 1, n, extra)
    for i in range(max(full - 1, 0), full + 1):
        if batch(i, n, extra):
            yield i, batch(i, n, extra), i + 1, batch(i + 1, n, extra)


def overlapped(eng, n, extra=0):
    full = n // 2
    yield 0, batch(0, n, extra), []
    with eng.Fori(1, full) as i:
        yield i, batch(i, n, extra), batch(i - 1, n, extra)
    yield full, batch(full, n, extra), batch(full - 1, n, extra)
    if batch(full, n, extra):
        yield full + 1, [], batch(full, n, extra)


def transfers(eng, n, extra=0):
    full = n // 2

    def turn(i):
        return i, batch(i + 1, n, extra), batch(i, n, extra), batch(i - 1, n, extra)

    yield 0, batch(1, n, extra), batch(0, n, extra), []
    if full > 2:
        with eng.Fori(1, full - 1) as i:
            yield turn(i)
    for i in range(max(full - 1, 1), full + 2):
        yield turn(i)


def overlapped_transfers(eng, n, load, store, freed_by_store, extra=0):
    full = n // 2

    def turn(i, ahead, ending, stored):
        if stored:
            freed_by_store(i - 2, stored)
        load(ahead)
        if ending:
            store(ending)

    load(batch(0, n, extra))
    turn(0, batch(1, n, extra), [], [])
    turn(1, batch(2, n, extra), batch(0, n, extra), [])
    if full - 1 > 2:
        with eng.Fori(2, full - 1) as i:
            turn(i, batch(i + 1, n, extra), batch(i - 1, n, extra), batch(i - 2, n, extra))
    for i in range(full - 1, full + 3):
        turn(i, batch(i + 1, n, extra), batch(i - 1, n, extra), batch(i - 2, n, extra))


def tiles_of(g, n):
    return 1 if isinstance(g, int) and g == n else TILES



class LoopOrder:

    def __init__(self, eng, sem, per, i, before=0):
        self.eng, self.sem, self.per, self.i, self.before, self.n = eng, sem, per, i, before, 0

    def __call__(self, instruction):
        instruction.then_inc(self.sem, 1)
        self.n += 1
        self.eng.wait_ge(self.sem, self.i * self.per + self.before + self.n)

    def end(self):
        assert self.n == self.per, (self.n, self.per)


def done(g):
    return g + 3


def freed(g):
    return g + 1


def broadcast(ap, n):
    return bass.AP(tensor=ap.tensor, offset=ap.offset, ap=list(ap.ap) + [[0, n]])


def spread(ap, axis, n):
    wide = ap.unsqueeze(axis)
    shape = list(wide.shape)
    shape[axis] = n
    return wide.broadcast_to(shape)


def named(items):
    return namedtuple("Named", items.keys())(*items.values())


class Buffers:

    def __init__(self, nc, ctx, tag):
        self.nc, self.ctx, self.tag, self.taken = nc, ctx, tag, []
        ctx.callback(self.give_back)

    def sb(self, name, shape, dt=F32):
        return self.ctx.enter_context(self.nc.sbuf_tensor(f"{self.tag}_{name}", shape, dt))

    def ps(self, name, shape):
        return self.ctx.enter_context(self.nc.psum_tensor(f"{self.tag}_{name}", shape, F32))

    def sem(self, name):
        self.taken.append(self.nc.alloc_semaphore(f"{self.tag}_{name}"))
        return self.taken[-1]

    def sems(self, names):
        return named({name: self.sem(name) for name in names})

    def give_back(self):
        if self.taken:
            self.nc.clear_and_free_semaphores(self.taken)
            self.nc.all_engine_barrier()


class Kept:

    def __init__(self, rows, cols):
        self.rows, self.cols, self.slots = rows, cols, P * cols + P



def prepare_weights(nc, K, I):
    with ExitStack() as ctx:
        A = Buffers(nc, ctx, "weights")
        L, H = GAT_LAYERS, GAT_HEADS
        n_att = L * H * 2
        n_rows = n_att + L * H + L + 2
        eb_at, b_at, bk_at, bv_at = n_att, n_att + L * H, n_att + L * H + L, n_att + L * H + L + 1
        w_raw = A.sb("w_raw", [P, L, H, D])
        rows = A.sb("rows", [n_rows, P])
        ew_raw = A.sb("ew_raw", [P, L, H, EDGE_F])
        hgt_raw = A.sb("hgt_raw", [P, 2, D])
        wa_raw = A.sb("wa_raw", [P, D])
        rel_raw = A.sb("rel_raw", [P, HGT_RELS, 2, D])
        p_col = A.sb("p_col", [P, HGT_RELS])
        p_scaled = A.sb("p_scaled", [P, HGT_RELS])
        skip_rep = A.sb("skip_rep", [P, 1])
        att_blk = A.sb("att_blk", [P, 2, CAT_S])
        conf = A.sb("conf", [P, CAT_CONF])
        conf_max = A.sb("conf_max", [P, 1])
        conf_sum = A.sb("conf_sum", [P, 1])
        wT = A.sb("wT", [P, L * H + 2 + CAT_TYPES, D])
        cols = A.sb("cols", [P, n_rows])
        rep = A.sb("rep", [P, L * H + L + 2, D])
        n_t = L * H + 2 + CAT_TYPES
        ps = [A.ps(f"ps_w{b}", [P, 512]) for b in range(8)]
        loaded, made, turned, copied, mixed = (A.sem(s) for s in ("loaded", "made", "turned", "copied", "mixed"))
        scores_act, conf_ready, dve_step = A.sem("scores_act"), A.sem("conf_ready"), A.sem("dve_step")
        n_loads = (4 + L + 2 + 4 + 3 * HGT_RELS * HGT_HEADS + 1 + 2 * CAT_HEADS * CAT_CONF + 2 + CAT_TYPES + 5 + 1)

        with nc.Block() as block:
            @block.gpsimd
            def _(eng):
                eng.memset(rel_raw[:, :, :, :], 0.0).then_inc(made, 1)
                eng.memset(att_blk[:, :, :], 0.0).then_inc(made, 1)
                eng.memset(K.ones[:, :], 1.0).then_inc(made, 1)
                eng.memset(K.minus_half[:, :], -0.5)
                eng.wait_ge(made, 3)
                for out, base, step, mult, cmp in ((K.ident, 0, -1, 1, ALU.is_equal), (K.from_prev, 1, -1, 1, ALU.is_equal),
                                                   (K.from_next, -1, -1, 1, ALU.is_equal), (K.upper, -1, 1, -1, ALU.is_ge)):
                    eng.affine_select(out[:, :], K.ones[:, :], pattern=[[step, P]], compare_op=cmp, fill=0.0,
                                      base=base, channel_multiplier=mult).then_inc(made, 1)

            @block.sync
            def _(eng):
                def load(out, in_):
                    eng.dma_start(out, in_).then_inc(loaded, 16)
                with nc.allow_non_contiguous_dma(reason="small weights"):
                    load(w_raw[:, :, :, :].rearrange("i l h o -> i l (h o)"), I.gat_w.rearrange("l i o -> i l o"))
                    load(rows[0:n_att, :], I.gat_att.rearrange("l h (j d) -> (l h j) d", j=2))
                    load(rows[eb_at:eb_at + L * H, :], I.gat_eb.rearrange("l (h o) -> (l h) o", h=H))
                    load(rows[b_at:b_at + L, :], I.gat_b)
                    for l in range(L):
                        load(ew_raw[:, l, :, :], I.gat_ew[l, :, :].rearrange("(h o) f -> o h f", h=H))
                    load(rows[bk_at:bk_at + 1, :], I.hgt_bk.unsqueeze(0))
                    load(rows[bv_at:bv_at + 1, :], I.hgt_bv.unsqueeze(0))
                    load(hgt_raw[:, 0, :], I.hgt_wk)
                    load(hgt_raw[:, 1, :], I.hgt_wv)
                    load(K.hgt_wq[:, :], I.hgt_wq)
                    load(wa_raw[:, :], I.hgt_wa)
                    eng.wait_ge(made, 2)
                    d = D // HGT_HEADS
                    for r in range(HGT_RELS):
                        for h in range(HGT_HEADS):
                            at = slice(h * d, (h + 1) * d)
                            load(rel_raw[at, r, 0, at], I.hgt_a[r, h, :, :])
                            load(rel_raw[at, r, 1, at], I.hgt_m[r, h, :, :])
                            load(p_col[at, r:r + 1], I.hgt_p[r:r + 1, h:h + 1].broadcast_to([d, 1]))
                    load(skip_rep[:, :], I.hgt_skip.broadcast_to([P, 1]))
                    c = D // CAT_HEADS
                    for h in range(CAT_HEADS):
                        for k in range(CAT_CONF):
                            for j in range(2):
                                s = k * CAT_HEADS + h
                                load(att_blk[h * c:(h + 1) * c, j, s:s + 1],
                                     I.cat_att[k, h, j * c:(j + 1) * c].unsqueeze(1))
                    load(conf[:, :], I.cat_conf.unsqueeze(0).broadcast_to([P, CAT_CONF]))
                    load(K.cat_imp[:, :], I.cat_imp.unsqueeze(0).broadcast_to([P, CAT_TYPES]))
                    for t in range(CAT_TYPES):
                        load(K.cat_wu[:, t, 0:D], I.cat_w[t, :, :])
                    load(K.gcn_w[:, :], I.gcn_w)
                    load(K.by_feature[:, 0:1], I.gcn_b.unsqueeze(1))
                    load(K.by_feature[:, 1:2], I.cat_b.unsqueeze(1))
                    load(K.by_feature[:, 2:3], I.hgt_bq.unsqueeze(1))
                    load(K.by_feature[:, 3:4], I.hgt_ba.unsqueeze(1))
                    load(K.hgt_ba[:, :], I.hgt_ba.unsqueeze(0).broadcast_to([P, D]))

            @block.tensor
            def _(eng):
                eng.wait_ge(made, 4)
                eng.wait_ge(loaded, 16 * n_loads)
                src = [w_raw[:, l, h, :] for l in range(L) for h in range(H)] + [hgt_raw[:, 0, :], hgt_raw[:, 1, :]]
                src += [K.cat_wu[:, t, 0:D] for t in range(CAT_TYPES)]
                for n, m in enumerate(src):
                    eng.transpose(ps[n // 4][:, n % 4 * D:n % 4 * D + D], m, K.ident[:, :])
                eng.transpose(ps[4][:, 0:n_rows], rows[:, :], K.ident[0:n_rows, 0:n_rows])
                for l in range(L):
                    b, o = 5 + l // 4, l % 4 * D
                    mm = eng.transpose(ps[b][0:H * EDGE_F, o:o + D], ew_raw[:, l, :, :].rearrange("o h f -> o (h f)"),
                                       K.ident[:, :])
                mm.then_inc(turned, 1)
                eng.wait_ge(copied, 1)
                for l in range(L):
                    for h in range(H):
                        for j in range(2):
                            col = (l * H + h) * 2 + (1 - j)
                            at = l * 4 + j * 2 + h
                            eng.matmul(ps[7][:, at:at + 1], wT[:, l * H + h, :], cols[:, col:col + 1],
                                       start=True, stop=True)
                        at = 32 + (l * H + h) * 20
                        eng.matmul(ps[7][:, at:at + EDGE_F], rep[:, l * H + h, :], ew_raw[:, l, h, :], start=True, stop=True)
                        eng.matmul(ps[7][:, at + EDGE_F:at + EDGE_F + 1], rep[:, l * H + h, :],
                                   cols[:, eb_at + l * H + h:eb_at + l * H + h + 1], start=True, stop=True)
                    eng.matmul(ps[l // 4][:, l % 4 * D:l % 4 * D + D], rep[:, L * H + l, :], K.ident[:, :],
                               start=True, stop=True)
                for r in range(HGT_RELS):
                    for j in range(2):
                        o = (r * 2 + j) * D
                        eng.matmul(ps[2][:, o:o + D], wT[:, L * H + j, :], rel_raw[:, r, j, :], start=True, stop=True)
                        eng.matmul(ps[3][:, o:o + D], rep[:, L * H + L + j, :], rel_raw[:, r, j, :], start=True, stop=True)
                for t in range(CAT_TYPES):
                    for j in range(2):
                        o = (t * 2 + j) * CAT_S
                        mm = eng.matmul(ps[4][:, o:o + CAT_S], wT[:, L * H + 2 + t, :], att_blk[:, j, :],
                                        start=True, stop=True)
                mm.then_inc(mixed, 1)

            @block.scalar
            def _(eng):
                eng.wait_ge(loaded, 16 * n_loads)
                eng.activation(K.hgt_gate[:, 1:2], skip_rep[:, :], ACT.Exp, scale=-1.0).then_inc(scores_act, 1)
                eng.wait_ge(conf_ready, 1)
                eng.activation(K.cat_pk[:, :], conf[:, :], ACT.Exp).then_inc(scores_act, 1)

            @block.vector
            def _(eng):
                step = Order(eng, dve_step)
                eng.wait_ge(loaded, 16 * n_loads)
                eng.wait_ge(made, 7)
                step(eng.tensor_reduce(conf_max[:, :], conf[:, :], AX.X, ALU.max))
                eng.tensor_scalar(conf[:, :], conf[:, :], conf_max[:, 0:1], None, ALU.subtract).then_inc(conf_ready, 1)
                step(eng.tensor_scalar(p_scaled[:, :], p_col[:, :], float(D // HGT_HEADS) ** -0.5, None, ALU.mult))
                for r in range(HGT_RELS):
                    step(eng.tensor_scalar(rel_raw[:, r, 0, :], rel_raw[:, r, 0, :], p_scaled[:, r:r + 1], None, ALU.mult))
                step(eng.tensor_scalar(K.gat_wh[:, :, :, :], w_raw[:, :, :, :], 1.0 / H, None, ALU.mult))
                step(eng.tensor_tensor(K.gat_wm[:, :, :], K.gat_wh[:, :, 0, :], K.gat_wh[:, :, 1, :], ALU.add))
                eng.wait_ge(turned, 1)
                for b in range(n_t // 4):
                    step(eng.tensor_copy(wT[:, 4 * b:4 * b + 4, :].rearrange("p a d -> p (a d)"), ps[b][:, :]))
                step(eng.tensor_copy(cols[:, :], ps[4][:, 0:n_rows]))
                for l in range(L):
                    b, o = 5 + l // 4, l % 4 * D
                    step(eng.tensor_scalar(K.gat_ewT[:, l, :], ps[b][0:H * EDGE_F, o:o + D], 1.0 / H, None, ALU.mult))
                    e0 = eb_at + l * H
                    step(eng.tensor_tensor(K.gat_bias[:, l:l + 1], cols[:, e0:e0 + 1], cols[:, e0 + 1:e0 + 2], ALU.add))
                    step(eng.scalar_tensor_tensor(K.gat_bias[:, l:l + 1], K.gat_bias[:, l:l + 1], 1.0 / H,
                                                  cols[:, b_at + l:b_at + l + 1], ALU.mult, ALU.add))
                    for h in range(H):
                        col = (l * H + h) * 2 + 1
                        step(eng.tensor_scalar(rep[:, l * H + h, :], K.ones[:, :], cols[:, col:col + 1], None, ALU.mult))
                    step(eng.tensor_scalar(rep[:, L * H + l, :], K.ones[:, :], K.gat_bias[:, l:l + 1], None, ALU.mult))
                step(eng.tensor_scalar(rep[:, L * H + L, :], K.ones[:, :], cols[:, bk_at:bk_at + 1], None, ALU.mult))
                eng.tensor_scalar(rep[:, L * H + L + 1, :], K.ones[:, :], cols[:, bv_at:bv_at + 1], None,
                                  ALU.mult).then_inc(copied, 1)
                eng.wait_ge(scores_act, 2)
                step(eng.tensor_scalar(K.hgt_gate[:, 1:2], K.hgt_gate[:, 1:2], 1.0, None, ALU.add))
                step(eng.reciprocal(K.hgt_gate[:, 0:1], K.hgt_gate[:, 1:2]))
                step(eng.tensor_scalar(K.hgt_gate[:, 1:2], K.hgt_gate[:, 0:1], -1.0, 1.0, ALU.mult, ALU.add))
                step(eng.tensor_scalar(K.hgt_wa[:, :], wa_raw[:, :], K.hgt_gate[:, 0:1], None, ALU.mult))
                step(eng.tensor_scalar(K.by_feature[:, 3:4], K.by_feature[:, 3:4], K.hgt_gate[:, 0:1], None, ALU.mult))
                step(eng.tensor_scalar(K.hgt_ba[:, :], K.hgt_ba[:, :], K.hgt_gate[:, 0:1], None, ALU.mult))
                step(eng.tensor_reduce(conf_sum[:, :], K.cat_pk[:, :], AX.X, ALU.add))
                step(eng.reciprocal(conf_sum[:, :], conf_sum[:, :]))
                step(eng.tensor_scalar(K.cat_pk[:, :], K.cat_pk[:, :], conf_sum[:, 0:1], None, ALU.mult))
                eng.wait_ge(mixed, 1)
                step(eng.tensor_copy(K.gat_v[:, :, :].rearrange("p l s -> p (l s)"), ps[7][:, 0:4 * L]))
                step(eng.tensor_copy(K.gat_u[:, :, :],
                                     ps[7][:, 32:32 + 20 * L * H].rearrange("p (a f) -> p a f", f=20)[:, :, 0:EDGE_F + 1]))
                for l in range(L):
                    step(eng.tensor_copy(K.gat_bias_rep[:, l, :], ps[l // 4][:, l % 4 * D:l % 4 * D + D]))
                step(eng.tensor_copy(K.hgt_kv[:, :, :].rearrange("p r o -> p (r o)"), ps[2][:, :]))
                step(eng.tensor_copy(K.hgt_kvb[:, :, :].rearrange("p r o -> p (r o)"), ps[3][:, :]))
                u = ps[4][:, 0:2 * CAT_TYPES * CAT_S].rearrange("p (t j s) -> p t j s", t=CAT_TYPES, j=2)
                step(eng.tensor_copy(K.cat_ui[:, :, :], u[:, :, 0, :]))
                step(eng.tensor_copy(K.cat_wu[:, :, D:D + CAT_S], u[:, :, 1, :]))



def describe_slots(nc, K, I):
    C = K.cols
    with ExitStack() as ctx:
        A = Buffers(nc, ctx, "slots")
        raw = A.sb("dst_raw", [P, C], I32)
        src_raw = A.sb("src_raw", [P, C], I32)
        typ2, typ4 = A.sb("typ2", [P, C], I32), A.sb("typ4", [P, C], I32)
        number = A.sb("number", [P, C + 1], I32)
        node_rows = A.sb("node_rows", [P, K.rows // P], I32)
        d1 = A.sb("d1", [P, C])
        diag = A.sb("diag", [P, 2, P])
        around = A.sb("around", [P, 4])
        a_end, head, t0 = A.sb("a_end", [P, C]), A.sb("head", [P, C]), A.sb("t0", [P, C + 1])
        seq = A.sb("seq", [16, P, 2])
        typ4f = A.sb("typ4f", [P, C])
        small = A.sb("small", [P, 8])
        ps = [A.ps(f"ps_s{b}", [P, 512]) for b in range(2)]
        loaded, iotas, diags, turned, step_sem, rows_out = (
            A.sem(s) for s in ("loaded", "iotas", "diags", "turned", "step", "rows_out"))

        with nc.Block() as block:
            @block.sync
            def _(eng):
                eng.dma_start(raw[:, :], I.dst).then_inc(loaded, 16)
                eng.dma_start(src_raw[:, :], I.src).then_inc(loaded, 16)
                eng.dma_start(typ2[:, :], I.type2).then_inc(loaded, 16)
                eng.dma_start(typ4[:, :], I.type4).then_inc(loaded, 16)
                eng.wait_ge(iotas, 3)
                eng.dma_start(K.row_of.rearrange("(p n) one -> p (n one)", p=P), node_rows[:, :]).then_inc(rows_out, 16)
                eng.wait_ge(rows_out, 16)

            @block.gpsimd
            def _(eng):
                eng.iota(number[:, 0:C], [[1, C]], base=0, channel_multiplier=C).then_inc(iotas, 1)
                eng.iota(number[:, C:C + 1], [[0, 1]], base=P * C, channel_multiplier=1).then_inc(iotas, 1)
                eng.iota(node_rows[:, :], [[1, K.rows // P]], base=0, channel_multiplier=K.rows // P).then_inc(iotas, 1)

            @block.tensor
            def _(eng):
                eng.wait_ge(diags, 1)
                eng.matmul(ps[0][:, 0:1], K.from_prev[:, :], d1[:, C - 1:C], start=True, stop=True)
                eng.matmul(ps[0][:, 1:2], K.from_next[:, :], d1[:, 0:1], start=True, stop=True)
                eng.matmul(ps[1][:, 0:P], K.ones[:, :], diag[:, 0, :], start=True, stop=True)
                eng.matmul(ps[1][:, P:2 * P], K.ones[:, :], diag[:, 1, :], start=True, stop=True).then_inc(turned, 1)

            @block.vector
            def _(eng):
                step = Order(eng, step_sem)
                eng.wait_ge(loaded, 16 * 4)
                eng.wait_ge(iotas, 3)
                step(eng.tensor_copy(d1[:, :], raw[:, :]))
                step(eng.tensor_scalar(d1[:, :], d1[:, :], 1.0, None, ALU.add))
                first, last = d1[:, 0:1], d1[:, C - 1:C]
                step(eng.tensor_scalar(diag[:, 0, :], K.ident[:, :], first, None, ALU.mult))
                eng.tensor_scalar(diag[:, 1, :], K.ident[:, :], last, None, ALU.mult).then_inc(diags, 1)
                step(eng.tensor_copy(K.slot_no[:, :], number[:, :]))
                step(eng.tensor_copy(K.gather_dst[:, 0:C], raw[:, :]))
                step(eng.tensor_copy(K.gather_dst[:, C:C + 1], raw[:, 0:1]))
                step(eng.tensor_copy(K.src_node[:, :], src_raw[:, :]))
                step(eng.memset(K.cont[:, 0:1], 0.0))
                step(eng.tensor_tensor(K.cont[:, 1:C], d1[:, 1:C], d1[:, 0:C - 1], ALU.is_equal))
                step(eng.memset(K.goes_on[:, C - 1:C], 0.0))
                step(eng.tensor_copy(K.goes_on[:, 0:C - 1], K.cont[:, 1:C]))
                step(eng.tensor_scalar(K.ends[:, :], K.goes_on[:, :], -1.0, 1.0, ALU.mult, ALU.add))
                step(eng.tensor_scalar(K.restart[:, :], K.cont[:, :], 1.0, -FAR, ALU.subtract, ALU.mult))
                eng.wait_ge(turned, 1)
                step(eng.tensor_tensor(around[:, 0:1], first, ps[0][:, 0:1], ALU.is_equal))
                step(eng.tensor_tensor(around[:, 1:2], last, ps[0][:, 1:2], ALU.is_equal))
                step(eng.tensor_tensor(around[:, 2:3], first, last, ALU.is_equal))
                step(eng.tensor_scalar(K.many[:, :], around[:, 2:3], -1.0, 1.0, ALU.mult, ALU.add))
                step(eng.tensor_scalar(K.carry[:, :], ps[1][:, 0:P], last, None, ALU.is_equal))
                step(eng.tensor_tensor(K.carry[:, :], K.carry[:, :], K.upper[:, :], ALU.mult))
                step(eng.tensor_scalar(head[:, :], d1[:, :], first, None, ALU.is_equal))
                step(eng.tensor_copy(K.in_head[:, :], head[:, :]))
                step(eng.tensor_scalar(K.in_tail[:, :], d1[:, :], last, None, ALU.is_equal))
                step(eng.tensor_tensor(t0[:, 0:C], K.in_tail[:, :], head[:, :], ALU.mult))
                step(eng.tensor_tensor(K.in_tail[:, :], K.in_tail[:, :], t0[:, 0:C], ALU.subtract))
                step(eng.tensor_tensor(t0[:, 0:C], K.in_tail[:, :], head[:, :], ALU.add))
                step(eng.tensor_scalar(K.inner[:, :], t0[:, 0:C], -1.0, 1.0, ALU.mult, ALU.add))
                step(eng.tensor_copy(a_end[:, :], K.ends[:, :]))
                step(eng.tensor_scalar(a_end[:, C - 1:C], around[:, 1:2], -1.0, 1.0, ALU.mult, ALU.add))
                step(eng.tensor_scalar(t0[:, 0:C], head[:, :], around[:, 0:1], None, ALU.mult))
                step(eng.tensor_tensor(t0[:, 0:C], t0[:, 0:C], a_end[:, :], ALU.mult))
                step(eng.tensor_tensor(K.own[:, 0:C], a_end[:, :], t0[:, 0:C], ALU.subtract))
                step(eng.tensor_reduce(K.own[:, C:C + 1], t0[:, 0:C], AX.X, ALU.add))
                step(eng.tensor_scalar(head[:, :], K.slot_no[:, 0:C], K.slot_no[:, 0:1], None, ALU.subtract))
                step(eng.tensor_tensor(head[:, :], head[:, :], t0[:, 0:C], ALU.mult))
                step(eng.tensor_reduce(small[:, 0:1], head[:, :], AX.X, ALU.add))
                step(eng.tensor_tensor(small[:, 0:1], small[:, 0:1], K.slot_no[:, 0:1], ALU.add))
                step(eng.tensor_copy(K.part_slot[:, :], small[:, 0:1]))
                step(eng.tensor_scalar(small[:, 1:2], small[:, 0:1], float(K.rows), None, ALU.add))
                step(eng.tensor_copy(K.part_row[:, :], small[:, 1:2]))
                step(eng.tensor_scalar(t0[:, 0:C], d1[:, :], -1.0 - NOWHERE, None, ALU.add))
                step(eng.tensor_copy(t0[:, C:C + 1], t0[:, 0:1]))
                step(eng.tensor_tensor(t0[:, :], t0[:, :], K.own[:, :], ALU.mult))
                step(eng.tensor_scalar(t0[:, :], t0[:, :], float(NOWHERE), None, ALU.add))
                step(eng.tensor_copy(K.node_of[:, :], t0[:, :]))
                step(eng.tensor_scalar(t0[:, :], K.slot_no[:, :], float(K.rows), None, ALU.add))
                step(eng.tensor_copy(K.slot_row[:, :], t0[:, :]))
                step(eng.tensor_copy(seq[:, :, 0], ps[1][0:16, 0:P]))
                step(eng.tensor_copy(seq[:, :, 1], ps[1][0:16, P:2 * P]))
                flat = seq[:, :, :].rearrange("c p e -> c (p e)")
                step(eng.memset(K.seq_cont[:, 0:1], 0.0))
                step(eng.tensor_tensor(K.seq_cont[:, 1:2 * P], flat[:, 1:2 * P], flat[:, 0:2 * P - 1], ALU.is_equal))
                step(eng.memset(K.seq_goes_on[:, 2 * P - 1:2 * P], 0.0))
                step(eng.tensor_copy(K.seq_goes_on[:, 0:2 * P - 1], K.seq_cont[:, 1:2 * P]))
                step(eng.tensor_scalar(K.seq_ends[:, :], K.seq_goes_on[:, :], -1.0, 1.0, ALU.mult, ALU.add))
                step(eng.tensor_scalar(K.seq_restart[:, :], K.seq_cont[:, :], 1.0, -FAR, ALU.subtract, ALU.mult))
                step(eng.tensor_copy(K.rel_mask[:, 0, :], typ2[:, :]))
                step(eng.tensor_copy(typ4f[:, :], typ4[:, :]))
                step(eng.tensor_scalar(K.rel_mask[:, 1, :], K.rel_mask[:, 0, :], 0.0, None, ALU.is_equal))
                step(eng.tensor_scalar(K.rel_mask[:, 0, :], K.rel_mask[:, 0, :], 1.0, None, ALU.is_equal))
                for t in range(CAT_TYPES):
                    step(eng.tensor_scalar(K.type_mask[:, t, :], typ4f[:, :], float(t), None, ALU.is_equal))


class RunTotals:

    def __init__(self, K, A, channels):
        self.K, self.n = K, channels
        self.edge = A.sb("rt_edge", [P, 2, channels])
        self.seq = A.sb("rt_seq", [channels, P, 2])
        self.back = A.sb("rt_back", [P, 2, channels])
        self.ps_seq, self.ps_back = A.ps("rt_ps_seq", [channels, 2 * P]), A.ps("rt_ps_back", [P, 2 * channels])
        self.edges_ready, self.seq_turned = A.sem("edges_ready"), A.sem("seq_turned")
        self.vector_calls = self.tensor_calls = 0

    def on_vector(self, eng, step, val, op, n, extra=None):
        K, C, k = self.K, self.K.cols, self.vector_calls
        self.vector_calls += 1
        keep, how = (K.cont, ALU.mult) if op is ALU.add else (K.restart, ALU.add)
        for c in range(n):
            v = val[:, c, :]
            step(eng.tensor_tensor_scan(v, keep[:, :], v, 0.0, how, op))
        step(eng.tensor_tensor(val[:, 0:n, :], val[:, 0:n, :], spread(K.ends[:, :], 1, n), ALU.mult))
        for c in range(n):
            v = val[:, c, ::-1]
            step(eng.tensor_tensor_scan(v, K.goes_on[:, ::-1], v, 0.0, ALU.mult, ALU.add))
        head, tail = self.edge[:, 0, 0:n], self.edge[:, 1, 0:n]
        if op is ALU.add:
            step(eng.tensor_scalar(head, val[:, 0:n, 0], K.many[:, 0:1], None, ALU.mult))
        else:
            step(eng.tensor_copy(head, val[:, 0:n, 0]))
        if extra is not None:
            step(eng.tensor_tensor(head, head, extra, ALU.add))
        step(eng.tensor_copy(tail, val[:, 0:n, C - 1]))
        eng.sem_inc(self.edges_ready, 1)
        eng.wait_ge(self.seq_turned, 2 * k + 1)
        seq = self.seq[0:n, :, :].rearrange("c p e -> c (p e)")
        step(eng.tensor_copy(self.seq[0:n, :, 0], self.ps_seq[0:n, 0:P]))
        step(eng.tensor_copy(self.seq[0:n, :, 1], self.ps_seq[0:n, P:2 * P]))
        keep = K.seq_cont if op is ALU.add else K.seq_restart
        step(eng.tensor_tensor_scan(seq, keep[0:n, :], seq, 0.0, how, op))
        step(eng.tensor_tensor(seq, seq, K.seq_ends[0:n, :], ALU.mult))
        step(eng.tensor_tensor_scan(seq[:, ::-1], K.seq_goes_on[0:n, ::-1], seq[:, ::-1], 0.0, ALU.mult, ALU.add))
        eng.sem_inc(self.edges_ready, 1)
        eng.wait_ge(self.seq_turned, 2 * k + 2)
        back = self.back[:, :, 0:n]
        step(eng.tensor_copy(back, self.ps_back[:, 0:2 * n].rearrange("p (e c) -> p e c", e=2)))
        step(eng.tensor_tensor(val[:, 0:n, :], val[:, 0:n, :], spread(K.inner[:, :], 1, n), ALU.mult))
        for c in range(n):
            for e, mask in enumerate((K.in_head, K.in_tail)):
                step(eng.scalar_tensor_tensor(val[:, c, :], mask[:, :], self.back[:, e, c:c + 1], val[:, c, :],
                                              ALU.mult, ALU.add))

    def on_tensor(self, eng, n):
        K, k = self.K, self.tensor_calls
        self.tensor_calls += 1
        eng.wait_ge(self.edges_ready, 2 * k + 1)
        for e in range(2):
            mm = eng.transpose(self.ps_seq[0:n, e * P:(e + 1) * P], self.edge[:, e, 0:n], K.ident[:, :])
        mm.then_inc(self.seq_turned, 1)
        eng.wait_ge(self.edges_ready, 2 * k + 2)
        for e in range(2):
            mm = eng.transpose(self.ps_back[:, e * n:(e + 1) * n], self.seq[0:n, :, e], K.ident[0:n, 0:n])
        mm.then_inc(self.seq_turned, 1)


def map_rows(nc, K):
    C = K.cols
    with ExitStack() as ctx:
        A = Buffers(nc, ctx, "map")
        R = RunTotals(K, A, 2)
        val = A.sb("val", [P, 2, C])
        extra = A.sb("extra", [P, 2])
        deg = A.sb("deg", [P, C + 1])
        power = A.sb("power", [P, C + 1])
        at = A.sb("at", [P, 2, TILES], I32)
        what = A.sb("what", [P, 2, TILES], I32)
        got = A.sb("got", [P, 2, TILES], I32)
        s = A.sems((
            "step", "deg_ready", "dinv_ready", "copied", "wrote0", "wrote1", "got0", "got1", "taken", "gate"))
        n = C // TILES
        with nc.Block() as block:
            @block.gpsimd
            def _(eng):
                for i, both in batches(eng, n, 1):
                    for g, u in both:
                        m = tiles_of(g, n)
                        eng.tensor_copy(at[:, u, 0:m], K.node_of[:, slot_cols(g, n)])
                        eng.tensor_copy(what[:, u, 0:m], K.slot_row[:, slot_cols(g, n)]).then_inc(s.copied, 1)
                        eng.wait_ge(s.copied, g + 1)
                        eng.sem_inc(s.gate, 1)
                        for t in range(m):
                            eng.indirect_dma_start(K.row_of, bass.IndirectOffsetOnAxis(ap=at[:, u, t:t + 1], axis=0),
                                                   what[:, u, t:t + 1], None, bounds_check=K.rows - 1,
                                                   oob_is_err=False).then_inc((s.wrote0, s.wrote1)[u], 16)
                    for g, u in both:
                        eng.wait_ge((s.wrote0, s.wrote1)[u], i * 16 * TILES + 16 * tiles_of(g, n))
                        eng.sem_inc(s.gate, 1)
                eng.sem_inc(s.taken, 2)
                for i, both in batches(eng, n):
                    for g, u in both:
                        eng.wait_ge(s.taken, freed(g))
                        eng.sem_inc(s.gate, 1)
                        eng.tensor_copy(at[:, u, :], K.src_node[:, bass.ts(g, TILES)]).then_inc(s.copied, 1)
                        eng.wait_ge(s.copied, n + 2 + g)
                        eng.sem_inc(s.gate, 1)
                        for t in range(TILES):
                            eng.indirect_dma_start(got[:, u, t:t + 1], None, K.row_of,
                                                   bass.IndirectOffsetOnAxis(ap=at[:, u, t:t + 1], axis=0)
                                                   ).then_inc((s.got0, s.got1)[u], 16)
                eng.wait_ge(s.deg_ready, 1)
                eng.tensor_tensor(K.dinv[:, :], deg[:, :], power[:, :], ALU.pow).then_inc(s.dinv_ready, 1)

            @block.tensor
            def _(eng):
                R.on_tensor(eng, 1)
                R.on_tensor(eng, 1)

            @block.vector
            def _(eng):
                step = Order(eng, s.step)
                step(eng.tensor_tensor(val[:, 0, :], K.slot_no[:, 0:C], K.own[:, 0:C], ALU.mult))
                step(eng.tensor_tensor(extra[:, 0:1], K.slot_no[:, C:C + 1], K.own[:, C:C + 1], ALU.mult))
                R.on_vector(eng, step, val, ALU.add, 1, extra[:, 0:1])
                step(eng.tensor_copy(K.dst_slot[:, :], val[:, 0, :]))
                step(eng.memset(val[:, 1, :], 1.0))
                R.on_vector(eng, step, val[:, 1:2, :], ALU.add, 1)
                step(eng.tensor_scalar(deg[:, 0:C], val[:, 1, :], 1.0, None, ALU.add))
                step(eng.memset(power[:, :], -0.5))
                eng.tensor_copy(deg[:, C:C + 1], deg[:, 0:1]).then_inc(s.deg_ready, 1)
                for i, both in batches(eng, n):
                    for g, u in both:
                        eng.wait_ge((s.got0, s.got1)[u], (i + 1) * 16 * TILES)
                        eng.tensor_scalar(K.src_row[:, bass.ts(g, TILES)], got[:, u, :], 0.0, None,
                                          ALU.add).then_inc(s.taken, 1)
                eng.wait_ge(s.dinv_ready, 1)



def stats_of(eng, step, gate, x, st, mv, n):
    for t in range(n):
        ins = eng.bn_stats(st[:, t, :], x[:, t, :])
    step(ins)
    eng.sem_inc(gate, 1)
    for t in range(n):
        ins = eng.bn_aggr(mv[:, t, :], st[:, t, :])
    step(ins)
    return eng.tensor_scalar(mv[:, 0:n, 1], mv[:, 0:n, 1], LN_EPS, None, ALU.add)


def node_pass(nc, K, I, out):
    B, T = BLOCKS, BLOCK // P
    turns = K.rows // (B * BLOCK)
    L = GAT_LAYERS
    LN = 4
    with ExitStack() as ctx:
        A = Buffers(nc, ctx, "nodes")
        x_in = A.sb("x_in", [P, B, T, D])
        xs = A.sb("xs", [P, B, T, D])
        rows = A.sb("rows", [P, B, 2, T, ROWW])
        h_rows = A.sb("h_rows", [P, B, 3, T, D])
        x_out = A.sb("x_out", [P, B, T, D])
        hT = A.sb("hT", [P, B, 2, BLOCK])
        st = A.sb("st", [P, B, T, 6])
        mv = A.sb("mv", [P, B, LN, T, 2])
        rstd, shift = A.sb("rstd", [P, B, LN, T]), A.sb("shift", [P, B, LN, T])
        zT = A.sb("zT", [P, B, BLOCK])
        psT = psZ = [A.ps(f"psZ{u}", [P, BLOCK]) for u in range(B)]
        banks = [A.ps(f"psR{u}", [P, BLOCK + 4 * T]) for u in range(B)]
        psR, psS = [b[:, 0:BLOCK] for b in banks], [b[:, BLOCK:BLOCK + 4 * T] for b in banks]
        s = A.sems((
            "x_loaded", "stats", "powered", "rstd_ready", "normed", "rows_done", "x1_done", "finished", "turned", "mixed",
            "rows_ready", "last_turned", "wide", "copiedT", "hT_ready", "zT_ready", "turned_back", "step", "rows_free", "out_free",
            "stored", "stored_h", "x2_done", "x3_done", "gate"))

        def node_view(table, i, u, w):
            at = (i * B + u) * BLOCK
            return table[bass.ds(at, BLOCK), 0:w].rearrange("(p t) w -> p t w", t=T)

        with nc.Block() as block:
            @block.sync
            def _(eng):
                def load(i):
                    for u in range(B):
                        eng.dma_start(x_in[:, u, :, :], node_view(I.x, i, u, D)).then_inc(s.x_loaded, 16)

                def stores(i, more):
                    for l in range(L):
                        for u in range(B):
                            eng.wait_ge(s.rows_done, (i * L + l) * B + u + 1)
                            eng.dma_start(node_view(K.tables[l], i, u, ROWW), rows[:, u, l % 2, :, :]).then_inc(s.stored, 16)
                        eng.wait_ge(s.stored, (i * L + l + 1) * 16 * B)
                        eng.sem_inc(s.rows_free, 1)
                    if more:
                        eng.wait_ge(s.x1_done, B * i + B)
                        load(i + 1)
                    for n in range(3):
                        for u in range(B):
                            eng.wait_ge(s.normed, (i * LN + n + 1) * B + u + 1)
                            eng.dma_start(node_view(K.tables[L + n], i, u, D), h_rows[:, u, n, :, :]).then_inc(s.stored_h, 16)
                    for u in range(B):
                        eng.wait_ge(s.finished, B * i + u + 1)
                        eng.dma_start(node_view(out, i, u, D), x_out[:, u, :, :]).then_inc(s.stored_h, 16)
                    eng.wait_ge(s.stored_h, (i + 1) * 4 * 16 * B)
                    eng.sem_inc(s.out_free, 1)

                eng.sem_inc(s.rows_free, 2)
                eng.sem_inc(s.out_free, 1)
                load(0)
                if turns > 1:
                    with eng.Fori(0, turns - 1) as i:
                        stores(i, True)
                stores(turns - 1, False)

            @block.gpsimd
            def _(eng):
                with eng.Fori(0, turns) as i:
                    for n in range(LN):
                        for u in range(B):
                            eng.wait_ge(s.stats, (i * LN + n) * B + u + 1)
                            eng.tensor_tensor(rstd[:, u, n, :], mv[:, u, n, :, 1], K.minus_half[:, 0:T], ALU.pow
                                              ).then_inc(s.powered, 1)
                            eng.wait_ge(s.powered, (i * LN + n) * B + u + 1)
                            eng.tensor_tensor(shift[:, u, n, :], mv[:, u, n, :, 0], rstd[:, u, n, :], ALU.mult
                                              ).then_inc(s.rstd_ready, 1)

            @block.vector
            def _(eng):
                with eng.Fori(0, turns) as i:
                    step = LoopOrder(eng, s.step, B * (2 * LN + 1), i)

                    def layer_norm_stats(n, x):
                        for u in range(B):
                            stats_of(eng, step, s.gate, x[:, u, :, :], st[:, u, :, :], mv[:, u, n, :, :], T)
                            eng.tensor_scalar(mv[:, u, n, :, 0], mv[:, u, n, :, 0], -1.0, None, ALU.mult).then_inc(s.stats, 1)

                    eng.wait_ge(s.x_loaded, 16 * B * (i + 1))
                    layer_norm_stats(0, x_in)
                    for l in range(L):
                        eng.wait_ge(s.rows_free, i * L + l + 1)
                        for u in range(B):
                            eng.wait_ge(s.rows_ready, (i * L + l) * B + u + 1)
                            to = rows[:, u, l % 2, :, :]
                            if l > 0:
                                eng.tensor_copy(to[:, :, 0:D], psR[u].rearrange("p (t d) -> p t d", d=D))
                            eng.tensor_copy(to[:, :, D:ROWW], psS[u].rearrange("p (t c) -> p t c", c=4)
                                            ).then_inc(s.rows_done, 1)
                    for u in range(B):
                        eng.wait_ge(s.last_turned, B * i + u + 1)
                        eng.tensor_tensor(xs[:, u, :, :], x_in[:, u, :, :],
                                          psR[u].rearrange("p (t d) -> p t d", d=D), ALU.add).then_inc(s.x1_done, 1)
                    eng.wait_ge(s.x1_done, B * i + B)
                    layer_norm_stats(1, xs)
                    eng.wait_ge(s.normed, (i * LN + 2) * B)
                    for u in range(B):
                        step(eng.scalar_tensor_tensor(xs[:, u, :, :], h_rows[:, u, 0, :, :], K.hgt_gate[:, 1:2],
                                                      xs[:, u, :, :], ALU.mult, ALU.add))
                        if u < B - 1:
                            eng.tensor_tensor(xs[:, u, :, :], xs[:, u, :, :], spread(K.hgt_ba[:, :], 1, T), ALU.add)
                        else:
                            eng.tensor_tensor(xs[:, u, :, :], xs[:, u, :, :], spread(K.hgt_ba[:, :], 1, T),
                                              ALU.add).then_inc(s.x2_done, 1)
                    eng.wait_ge(s.x2_done, i + 1)
                    layer_norm_stats(2, xs)
                    for u in range(B):
                        eng.wait_ge(s.turned_back, 2 * B * i + u + 1)
                        eng.tensor_tensor(xs[:, u, :, :], xs[:, u, :, :],
                                          psZ[u][:, :].rearrange("p (t d) -> p t d", d=D), ALU.add).then_inc(s.x3_done, 1)
                    eng.wait_ge(s.x3_done, B * i + B)
                    layer_norm_stats(3, xs)
                    eng.wait_ge(s.out_free, i + 1)
                    for u in range(B):
                        eng.wait_ge(s.turned_back, (2 * i + 1) * B + u + 1)
                        eng.tensor_tensor(x_out[:, u, :, :], xs[:, u, :, :],
                                          psZ[u][:, :].rearrange("p (t d) -> p t d", d=D), ALU.add).then_inc(s.finished, 1)
                    step.end()

            @block.tensor
            def _(eng):
                with eng.Fori(0, turns) as i:
                    def turn_rows(n, ln, h):
                        for u in range(B):
                            eng.wait_ge(s.normed, (i * LN + ln) * B + u + 1)
                            for t in range(T):
                                mm = eng.transpose(psT[u][:, t * P:(t + 1) * P], h(u)[:, t, 0:D], K.ident[:, :])
                            mm.then_inc(s.turned, 1)

                    turn_rows(0, 0, lambda u: rows[:, u, 0, :, :])
                    for l in range(L):
                        for u in range(B):
                            if l == 0:
                                eng.wait_ge(s.copiedT, 3 * B * i + u + 1)
                            else:
                                eng.wait_ge(s.hT_ready, (i * L + l - 1) * B + u + 1)
                            eng.matmul(psZ[u][:, :], K.gat_wm[:, l, :], hT[:, u, l % 2, :], start=True, stop=True
                                       ).then_inc(s.mixed, 1)
                        for u in range(B):
                            if l > 0:
                                eng.wait_ge(s.rows_done, (i * L + l - 1) * B + u + 1)
                            for t in range(T):
                                if l > 0:
                                    eng.transpose(psR[u][:, t * P:(t + 1) * P], hT[:, u, l % 2, t * P:(t + 1) * P],
                                                  K.ident[:, :])
                                mm = eng.matmul(psS[u][:, 4 * t:4 * t + 4], hT[:, u, l % 2, t * P:(t + 1) * P],
                                                K.gat_v[:, l, :], start=True, stop=True)
                            mm.then_inc(s.rows_ready, 1)
                    for u in range(B):
                        eng.wait_ge(s.hT_ready, (i * L + L - 1) * B + u + 1)
                        eng.wait_ge(s.rows_done, (i * L + L - 1) * B + u + 1)
                        for t in range(T):
                            mm = eng.transpose(psR[u][:, t * P:(t + 1) * P], hT[:, u, L % 2, t * P:(t + 1) * P], K.ident[:, :])
                        mm.then_inc(s.last_turned, 1)
                    for n, w in enumerate((K.gcn_w[:, :], K.cat_wu[:, 0, 0:D])):
                        turn_rows(1 + n, 2 + n, lambda u: h_rows[:, u, 1 + n, :, :])
                        for u in range(B):
                            eng.wait_ge(s.copiedT, (3 * i + n + 1) * B + u + 1)
                            eng.matmul(psZ[u][:, :], w, hT[:, u, n, :], start=True, stop=True).then_inc(s.wide, 1)
                        for u in range(B):
                            eng.wait_ge(s.zT_ready, (2 * i + n) * B + u + 1)
                            for t in range(T):
                                mm = eng.transpose(psZ[u][:, t * P:(t + 1) * P], zT[:, u, t * P:(t + 1) * P], K.ident[:, :])
                            mm.then_inc(s.turned_back, 1)

            @block.scalar
            def _(eng):
                eng.preload_act_table(ACT.Gelu)
                with eng.Fori(0, turns) as i:
                    def copy_turned(n, buf):
                        for u in range(B):
                            eng.wait_ge(s.turned, (3 * i + n) * B + u + 1)
                            eng.activation(hT[:, u, buf, :], psT[u][:, :], ACT.Copy).then_inc(s.copiedT, 1)

                    def layer_norm(n, x, to):
                        for u in range(B):
                            eng.wait_ge(s.rstd_ready, (i * LN + n) * B + u + 1)
                            for t in range(T):
                                ins = eng.activation(to(u)[:, t, 0:D], x[:, u, t, :], ACT.Relu, bias=shift[:, u, n, t:t + 1],
                                                     scale=rstd[:, u, n, t:t + 1])
                            ins.then_inc(s.normed, 1)

                    def product(n, func, bias):
                        for u in range(B):
                            eng.wait_ge(s.wide, (2 * i + n) * B + u + 1)
                            eng.activation(zT[:, u, :], psZ[u][:, :], func, bias=bias).then_inc(s.zT_ready, 1)

                    eng.wait_ge(s.rows_free, i * L + 2)
                    layer_norm(0, x_in, lambda u: rows[:, u, 0, :, :])
                    copy_turned(0, 0)
                    for l in range(L):
                        for u in range(B):
                            eng.wait_ge(s.mixed, (i * L + l) * B + u + 1)
                            eng.activation(hT[:, u, (l + 1) % 2, :], psZ[u][:, :],
                                           ACT.Relu if l < L - 1 else ACT.Identity,
                                           bias=K.gat_bias[:, l:l + 1]).then_inc(s.hT_ready, 1)
                    eng.wait_ge(s.out_free, i + 1)
                    layer_norm(1, xs, lambda u: h_rows[:, u, 0, :, :])
                    layer_norm(2, xs, lambda u: h_rows[:, u, 1, :, :])
                    copy_turned(1, 0)
                    product(0, ACT.Gelu, K.by_feature[:, 0:1])
                    layer_norm(3, xs, lambda u: h_rows[:, u, 2, :, :])
                    copy_turned(2, 1)
                    product(1, ACT.Identity, K.by_feature[:, 1:2])



def column(tile, c):
    w = tile.shape[2]
    return tile[:, :, :].rearrange("p c w -> p (c w)")[:, bass.ds(c * w, w)]


def slot_cols(g, n):
    return slice(TILES * g, TILES * g + 1) if tiles_of(g, n) == 1 else bass.ts(g, TILES)


def slot_rows(K, table, first, g, w=None):
    C, w = K.cols, w or table.shape[1]
    if tiles_of(g, C // TILES) == 1:
        return table[first + P * C:first + P * C + P, 0:w].unsqueeze(1)
    return table[first:first + P * C, 0:w].rearrange("(p c) w -> p c w", p=P)[:, bass.ts(g, TILES), :]


def gather(eng, table, index, to, sem):
    eng.indirect_dma_start(to, None, table, bass.IndirectOffsetOnAxis(ap=index, axis=0)).then_inc(sem, 16)


def turn_tiles(eng, K, ps, h, tiles):
    for t in range(tiles):
        mm = eng.transpose(ps[:, t * P:(t + 1) * P], h[:, t, 0:D], K.ident[:, :])
    return mm


def turn_back(eng, K, ps, hT, tiles):
    for t in range(tiles):
        mm = eng.transpose(ps[:, t * P:(t + 1) * P], hT[:, t * P:(t + 1) * P], K.ident[:, :])
    return mm


def by_tile(ps, tiles, w=D):
    return ps[:, 0:tiles * w].rearrange("p (t w) -> p t w", w=w)


def enter_slots(nc, K):
    C = K.cols
    n = C // TILES
    with ExitStack() as ctx:
        A = Buffers(nc, ctx, "enter")
        at = A.sb("at", [P, 2, TILES], I32)
        rows = A.sb("rows", [P, 2, TILES, ROWW])
        s = A.sems(("indexed", "r0_in", "r1_in", "taken", "stored", "free", "gate"))
        with nc.Block() as block:
            @block.gpsimd
            def _(eng):
                for i, both in batches(eng, n, 1):
                    for g, u in both:
                        eng.wait_ge(s.free, freed(g))
                        eng.wait_ge(s.taken, freed(g))
                        eng.sem_inc(s.gate, 1)
                        m = tiles_of(g, n)
                        eng.tensor_copy(at[:, u, 0:m], K.gather_dst[:, slot_cols(g, n)]).then_inc(s.indexed, 1)
                        eng.wait_ge(s.indexed, g + 1)
                        eng.sem_inc(s.gate, 1)
                        for t in range(m):
                            gather(eng, K.tables[0][0:K.rows, :], at[:, u, t:t + 1], rows[:, u, t, :], (s.r0_in, s.r1_in)[u])

            @block.vector
            def _(eng):
                eng.sem_inc(s.taken, 2)
                for i, both in batches(eng, n, 1):
                    for g, u in both:
                        m = tiles_of(g, n)
                        eng.wait_ge((s.r0_in, s.r1_in)[u], i * 16 * TILES + 16 * m)
                        eng.tensor_scalar(K.sc[:, :, slot_cols(g, n)], rows[:, u, 0:m, D:ROWW].rearrange("p t c -> p c t"),
                                          0.0, None, ALU.add).then_inc(s.taken, 1)

            @block.sync
            def _(eng):
                eng.sem_inc(s.free, 2)
                for i, both in batches(eng, n, 1):
                    for g, u in both:
                        m = tiles_of(g, n)
                        eng.wait_ge((s.r0_in, s.r1_in)[u], i * 16 * TILES + 16 * m)
                        eng.dma_start(slot_rows(K, K.tables[0], K.rows, g), rows[:, u, 0:m, :]).then_inc(s.stored, 16)
                        eng.wait_ge(s.stored, g * 16 + 16)
                        eng.sem_inc(s.free, 1)



def gather_rows(nc, K, l, table, w, to, scores=None):
    n = K.cols // TILES
    with ExitStack() as ctx:
        A = Buffers(nc, ctx, f"gather{l}")
        at = A.sb("at", [P, 2, TILES], I32)
        ring = A.sb("ring", [P, 2, TILES, w])
        s = A.sems(("indexed", "r0_in", "r1_in", "taken", "gate"))
        with nc.Block() as block:
            @block.gpsimd
            def _(eng):
                eng.sem_inc(s.taken, 2)
                for i, both in batches(eng, n):
                    for g, u in both:
                        eng.wait_ge(s.taken, freed(g))
                        eng.sem_inc(s.gate, 1)
                        eng.tensor_copy(at[:, u, :], K.src_row[:, bass.ts(g, TILES)]).then_inc(s.indexed, 1)
                        eng.wait_ge(s.indexed, g + 1)
                        eng.sem_inc(s.gate, 1)
                        for t in range(TILES):
                            gather(eng, table, at[:, u, t:t + 1], ring[:, u, t, :], (s.r0_in, s.r1_in)[u])

            @block.vector
            def _(eng):
                for i, both in batches(eng, n):
                    for g, u in both:
                        eng.wait_ge((s.r0_in, s.r1_in)[u], (i + 1) * 16 * TILES)
                        if scores is not None:
                            eng.tensor_scalar(scores[:, :, bass.ts(g, TILES)],
                                              ring[:, u, :, D:D + GAT_HEADS].rearrange("p t h -> p h t"), 0.0, None, ALU.add)
                        eng.tensor_scalar(to[:, bass.ds(g * TILES + 1, TILES), :], ring[:, u, :, 0:D], 0.0, None, ALU.max
                                          ).then_inc(s.taken, 1)


def gat_weights(nc, K, I, l, src_score, alpha, alpha_self):
    C, H = K.cols, GAT_HEADS
    with ExitStack() as ctx:
        A = Buffers(nc, ctx, f"attend{l}")
        R = RunTotals(K, A, 4)
        node = A.sb("node", [P, 4, C])
        extra = A.sb("extra", [P, 4])
        part = C // 4
        edge_x = A.sb("edge_x", [P, C, EDGE_F])
        prod = A.sb("prod", [P, part, EDGE_F])
        edge, top = A.sb("edge", [P, H, C]), A.sb("top", [P, H, C])
        loop = A.sb("loop", [P, H, C])
        step_sem, to_exp, from_exp, x_in = A.sem("step"), A.sem("to_exp"), A.sem("from_exp"), A.sem("x_in")
        with nc.Block() as block:
            @block.sync
            def _(eng):
                eng.dma_start(edge_x[:, :, :], I.edge_x).then_inc(x_in, 16)

            @block.vector
            def _(eng):
                step = Order(eng, step_sem)
                step(eng.tensor_tensor(node[:, :, :], K.sc[:, :, 0:C], spread(K.own[:, 0:C], 1, 4), ALU.mult))
                step(eng.tensor_scalar(extra[:, :], K.sc[:, :, C], K.own[:, C:C + 1], None, ALU.mult))
                R.on_vector(eng, step, node, ALU.add, 4, extra[:, :])
                eng.wait_ge(x_in, 16)
                for h in range(H):
                    u = K.gat_u[:, l * H + h, :]
                    for c in range(0, C, part):
                        step(eng.tensor_tensor(prod[:, :, :], edge_x[:, c:c + part, :], spread(u[:, 0:EDGE_F], 1, part), ALU.mult))
                        step(eng.tensor_reduce(edge[:, h, c:c + part], prod[:, :, :], AX.X, ALU.add))
                    step(eng.tensor_scalar(node[:, 2 + h, :], node[:, 2 + h, :], u[:, EDGE_F:EDGE_F + 1], None, ALU.add))
                step(eng.tensor_tensor(edge[:, :, :], edge[:, :, :], node[:, 2:4, :], ALU.add))
                step(eng.tensor_tensor(edge[:, :, :], edge[:, :, :], src_score[:, :, :], ALU.add))
                step(eng.scalar_tensor_tensor(edge[:, :, :], edge[:, :, :], 0.2, edge[:, :, :], ALU.mult, ALU.max))
                step(eng.tensor_tensor(loop[:, :, :], node[:, 0:2, :], node[:, 2:4, :], ALU.add))
                step(eng.scalar_tensor_tensor(loop[:, :, :], loop[:, :, :], 0.2, loop[:, :, :], ALU.mult, ALU.max))
                step(eng.tensor_copy(top[:, :, :], edge[:, :, :]))
                R.on_vector(eng, step, top, ALU.max, H)
                step(eng.tensor_tensor(top[:, :, :], top[:, :, :], loop[:, :, :], ALU.max))
                step(eng.tensor_tensor(edge[:, :, :], edge[:, :, :], top[:, :, :], ALU.subtract))
                step(eng.tensor_tensor(loop[:, :, :], loop[:, :, :], top[:, :, :], ALU.subtract))
                eng.sem_inc(to_exp, 1)
                eng.wait_ge(from_exp, 2)
                step(eng.tensor_copy(top[:, :, :], edge[:, :, :]))
                R.on_vector(eng, step, top, ALU.add, H)
                step(eng.tensor_tensor(top[:, :, :], top[:, :, :], loop[:, :, :], ALU.add))
                step(eng.reciprocal(top[:, :, :], top[:, :, :]))
                step(eng.tensor_tensor(alpha[:, :, :], edge[:, :, :], top[:, :, :], ALU.mult))
                step(eng.tensor_tensor(loop[:, :, :], loop[:, :, :], top[:, :, :], ALU.mult))
                step(eng.tensor_tensor(alpha_self[:, :, 0:C], loop[:, :, :], spread(K.own[:, 0:C], 1, H), ALU.mult))
                step(eng.tensor_copy(alpha_self[:, :, C], loop[:, :, 0]))

            @block.tensor
            def _(eng):
                R.on_tensor(eng, 4)
                R.on_tensor(eng, H)
                R.on_tensor(eng, H)

            @block.scalar
            def _(eng):
                eng.preload_act_table(ACT.Exp)
                eng.wait_ge(to_exp, 1)
                eng.activation(edge[:, :, :], edge[:, :, :], ACT.Exp).then_inc(from_exp, 1)
                eng.activation(loop[:, :, :], loop[:, :, :], ACT.Exp).then_inc(from_exp, 1)


def gat_slots(nc, K, I, l, G, alpha, alpha_self):
    C, H = K.cols, GAT_HEADS
    n = C // TILES
    E2 = H * EDGE_F
    last = l == GAT_LAYERS - 1
    table = K.gat_out if last else K.tables[l + 1]
    first, w = (0, D) if last else (K.rows, ROWW)
    with ExitStack() as ctx:
        A = Buffers(nc, ctx, f"gat{l}")
        own = A.sb("own", [P, 2, TILES, ROWW])
        part = A.sb("part", [P, 2, H * D])
        edge_x, part_e = A.sb("edge_x", [P, 2, TILES, EDGE_F]), A.sb("part_e", [P, 2, TILES, E2])
        run, run_e = A.sb("run", [P, 2, TILES, H * D]), A.sb("run_e", [P, 2, TILES, E2])
        loop = A.sb("loop", [P, 2, TILES, H, D])
        aggT = A.sb("aggT", [P, 2, H, GROUP])
        edgeT = A.sb("edgeT", [E2, 2, GROUP])
        zT, hT = A.sb("zT", [P, 2, GROUP]), A.sb("hT", [P, 2, GROUP])
        rows = A.sb("rows", [P, 2, TILES, ROWW])
        psA = [[A.ps(f"psA{u}{h}", [P, GROUP]) for h in range(H)] for u in range(2)]
        psE, psZ, psR, psS = (A.ps(m, [P, GROUP]) for m in ("psE", "psZ", "psR", "psS"))
        s = A.sems((
            "own0_in", "own1_in", "x0_in", "x1_in", "part_ready", "run_ready", "looped", "agg_turned", "aggT0", "aggT1", "edgeT_ready",
            "mixed", "zT_ready", "hT_ready", "rows_ready", "rows_done", "stored", "free", "gate", "zeroed"))
        with nc.Block() as block:
            @block.sync
            def _(eng):
                def load(both):
                    for g, u in both:
                        eng.wait_ge(s.looped, freed(g))
                        eng.dma_start(own[:, u, :, :], slot_rows(K, K.tables[l], K.rows, g)).then_inc((s.own0_in, s.own1_in)[u], 16)
                        eng.wait_ge(s.agg_turned, freed(g))
                        eng.dma_start(edge_x[:, u, :, :], I.edge_x[:, bass.ts(g, TILES), :]).then_inc((s.x0_in, s.x1_in)[u], 16)

                eng.sem_inc(s.free, 2)

                def store(both):
                    for g, u in both:
                        eng.wait_ge(s.rows_done, g + 2)
                        eng.dma_start(slot_rows(K, table, first, g), rows[:, u, :, 0:w]).then_inc(s.stored, 16)

                def stored(i, both):
                    eng.wait_ge(s.stored, i * 32 + 16 * len(both))
                    eng.sem_inc(s.free, len(both))

                overlapped_transfers(eng, n, load, store, stored)

            @block.vector
            def _(eng):
                eng.memset(run[:, 1, TILES - 1, :], 0.0).then_inc(s.run_ready, 1)
                eng.memset(run_e[:, 1, TILES - 1, :], 0.0).then_inc(s.run_ready, 1)
                eng.sem_inc(s.rows_done, 1)
                def sum_runs(i, g, u):
                    def weigh(t):
                        for h in range(H):
                            ins = eng.tensor_scalar(part[:, t % 2, h * D:(h + 1) * D], column(G, g * TILES + t + 1),
                                                    alpha[:, h, bass.ds(g * TILES + t, 1)], None, ALU.mult)
                        ins.then_inc(s.part_ready, 1)

                    eng.wait_ge((s.x0_in, s.x1_in)[u], (i + 1) * 16)
                    for h in range(H):
                        eng.tensor_tensor(part_e[:, u, :, h * EDGE_F:(h + 1) * EDGE_F], edge_x[:, u, :, :],
                                          spread(alpha[:, h, bass.ts(g, TILES)], 2, EDGE_F), ALU.mult)
                    weigh(0)
                    eng.wait_ge(s.agg_turned, freed(g))
                    for t in range(TILES):
                        c = g * TILES + t
                        eng.wait_ge(s.run_ready, c + 2)
                        if t + 1 < TILES:
                            weigh(t + 1)
                        before = (u, t - 1) if t else (1 - u, TILES - 1)
                        eng.wait_ge(s.part_ready, c + 1)
                        eng.scalar_tensor_tensor(run_e[:, u, t, :], run_e[:, before[0], before[1], :],
                                                 K.cont[:, bass.ds(c, 1)], part_e[:, u, t, :], ALU.mult, ALU.add)
                        eng.scalar_tensor_tensor(run[:, u, t, :], run[:, before[0], before[1], :],
                                                 K.cont[:, bass.ds(c, 1)], part[:, t % 2, :], ALU.mult, ALU.add
                                                 ).then_inc(s.run_ready, 1)

                def rows_out(g, u):
                    eng.wait_ge(s.rows_ready, g + 1)
                    eng.wait_ge(s.free, freed(g))
                    if not last:
                        eng.tensor_scalar(K.sc_next[:, :, bass.ts(g, TILES)],
                                          psS[:, 16 * u:16 * u + 16].rearrange("p (t c) -> p c t", c=4), 0.0, None, ALU.add)
                        eng.tensor_copy(rows[:, u, :, D:ROWW], psS[:, 16 * u:16 * u + 16].rearrange("p (t c) -> p t c", c=4))
                    eng.tensor_copy(rows[:, u, :, 0:D], by_tile(psR, TILES)).then_inc(s.rows_done, 1)

                for i, begun, ending in overlapped(eng, n):
                    for g, u in ending:
                        eng.wait_ge(s.agg_turned, done(g))
                        eng.tensor_copy(aggT[:, u, 0, :], psA[u][0][:, :]).then_inc(s.aggT0, 1)
                    for k in range(2):
                        for g, u in begun[k:k + 1]:
                            sum_runs(i, g, u)
                        for g, u in ending[k:k + 1]:
                            rows_out(g, u)

            @block.scalar
            def _(eng):
                eng.preload_act_table(ACT.Relu)
                eng.sem_inc(s.looped, 2)
                eng.sem_inc(s.edgeT_ready, 1)
                eng.sem_inc(s.hT_ready, 1)

                def loops(i, g, u):
                    eng.wait_ge((s.own0_in, s.own1_in)[u], (i + 1) * 16)
                    eng.wait_ge(s.agg_turned, freed(g))
                    eng.sem_inc(s.gate, 1)
                    for t in range(TILES):
                        for h in range(H):
                            ins = eng.activation(loop[:, u, t, h, :], own[:, u, t, 0:D], ACT.Relu,
                                                 scale=alpha_self[:, h, bass.ds(g * TILES + t, 1)])
                    ins.then_inc(s.looped, 1)

                for i, begun, ending in overlapped(eng, n):
                    for g, u in ending:
                        eng.wait_ge(s.agg_turned, done(g))
                        eng.activation(aggT[:, u, 1, :], psA[u][1][:, :], ACT.Copy).then_inc(s.aggT1, 1)
                        eng.activation(edgeT[:, u, :], psE[0:E2, :], ACT.Copy).then_inc(s.edgeT_ready, 1)
                    for g, u in begun[0:1]:
                        loops(i, g, u)
                    for g, u in ending:
                        eng.wait_ge(s.mixed, g + 1)
                        eng.activation(zT[:, u, :], psZ[:, :], ACT.Identity, bias=K.gat_bias[:, l:l + 1]
                                       ).then_inc(s.zT_ready, 1)
                        eng.activation(hT[:, u, :], psZ[:, :], ACT.Relu, bias=K.gat_bias[:, l:l + 1]
                                       ).then_inc(s.hT_ready, 1)
                    for g, u in begun[1:2]:
                        loops(i, g, u)

            @block.tensor
            def _(eng):
                eng.sem_inc(s.agg_turned, 2)

                def turn_sums(g, u):
                    eng.wait_ge(s.run_ready, g * TILES + 2 + TILES)
                    eng.wait_ge(s.looped, done(g))
                    if not isinstance(g, int) or g > 1:
                        eng.wait_ge(s.aggT0, g - 1)
                        eng.wait_ge(s.aggT1, g - 1)
                    for t in range(TILES):
                        for h in range(H):
                            o = psA[u][h][:, t * P:(t + 1) * P]
                            eng.matmul(o, run[:, u, t, h * D:(h + 1) * D], K.ident[:, :], is_transpose=True,
                                       start=True, stop=False)
                            eng.matmul(o, loop[:, u, t, h, :], K.ident[:, :], is_transpose=True, start=False, stop=True)
                    eng.wait_ge(s.edgeT_ready, g + 1)
                    for t in range(TILES):
                        mm = eng.transpose(psE[0:E2, t * P:(t + 1) * P], run_e[:, u, t, :], K.ident[:, :])
                    mm.then_inc(s.agg_turned, 1)

                def turn_rows(g, u):
                    eng.wait_ge(s.zT_ready, g + 1)
                    eng.wait_ge(s.hT_ready, g + 2)
                    eng.wait_ge(s.rows_done, g + 1)
                    for t in range(TILES):
                        mm = eng.transpose(psR[:, t * P:(t + 1) * P], zT[:, u, t * P:(t + 1) * P], K.ident[:, :])
                        if not last:
                            mm = eng.matmul(psS[:, 16 * u + 4 * t:16 * u + 4 * t + 4], hT[:, u, t * P:(t + 1) * P],
                                            K.gat_v[:, l + 1, :], start=True, stop=True)
                    mm.then_inc(s.rows_ready, 1)

                for i, begun, ending in overlapped(eng, n):
                    for g, u in ending:
                        eng.wait_ge(s.aggT0, g + 1)
                        eng.wait_ge(s.aggT1, g + 1)
                        eng.wait_ge(s.edgeT_ready, g + 2)
                        eng.wait_ge(s.hT_ready, g + 1)
                        for h in range(H):
                            eng.matmul(psZ[:, :], K.gat_wh[:, l, h, :], aggT[:, u, h, :], start=(h == 0), stop=False)
                        eng.matmul(psZ[:, :], K.gat_ewT[:, l, :], edgeT[:, u, :], start=False, stop=True).then_inc(s.mixed, 1)
                    for k in range(2):
                        for g, u in ending[k:k + 1]:
                            turn_rows(g, u)
                        for g, u in begun[k:k + 1]:
                            turn_sums(g, u)


def gat_extra(nc, K, l, alpha_self):
    C, H = K.cols, GAT_HEADS
    last = l == GAT_LAYERS - 1
    table = K.gat_out if last else K.tables[l + 1]
    first, w = (0, D) if last else (K.rows, ROWW)
    with ExitStack() as ctx:
        A = Buffers(nc, ctx, f"gatx{l}")
        own, rows = A.sb("own", [P, ROWW]), A.sb("rows", [P, ROWW])
        piece, ends = A.sb("piece", [P, w]), A.sb("ends", [P, D])
        loop, loopT = A.sb("loop", [P, H, D]), A.sb("loopT", [P, H * D])
        zT, hT = A.sb("zT", [P, P]), A.sb("hT", [P, P])
        psA, psZ, psR = A.ps("psA", [P, H * D]), A.ps("psZ", [P, P]), A.ps("psR", [P, ROWW])
        s = A.sems((
            "own_in", "piece_in", "ends_in", "ends_ready", "looped", "turned", "loopT_ready", "mixed", "zT_ready",
            "hT_ready", "rows_ready", "rows_done", "stored"))
        with nc.Block() as block:
            @block.sync
            def _(eng):
                eng.dma_start(own[:, :], slot_rows(K, K.tables[l], K.rows, C // TILES)[:, 0, :]).then_inc(s.own_in, 16)
                ends_of = table[first:first + P * C, 0:D].rearrange("(p c) w -> p c w", p=P)
                eng.dma_start(ends[:, :], ends_of[:, C - 1, :]).then_inc(s.ends_in, 16)
                eng.wait_ge(s.rows_done, 1)
                eng.dma_start(slot_rows(K, table, first, C // TILES)[:, 0, :], rows[:, 0:w]).then_inc(s.stored, 16)
                eng.wait_ge(s.stored, 16)

            @block.gpsimd
            def _(eng):
                gather(eng, table[0:first + P * C, :], (K.part_slot if last else K.part_row)[:, :], piece[:, :], s.piece_in)

            @block.vector
            def _(eng):
                eng.wait_ge(s.ends_in, 16)
                eng.tensor_tensor(ends[:, :], ends[:, :], K.gat_bias_rep[:, l, :], ALU.subtract).then_inc(s.ends_ready, 1)
                eng.wait_ge(s.turned, 1)
                eng.tensor_copy(loopT[:, :], psA[:, :]).then_inc(s.loopT_ready, 1)
                eng.wait_ge(s.mixed, 1)
                eng.tensor_copy(zT[:, :], psZ[:, :]).then_inc(s.zT_ready, 1)
                eng.tensor_scalar(hT[:, :], psZ[:, :], 0.0, None, ALU.max).then_inc(s.hT_ready, 1)
                eng.wait_ge(s.rows_ready, 1)
                if not last:
                    eng.tensor_copy(K.sc_next[:, :, C], psR[:, D:ROWW])
                eng.tensor_copy(rows[:, 0:w], psR[:, 0:w]).then_inc(s.rows_done, 1)

            @block.scalar
            def _(eng):
                eng.wait_ge(s.own_in, 16)
                for h in range(H):
                    eng.activation(loop[:, h, :], own[:, 0:D], ACT.Relu, scale=alpha_self[:, h, C:C + 1]).then_inc(s.looped, 1)

            @block.tensor
            def _(eng):
                eng.wait_ge(s.looped, H)
                for h in range(H):
                    mm = eng.transpose(psA[:, h * D:(h + 1) * D], loop[:, h, :], K.ident[:, :])
                mm.then_inc(s.turned, 1)
                eng.wait_ge(s.piece_in, 16)
                eng.wait_ge(s.ends_ready, 1)
                eng.wait_ge(s.loopT_ready, 1)
                for h in range(H):
                    eng.matmul(psZ[:, :], K.gat_wh[:, l, h, :], loopT[:, h * D:(h + 1) * D], start=(h == 0), stop=False)
                eng.matmul(psZ[:, :], piece[:, 0:D], K.ident[:, :], start=False, stop=False)
                eng.matmul(psZ[:, :], ends[:, :], K.carry[:, :], start=False, stop=True).then_inc(s.mixed, 1)
                eng.wait_ge(s.zT_ready, 1)
                eng.wait_ge(s.hT_ready, 1)
                mm = eng.transpose(psR[:, 0:D], zT[:, :], K.ident[:, :])
                if not last:
                    mm = eng.matmul(psR[:, D:ROWW], hT[:, :], K.gat_v[:, l + 1, :], start=True, stop=True)
                mm.then_inc(s.rows_ready, 1)


def stats_then_negated(eng, step, gate, x, st, mv, n):
    stats_of(eng, step, gate, x, st, mv, n)
    return eng.tensor_scalar(mv[:, 0:n, 0], mv[:, 0:n, 0], -1.0, None, ALU.mult)


def rstd_and_shift(eng, K, s, g, mv, rstd, shift):
    eng.wait_ge(s.stats, g + 1)
    eng.tensor_tensor(rstd, mv[:, :, 1], K.minus_half[:, :], ALU.pow).then_inc(s.powered, 1)
    eng.wait_ge(s.powered, g + 1)
    eng.tensor_tensor(shift, mv[:, :, 0], rstd, ALU.mult).then_inc(s.rstd_ready, 1)


def norm_relu(eng, x, rstd, shift, out, n):
    for t in range(n):
        ins = eng.activation(out[:, t, 0:D], x[:, t, :], ACT.Relu, bias=shift[:, t:t + 1], scale=rstd[:, t:t + 1])
    return ins


def gat_to_hgt(nc, K, I):
    C = K.cols
    n = C // TILES
    with ExitStack() as ctx:
        A = Buffers(nc, ctx, "to_hgt")
        at = A.sb("at", [P, 2, TILES], I32)
        z, x = A.sb("z", [P, 2, TILES, D]), A.sb("x", [P, 2, TILES, D])
        x1, rows, q = (A.sb(m, [P, 2, TILES, D]) for m in ("x1", "rows", "q"))
        hT, qT = A.sb("hT", [P, 2, GROUP]), A.sb("qT", [P, 2, GROUP])
        st, mv = A.sb("st", [P, 2, TILES, 6]), A.sb("mv", [P, 2, TILES, 2])
        rstd, shift = A.sb("rstd", [P, 2, TILES]), A.sb("shift", [P, 2, TILES])
        psT = [A.ps(f"psT{u}", [P, GROUP]) for u in range(2)]
        psZ = [A.ps(f"psZ{u}", [P, GROUP]) for u in range(2)]
        psQ = [A.ps(f"psQ{u}", [P, GROUP]) for u in range(2)]
        s = A.sems((
            "indexed", "z0_in", "z1_in", "x0_in", "x1_in", "summed", "stats", "powered", "rstd_ready", "normed", "turned",
            "copiedT", "projected", "qT_ready", "q_turned", "q_done", "stored", "free", "q_stored", "q_free", "step", "gate"))
        with nc.Block() as block:
            @block.sync
            def _(eng):
                def load(both):
                    for g, u in both:
                        m = tiles_of(g, n)
                        eng.wait_ge(s.summed, freed(g))
                        eng.dma_start(z[:, u, 0:m, :], slot_rows(K, K.gat_out, 0, g)).then_inc((s.z0_in, s.z1_in)[u], 16)

                eng.sem_inc(s.q_free, 2)
                load(batch(0, n, 1))
                for i, ahead, begun, ending in transfers(eng, n, 1):
                    load(ahead)
                    for g, u in begun:
                        m = tiles_of(g, n)
                        eng.wait_ge(s.normed, g + 1)
                        eng.dma_start(slot_rows(K, K.tables[5], K.rows, g), rows[:, u, 0:m, :]).then_inc(s.stored, 16)
                        eng.dma_start(slot_rows(K, K.resid, 0, g), x1[:, u, 0:m, :]).then_inc(s.stored, 16)
                    if begun:
                        eng.wait_ge(s.stored, i * 64 + 32 * len(begun))
                        for g, u in begun:
                            eng.wait_ge(s.turned, g + 1)
                        eng.sem_inc(s.free, 2)
                    for g, u in ending:
                        m = tiles_of(g, n)
                        eng.wait_ge(s.q_done, done(g))
                        eng.dma_start(slot_rows(K, K.hgt_q, 0, g), q[:, u, 0:m, :]).then_inc(s.q_stored, 16)
                        eng.wait_ge(s.q_stored, g * 16 + 16)
                        eng.sem_inc(s.q_free, 1)

            @block.gpsimd
            def _(eng):
                eng.sem_inc(s.free, 2)

                def gather_x(i, both):
                    for g, u in both:
                        m = tiles_of(g, n)
                        eng.wait_ge(s.summed, freed(g))
                        eng.sem_inc(s.gate, 1)
                        eng.tensor_copy(at[:, u, 0:m], K.gather_dst[:, slot_cols(g, n)]).then_inc(s.indexed, 1)
                        eng.wait_ge(s.indexed, g + 1)
                        eng.sem_inc(s.gate, 1)
                        for t in range(m):
                            gather(eng, I.x, at[:, u, t:t + 1], x[:, u, t, :], (s.x0_in, s.x1_in)[u])

                gather_x(0, batch(0, n, 1))
                for i, both, j, ahead in batches_ahead(eng, n, 1):
                    for g, u in both:
                        rstd_and_shift(eng, K, s, g, mv[:, u, :, :], rstd[:, u, :], shift[:, u, :])
                    gather_x(j, ahead)

            @block.vector
            def _(eng):
                eng.memset(mv[:, :, :, :], 1.0).then_inc(s.step, 1)
                eng.wait_ge(s.step, 1)
                eng.sem_inc(s.summed, 2)
                eng.sem_inc(s.q_done, 2)
                for i, begun, ending in overlapped(eng, n, 1):
                    step = LoopOrder(eng, s.step, 4, i, 1)
                    for g, u in begun:
                        m = tiles_of(g, n)
                        eng.wait_ge((s.z0_in, s.z1_in)[u], (i + 1) * 16)
                        eng.wait_ge((s.x0_in, s.x1_in)[u], i * 16 * TILES + 16 * m)
                        eng.wait_ge(s.free, freed(g))
                        eng.tensor_tensor(x1[:, u, 0:m, :], z[:, u, 0:m, :], x[:, u, 0:m, :], ALU.add).then_inc(s.summed, 1)
                    for g, u in begun:
                        eng.wait_ge(s.summed, done(g))
                        stats_then_negated(eng, step, s.gate, x1[:, u, :, :], st[:, u, :, :], mv[:, u, :, :], tiles_of(g, n)
                                           ).then_inc(s.stats, 1)
                    for g, u in ending:
                        m = tiles_of(g, n)
                        eng.wait_ge(s.q_turned, g + 1)
                        eng.wait_ge(s.q_free, freed(g))
                        eng.tensor_copy(q[:, u, 0:m, :], by_tile(psQ[u], m)).then_inc(s.q_done, 1)

            @block.tensor
            def _(eng):
                for i, both in batches(eng, n, 1):
                    for g, u in both:
                        eng.wait_ge(s.normed, g + 1)
                        turn_tiles(eng, K, psT[u], rows[:, u, :, :], tiles_of(g, n)).then_inc(s.turned, 1)
                    for g, u in both:
                        w = tiles_of(g, n) * P
                        eng.wait_ge(s.copiedT, g + 1)
                        eng.matmul(psZ[u][:, 0:w], K.hgt_wq[:, :], hT[:, u, 0:w], start=True, stop=True).then_inc(s.projected, 1)
                    for g, u in both:
                        eng.wait_ge(s.qT_ready, g + 1)
                        eng.wait_ge(s.q_done, freed(g))
                        turn_back(eng, K, psQ[u], qT[:, u, :], tiles_of(g, n)).then_inc(s.q_turned, 1)

            @block.scalar
            def _(eng):
                eng.preload_act_table(ACT.Relu)
                for i, both in batches(eng, n, 1):
                    for g, u in both:
                        eng.wait_ge(s.rstd_ready, g + 1)
                        norm_relu(eng, x1[:, u, :, :], rstd[:, u, :], shift[:, u, :], rows[:, u, :, :], tiles_of(g, n)
                                  ).then_inc(s.normed, 1)
                    for g, u in both:
                        w = tiles_of(g, n) * P
                        eng.wait_ge(s.turned, g + 1)
                        eng.activation(hT[:, u, 0:w], psT[u][:, 0:w], ACT.Copy).then_inc(s.copiedT, 1)
                    for g, u in both:
                        w = tiles_of(g, n) * P
                        eng.wait_ge(s.projected, g + 1)
                        eng.activation(qT[:, u, 0:w], psZ[u][:, 0:w], ACT.Identity, bias=K.by_feature[:, 2:3]
                                       ).then_inc(s.qT_ready, 1)



def typed_edges(nc, K, kind, V, score):
    C = K.cols
    n = C // TILES
    hgt = kind == "hgt"
    types = HGT_RELS if hgt else CAT_TYPES
    mask = K.rel_mask if hgt else K.type_mask
    src_table, dst_table = (K.tables[5], K.hgt_q) if hgt else (K.tables[7], K.cat_si)
    wd = dst_table.shape[1]
    wo = 2 * D if hgt else D + CAT_S
    heads = HGT_HEADS if hgt else CAT_HEADS
    with ExitStack() as ctx:
        A = Buffers(nc, ctx, kind)
        at, at_d = A.sb("at", [P, 2, TILES], I32), A.sb("at_d", [P, 2, TILES], I32)
        src, dst = A.sb("src", [P, 2, TILES, D]), A.sb("dst", [P, 2, TILES, wd])
        diag = A.sb("diag", [P, 2, TILES, types, P])
        hT = A.sb("hT", [P, 2, TILES, types * P])
        prod = A.sb("prod", [P, TILES, wd])
        part = A.sb("part", [P, TILES, CAT_S])
        psT = [A.ps(f"psT{t}", [P, types * P]) for t in range(TILES)]
        psO = [A.ps(f"psO{t}", [P, wo]) for t in range(TILES)]
        s = A.sems((
            "indexed", "indexed_d", "e0_in", "e1_in", "d0_in", "d1_in", "diag_ready", "turned", "copiedT", "made", "taken", "step", "gate"))
        with nc.Block() as block:
            @block.gpsimd
            def _(eng):
                eng.sem_inc(s.taken, 2)
                for i, both in batches(eng, n):
                    for g, u in both:
                        eng.wait_ge(s.turned, g * TILES + TILES)
                        eng.sem_inc(s.gate, 1)
                        eng.tensor_copy(at[:, u, :], K.src_row[:, bass.ts(g, TILES)]).then_inc(s.indexed, 1)
                        eng.wait_ge(s.indexed, g + 1)
                        eng.sem_inc(s.gate, 1)
                        for t in range(TILES):
                            gather(eng, src_table, at[:, u, t:t + 1], src[:, u, t, :], (s.e0_in, s.e1_in)[u])
                        eng.wait_ge(s.taken, freed(g))
                        eng.sem_inc(s.gate, 1)
                        eng.tensor_copy(at_d[:, u, :], K.dst_slot[:, bass.ts(g, TILES)]).then_inc(s.indexed_d, 1)
                        eng.wait_ge(s.indexed_d, g + 1)
                        eng.sem_inc(s.gate, 1)
                        for t in range(TILES):
                            gather(eng, dst_table, at_d[:, u, t:t + 1], dst[:, u, t, :], (s.d0_in, s.d1_in)[u])

            @block.tensor
            def _(eng):
                def turn(i, g, u):
                    eng.wait_ge((s.e0_in, s.e1_in)[u], (i + 1) * 16 * TILES)
                    eng.wait_ge(s.diag_ready, g + 1)
                    for t in range(TILES):
                        eng.matmul(psT[t][:, :], src[:, u, t, :], diag[:, u, t, :, :].rearrange("p r q -> p (r q)"),
                                   start=True, stop=True).then_inc(s.turned, 1)

                eng.sem_inc(s.made, 2)
                eng.sem_inc(s.turned, 2 * TILES)
                for i, both in batches(eng, n):
                    for g, u in both:
                        turn(i, g, u)
                        eng.wait_ge(s.taken, g + 2)
                        for t in range(TILES):
                            eng.wait_ge(s.copiedT, g * TILES + t + 1)
                            for r in range(types):
                                w = (K.hgt_kv if hgt else K.cat_wu)[:, r, :]
                                mm = eng.matmul(psO[t][:, :], hT[:, u, t, r * P:(r + 1) * P], w, start=(r == 0),
                                                stop=(not hgt and r == types - 1))
                            if hgt:
                                for r in range(types):
                                    mm = eng.matmul(psO[t][:, :], diag[:, u, t, r, :], K.hgt_kvb[:, r, :], start=False,
                                                    stop=(r == types - 1))
                        mm.then_inc(s.made, 1)

            @block.scalar
            def _(eng):
                eng.preload_act_table(ACT.Copy)
                for i, both in batches(eng, n):
                    for g, u in both:
                        for t in range(TILES):
                            eng.wait_ge(s.made, freed(g))
                            eng.wait_ge(s.turned, (g + 2) * TILES + t + 1)
                            eng.activation(hT[:, u, t, :], psT[t][:, :], ACT.Copy).then_inc(s.copiedT, 1)

            @block.vector
            def _(eng):
                def masked_identities(g, u):
                    eng.wait_ge(s.made, freed(g))
                    for t in range(TILES):
                        for r in range(types):
                            ins = eng.tensor_scalar(diag[:, u, t, r, :], K.ident[:, :],
                                                    mask[:, r, bass.ds(g * TILES + t, 1)], None, ALU.mult)
                    ins.then_inc(s.diag_ready, 1)

                masked_identities(0, 0)
                for i, both, j, ahead in batches_ahead(eng, n):
                    step = LoopOrder(eng, s.step, 2 * (1 if hgt else 5), i)
                    for g, u in both:
                        if u == 0 and len(both) > 1 or u == 1 and ahead:
                            masked_identities(g + 1, 1 - u)
                        eng.wait_ge((s.d0_in, s.d1_in)[u], (i + 1) * 16 * TILES)
                        eng.wait_ge(s.made, done(g))
                        to = V[:, bass.ds(g * TILES + 1, TILES), :]
                        for t in range(TILES):
                            o = psO[t][:, D:2 * D] if hgt else psO[t][:, 0:D]
                            eng.tensor_scalar(column(V, g * TILES + t + 1), o, 0.0, None, ALU.add)
                            if hgt:
                                ins = eng.tensor_tensor(prod[:, t, :], psO[t][:, 0:D], dst[:, u, t, :], ALU.mult)
                            else:
                                m = spread(mask[:, :, bass.ds(g * TILES + t, 1)].rearrange("p r one -> p (r one)"), 2, CAT_S)
                                ins = eng.tensor_tensor(prod[:, t, :].rearrange("p (r s) -> p r s", r=types),
                                                        dst[:, u, t, :].rearrange("p (r s) -> p r s", r=types), m, ALU.mult)
                        step(ins)
                        if hgt:
                            for t in range(TILES):
                                ins = eng.tensor_reduce(score[:, :, bass.ds(g * TILES + t, 1)],
                                                        prod[:, t, :].rearrange("p (h d) -> p h d", h=heads), AX.X, ALU.add)
                        else:
                            for t in range(TILES):
                                ins = eng.tensor_reduce(part[:, t, :], prod[:, t, :].rearrange("p (r s) -> p s r", r=types),
                                                        AX.X, ALU.add)
                            step(ins)
                            for t in range(TILES):
                                ins = eng.tensor_tensor(part[:, t, :], part[:, t, :], psO[t][:, D:D + CAT_S], ALU.add)
                            step(ins)
                            step(eng.scalar_tensor_tensor(part[:, :, :], part[:, :, :], 0.2, part[:, :, :], ALU.mult, ALU.max))
                            for t in range(TILES):
                                pk = spread(K.cat_pk[:, :], 2, CAT_HEADS)
                                ins = eng.tensor_tensor(part[:, t, :].rearrange("p (k h) -> p k h", k=CAT_CONF),
                                                        part[:, t, :].rearrange("p (k h) -> p k h", k=CAT_CONF), pk, ALU.mult)
                            step(ins)
                            for t in range(TILES):
                                ins = eng.tensor_reduce(score[:, :, bass.ds(g * TILES + t, 1)],
                                                        part[:, t, :].rearrange("p (k h) -> p h k", k=CAT_CONF), AX.X, ALU.add)
                        ins.then_inc(s.taken, 1)


def typed_weights(nc, K, kind, score):
    C = K.cols
    hgt = kind == "hgt"
    types, heads = (HGT_RELS, HGT_HEADS) if hgt else (CAT_TYPES, CAT_HEADS)
    mask = K.rel_mask if hgt else K.type_mask
    with ExitStack() as ctx:
        A = Buffers(nc, ctx, kind + "_attend")
        R = RunTotals(K, A, types * heads)
        val = A.sb("val", [P, types * heads, C])
        top = A.sb("top", [P, heads, C])
        away = A.sb("away", [P, types, C])
        imp = A.sb("imp", [P, C])
        step_sem, to_exp, from_exp = A.sem("step"), A.sem("to_exp"), A.sem("from_exp")
        with nc.Block() as block:
            @block.vector
            def _(eng):
                step = Order(eng, step_sem)

                def of_type(r):
                    return val[:, r * heads:(r + 1) * heads, :]

                def own_type():
                    for r in range(types):
                        step(eng.tensor_tensor(of_type(r), of_type(r), spread(mask[:, r, :], 1, heads), ALU.mult))
                    step(eng.tensor_tensor(top[:, :, :], of_type(0), of_type(1), ALU.add))
                    for r in range(2, types):
                        step(eng.tensor_tensor(top[:, :, :], top[:, :, :], of_type(r), ALU.add))

                step(eng.tensor_scalar(away[:, :, :], mask[:, :, :], 1.0, -FAR, ALU.subtract, ALU.mult))
                for r in range(types):
                    step(eng.tensor_tensor(of_type(r), score[:, :, :], spread(mask[:, r, :], 1, heads), ALU.mult))
                    step(eng.tensor_tensor(of_type(r), of_type(r), spread(away[:, r, :], 1, heads), ALU.add))
                R.on_vector(eng, step, val, ALU.max, types * heads)
                own_type()
                step(eng.tensor_tensor(score[:, :, :], score[:, :, :], top[:, :, :], ALU.subtract))
                eng.sem_inc(to_exp, 1)
                eng.wait_ge(from_exp, 1)
                for r in range(types):
                    step(eng.tensor_tensor(of_type(r), score[:, :, :], spread(mask[:, r, :], 1, heads), ALU.mult))
                R.on_vector(eng, step, val, ALU.add, types * heads)
                own_type()
                step(eng.reciprocal(top[:, :, :], top[:, :, :]))
                step(eng.tensor_tensor(score[:, :, :], score[:, :, :], top[:, :, :], ALU.mult))
                if not hgt:
                    step(eng.tensor_scalar(imp[:, :], mask[:, 0, :], K.cat_imp[:, 0:1], None, ALU.mult))
                    for r in range(1, types):
                        step(eng.scalar_tensor_tensor(imp[:, :], mask[:, r, :], K.cat_imp[:, r:r + 1], imp[:, :],
                                                      ALU.mult, ALU.add))
                    step(eng.tensor_tensor(score[:, :, :], score[:, :, :], spread(imp[:, :], 1, heads), ALU.mult))

            @block.tensor
            def _(eng):
                R.on_tensor(eng, types * heads)
                R.on_tensor(eng, types * heads)

            @block.scalar
            def _(eng):
                eng.preload_act_table(ACT.Exp)
                eng.wait_ge(to_exp, 1)
                eng.activation(score[:, :, :], score[:, :, :], ACT.Exp).then_inc(from_exp, 1)


def run_sums(nc, K, tag, V, weight, heads):
    C = K.cols
    n = C // TILES
    with ExitStack() as ctx:
        A = Buffers(nc, ctx, tag)
        piece, rows = A.sb("piece", [P, D]), A.sb("rows", [P, D])
        psX = A.ps("psX", [P, D])
        s = A.sems(("weighed", "summed", "stored", "piece_in", "mixed", "rows_done",
                                                     "out", "gate"))
        with nc.Block() as block:
            @block.vector
            def _(eng):
                eng.memset(V[:, 0, :], 0.0).then_inc(s.summed, 1)
                for i, both in batches(eng, n):
                    for g, u in both:
                        to = V[:, bass.ds(g * TILES + 1, TILES), :]
                        if weight is not None:
                            to = to.rearrange("p t (h d) -> p t h d", h=heads)
                            w = weight[:, :, bass.ts(g, TILES)].rearrange("p h t -> p t h")
                            eng.tensor_tensor(to, to, spread(w, 3, D // heads), ALU.mult).then_inc(s.weighed, 1)
                            eng.wait_ge(s.weighed, g + 1)
                        for t in range(TILES):
                            c = g * TILES + t
                            eng.wait_ge(s.summed, c + 1)
                            eng.scalar_tensor_tensor(column(V, c + 1), column(V, c), K.cont[:, bass.ds(c, 1)], column(V, c + 1),
                                                     ALU.mult, ALU.add).then_inc(s.summed, 1)
                eng.wait_ge(s.mixed, 1)
                eng.wait_ge(s.piece_in, 16)
                eng.tensor_tensor(rows[:, :], piece[:, :], psX[:, :], ALU.add).then_inc(s.rows_done, 1)

            @block.tensor
            def _(eng):
                eng.wait_ge(s.summed, C + 1)
                eng.matmul(psX[:, :], K.carry[:, :], V[:, C, :], start=True, stop=True).then_inc(s.mixed, 1)

            @block.sync
            def _(eng):
                for i, both in batches(eng, n):
                    for g, u in both:
                        eng.wait_ge(s.summed, g * TILES + TILES + 1)
                        eng.dma_start(slot_rows(K, K.sums, 0, g), V[:, bass.ds(g * TILES + 1, TILES), :]).then_inc(s.stored, 16)
                eng.wait_ge(s.stored, 16 * n)
                eng.sem_inc(s.out, 1)
                eng.wait_ge(s.rows_done, 1)
                eng.dma_start(slot_rows(K, K.sums, 0, n)[:, 0, :], rows[:, :]).then_inc(s.stored, 16)
                eng.wait_ge(s.stored, 16 * n + 16)

            @block.gpsimd
            def _(eng):
                eng.wait_ge(s.out, 1)
                gather(eng, K.sums[0:P * C, :], K.part_slot[:, :], piece[:, :], s.piece_in)


def hgt_to_gcn(nc, K):
    C = K.cols
    n = C // TILES
    with ExitStack() as ctx:
        A = Buffers(nc, ctx, "to_gcn")
        sums, x, h, x2, rows = (A.sb(m, [P, 2, TILES, D]) for m in ("sums", "x", "h", "x2", "rows"))
        hT, zT = A.sb("hT", [P, 2, GROUP]), A.sb("zT", [P, 2, GROUP])
        st, mv = A.sb("st", [P, 2, TILES, 6]), A.sb("mv", [P, 2, TILES, 2])
        rstd, shift, dinv = (A.sb(m, [P, 2, TILES]) for m in ("rstd", "shift", "dinv"))
        psT = [A.ps(f"psT{u}", [P, GROUP]) for u in range(2)]
        psZ = [A.ps(f"psZ{u}", [P, GROUP]) for u in range(2)]
        psO = [A.ps(f"psO{u}", [P, GROUP]) for u in range(2)]
        s = A.sems((
            "s0_in", "s1_in", "xh0_in", "xh1_in", "turned", "gelu_done", "projected", "zT_ready", "turned_back", "summed",
            "stats", "powered", "scaled", "rstd_ready", "rows_done", "stored", "free", "step", "gate"))
        with nc.Block() as block:
            @block.sync
            def _(eng):
                def load_sums(both):
                    for g, u in both:
                        m = tiles_of(g, n)
                        eng.wait_ge(s.turned, freed(g))
                        eng.dma_start(sums[:, u, 0:m, :], slot_rows(K, K.sums, 0, g)).then_inc((s.s0_in, s.s1_in)[u], 16)

                eng.sem_inc(s.free, 2)
                load_sums(batch(0, n, 1))
                for i, ahead, begun, ending in transfers(eng, n, 1):
                    load_sums(ahead)
                    for g, u in begun:
                        m = tiles_of(g, n)
                        eng.wait_ge(s.summed, freed(g))
                        for to, of, first in ((x, K.resid, 0), (h, K.tables[5], K.rows)):
                            eng.dma_start(to[:, u, 0:m, :], slot_rows(K, of, first, g)).then_inc((s.xh0_in, s.xh1_in)[u], 16)
                    for g, u in ending:
                        m = tiles_of(g, n)
                        eng.wait_ge(s.rows_done, g + 1)
                        eng.dma_start(slot_rows(K, K.tables[6], K.rows, g), rows[:, u, 0:m, :]).then_inc(s.stored, 16)
                        eng.dma_start(slot_rows(K, K.resid, 0, g), x2[:, u, 0:m, :]).then_inc(s.stored, 16)
                    if ending:
                        eng.wait_ge(s.stored, (i - 1) * 64 + 32 * len(ending))
                        eng.sem_inc(s.free, 2)

            @block.tensor
            def _(eng):
                eng.sem_inc(s.turned, 2)
                for i, both in batches(eng, n, 1):
                    for g, u in both:
                        eng.wait_ge((s.s0_in, s.s1_in)[u], (i + 1) * 16)
                        turn_tiles(eng, K, psT[u], sums[:, u, :, :], tiles_of(g, n)).then_inc(s.turned, 1)
                    for g, u in both:
                        w = tiles_of(g, n) * P
                        eng.wait_ge(s.gelu_done, g + 1)
                        eng.matmul(psZ[u][:, 0:w], K.hgt_wa[:, :], hT[:, u, 0:w], start=True, stop=True).then_inc(s.projected, 1)
                    for g, u in both:
                        eng.wait_ge(s.zT_ready, g + 1)
                        eng.wait_ge(s.summed, freed(g))
                        turn_back(eng, K, psO[u], zT[:, u, :], tiles_of(g, n)).then_inc(s.turned_back, 1)

            @block.scalar
            def _(eng):
                eng.preload_act_table(ACT.Gelu)
                for i, begun, ending in overlapped(eng, n, 1):
                    for g, u in begun:
                        w = tiles_of(g, n) * P
                        eng.wait_ge(s.turned, done(g))
                        eng.activation(hT[:, u, 0:w], psT[u][:, 0:w], ACT.Gelu).then_inc(s.gelu_done, 1)
                    for g, u in begun:
                        w = tiles_of(g, n) * P
                        eng.wait_ge(s.projected, g + 1)
                        eng.activation(zT[:, u, 0:w], psZ[u][:, 0:w], ACT.Identity, bias=K.by_feature[:, 3:4]
                                       ).then_inc(s.zT_ready, 1)
                    for g, u in ending:
                        eng.wait_ge(s.rstd_ready, g + 1)
                        norm_relu(eng, x2[:, u, :, :], rstd[:, u, :], shift[:, u, :], rows[:, u, :, :], tiles_of(g, n)
                                  ).then_inc(s.rows_done, 1)

            @block.gpsimd
            def _(eng):
                for i, both in batches(eng, n, 1):
                    for g, u in both:
                        eng.wait_ge(s.stats, g + 1)
                        eng.tensor_tensor(rstd[:, u, :], mv[:, u, :, 1], K.minus_half[:, :], ALU.pow).then_inc(s.powered, 1)
                        eng.wait_ge(s.powered, g + 1)
                        eng.tensor_tensor(rstd[:, u, :], rstd[:, u, :], dinv[:, u, :], ALU.mult).then_inc(s.scaled, 1)
                        eng.wait_ge(s.scaled, g + 1)
                        eng.tensor_tensor(shift[:, u, :], mv[:, u, :, 0], rstd[:, u, :], ALU.mult).then_inc(s.rstd_ready, 1)

            @block.vector
            def _(eng):
                eng.memset(dinv[:, :, :], 1.0).then_inc(s.step, 1)
                eng.memset(mv[:, :, :, :], 1.0).then_inc(s.step, 1)
                eng.wait_ge(s.step, 2)
                eng.sem_inc(s.summed, 2)
                for i, both in batches(eng, n, 1):
                    step = LoopOrder(eng, s.step, 6, i, 2)
                    for g, u in both:
                        m = tiles_of(g, n)
                        eng.wait_ge(s.free, freed(g))
                        eng.wait_ge((s.xh0_in, s.xh1_in)[u], (i + 1) * 32)
                        step(eng.scalar_tensor_tensor(x2[:, u, 0:m, :], h[:, u, 0:m, :], K.hgt_gate[:, 1:2], x[:, u, 0:m, :],
                                                      ALU.mult, ALU.add))
                        eng.wait_ge(s.turned_back, g + 1)
                        eng.tensor_tensor(x2[:, u, 0:m, :], x2[:, u, 0:m, :], by_tile(psO[u], m), ALU.add).then_inc(s.summed, 1)
                        eng.tensor_scalar(dinv[:, u, 0:m], K.dinv[:, slot_cols(g, n)], 0.0, None, ALU.add)
                    for g, u in both:
                        eng.wait_ge(s.summed, done(g))
                        stats_then_negated(eng, step, s.gate, x2[:, u, :, :], st[:, u, :, :], mv[:, u, :, :], tiles_of(g, n)
                                           ).then_inc(s.stats, 1)


def gcn_to_cat(nc, K):
    C = K.cols
    n = C // TILES
    SI = CAT_TYPES * CAT_S
    with ExitStack() as ctx:
        A = Buffers(nc, ctx, "to_cat")
        sums, own, x, x3, rows, out = (A.sb(m, [P, 2, TILES, D]) for m in ("sums", "own", "x", "x3", "rows", "out"))
        si = A.sb("si", [P, 2, TILES, SI])
        hT, zT, h7T, z7T = (A.sb(m, [P, 2, GROUP]) for m in ("hT", "zT", "h7T", "z7T"))
        st, mv = A.sb("st", [P, 2, TILES, 6]), A.sb("mv", [P, 2, TILES, 2])
        rstd, shift = A.sb("rstd", [P, 2, TILES]), A.sb("shift", [P, 2, TILES])
        ps6 = [A.ps(f"ps6{u}", [P, GROUP]) for u in range(2)]
        ps7 = [A.ps(f"ps7{u}", [P, GROUP]) for u in range(2)]
        psI = [A.ps(f"psI{u}", [P, TILES * SI]) for u in range(2)]
        s = A.sems((
            "in0", "in1", "x0_in", "x1_in", "scaled", "turned", "copiedT", "projected", "gelu_done", "turned_back", "x3_done",
            "stats", "powered", "rstd_ready", "normed", "turned7", "copied7", "projected7", "z7_ready", "rows_ready",
            "rows_done", "stored", "free", "step", "gate"))
        with nc.Block() as block:
            @block.sync
            def _(eng):
                def load(both):
                    for g, u in both:
                        m = tiles_of(g, n)
                        eng.wait_ge(s.turned, freed(g))
                        for to, of, first in ((sums, K.sums, 0), (own, K.tables[6], K.rows)):
                            eng.dma_start(to[:, u, 0:m, :], slot_rows(K, of, first, g)).then_inc((s.in0, s.in1)[u], 16)

                load(batch(0, n, 1))
                eng.sem_inc(s.free, 2)
                for i, ahead, begun, ending in transfers(eng, n, 1):
                    load(ahead)
                    for g, u in begun:
                        m = tiles_of(g, n)
                        eng.wait_ge(s.x3_done, freed(g))
                        eng.dma_start(x[:, u, 0:m, :], slot_rows(K, K.resid, 0, g)).then_inc((s.x0_in, s.x1_in)[u], 16)
                    for g, u in ending:
                        m = tiles_of(g, n)
                        eng.wait_ge(s.rows_done, done(g))
                        eng.dma_start(slot_rows(K, K.tables[7], K.rows, g), rows[:, u, 0:m, :]).then_inc(s.stored, 16)
                        eng.dma_start(slot_rows(K, K.resid, 0, g), out[:, u, 0:m, :]).then_inc(s.stored, 16)
                        eng.dma_start(slot_rows(K, K.cat_si, 0, g), si[:, u, 0:m, :]).then_inc(s.stored, 16)
                    if ending:
                        eng.wait_ge(s.stored, (i - 1) * 96 + 48 * len(ending))
                        eng.sem_inc(s.free, 2)

            @block.tensor
            def _(eng):
                eng.sem_inc(s.turned, 2)
                for i, begun, ending in overlapped(eng, n, 1):
                    for g, u in begun:
                        eng.wait_ge(s.scaled, g + 1)
                        eng.wait_ge(s.x3_done, freed(g))
                        turn_tiles(eng, K, ps6[u], sums[:, u, :, :], tiles_of(g, n)).then_inc(s.turned, 1)
                    for g, u in ending:
                        eng.wait_ge(s.normed, g + 1)
                        eng.wait_ge(s.rows_done, freed(g))
                        turn_tiles(eng, K, ps7[u], rows[:, u, :, :], tiles_of(g, n)).then_inc(s.turned7, 1)
                    for g, u in begun:
                        w = tiles_of(g, n) * P
                        eng.wait_ge(s.copiedT, g + 1)
                        eng.matmul(ps6[u][:, 0:w], K.gcn_w[:, :], hT[:, u, 0:w], start=True, stop=True).then_inc(s.projected, 1)
                    for g, u in ending:
                        w = tiles_of(g, n) * P
                        eng.wait_ge(s.copied7, g + 1)
                        eng.matmul(ps7[u][:, 0:w], K.cat_wu[:, 0, 0:D], h7T[:, u, 0:w], start=True, stop=True
                                   ).then_inc(s.projected7, 1)
                    for g, u in ending:
                        for t in range(tiles_of(g, n)):
                            eng.matmul(psI[u][:, t * SI:(t + 1) * SI], h7T[:, u, t * P:(t + 1) * P],
                                       K.cat_ui[:, :, :].rearrange("p t s -> p (t s)"), start=True, stop=True)
                    for g, u in begun:
                        eng.wait_ge(s.gelu_done, g + 1)
                        turn_back(eng, K, ps6[u], zT[:, u, :], tiles_of(g, n)).then_inc(s.turned_back, 1)
                    for g, u in ending:
                        eng.wait_ge(s.z7_ready, g + 1)
                        turn_back(eng, K, ps7[u], z7T[:, u, :], tiles_of(g, n)).then_inc(s.rows_ready, 1)

            @block.scalar
            def _(eng):
                eng.preload_act_table(ACT.Gelu)
                for i, begun, ending in overlapped(eng, n, 1):
                    for g, u in ending:
                        eng.wait_ge(s.rstd_ready, g + 1)
                        eng.wait_ge(s.free, freed(g))
                        norm_relu(eng, x3[:, u, :, :], rstd[:, u, :], shift[:, u, :], rows[:, u, :, :], tiles_of(g, n)
                                  ).then_inc(s.normed, 1)
                    for g, u in begun:
                        w = tiles_of(g, n) * P
                        eng.wait_ge(s.turned, done(g))
                        eng.activation(hT[:, u, 0:w], ps6[u][:, 0:w], ACT.Copy).then_inc(s.copiedT, 1)
                    for g, u in ending:
                        w = tiles_of(g, n) * P
                        eng.wait_ge(s.turned7, g + 1)
                        eng.activation(h7T[:, u, 0:w], ps7[u][:, 0:w], ACT.Copy).then_inc(s.copied7, 1)
                    for g, u in begun:
                        w = tiles_of(g, n) * P
                        eng.wait_ge(s.projected, g + 1)
                        eng.activation(zT[:, u, 0:w], ps6[u][:, 0:w], ACT.Gelu, bias=K.by_feature[:, 0:1]
                                       ).then_inc(s.gelu_done, 1)
                    for g, u in ending:
                        w = tiles_of(g, n) * P
                        eng.wait_ge(s.projected7, g + 1)
                        eng.activation(z7T[:, u, 0:w], ps7[u][:, 0:w], ACT.Identity, bias=K.by_feature[:, 1:2]
                                       ).then_inc(s.z7_ready, 1)

            @block.gpsimd
            def _(eng):
                for i, both in batches(eng, n, 1):
                    for g, u in both:
                        rstd_and_shift(eng, K, s, g, mv[:, u, :, :], rstd[:, u, :], shift[:, u, :])

            @block.vector
            def _(eng):
                eng.memset(mv[:, :, :, :], 1.0).then_inc(s.step, 1)
                eng.wait_ge(s.step, 1)
                eng.sem_inc(s.x3_done, 2)
                eng.sem_inc(s.rows_done, 2)
                for i, begun, ending in overlapped(eng, n, 1):
                    step = LoopOrder(eng, s.step, 6, i, 1 if isinstance(i, int) and i == 0 else -3)
                    for g, u in ending:
                        m = tiles_of(g, n)
                        eng.wait_ge((s.x0_in, s.x1_in)[u], i * 16)
                        eng.wait_ge(s.rows_done, freed(g))
                        eng.wait_ge(s.turned_back, g + 1)
                        eng.tensor_tensor(x3[:, u, 0:m, :], by_tile(ps6[u], m), x[:, u, 0:m, :], ALU.add).then_inc(s.x3_done, 1)
                    for g, u in ending:
                        eng.wait_ge(s.x3_done, done(g))
                        stats_then_negated(eng, step, s.gate, x3[:, u, :, :], st[:, u, :, :], mv[:, u, :, :], tiles_of(g, n)
                                           ).then_inc(s.stats, 1)
                    for g, u in begun:
                        m = tiles_of(g, n)
                        eng.wait_ge((s.in0, s.in1)[u], (i + 1) * 32)
                        step(eng.tensor_tensor(sums[:, u, 0:m, :], sums[:, u, 0:m, :], own[:, u, 0:m, :], ALU.add))
                        eng.tensor_tensor(sums[:, u, 0:m, :], sums[:, u, 0:m, :], spread(K.dinv[:, slot_cols(g, n)], 2, D),
                                          ALU.mult).then_inc(s.scaled, 1)
                    for g, u in ending:
                        m = tiles_of(g, n)
                        eng.wait_ge(s.rows_ready, g + 1)
                        eng.tensor_tensor(out[:, u, 0:m, :], by_tile(ps7[u], m), x3[:, u, 0:m, :], ALU.add)
                        eng.tensor_copy(si[:, u, 0:m, :], by_tile(psI[u], m, SI)).then_inc(s.rows_done, 1)


def leave_slots(nc, K, out):
    C = K.cols
    n = C // TILES
    with ExitStack() as ctx:
        A = Buffers(nc, ctx, "leave")
        at = A.sb("at", [P, 2, TILES], I32)
        sums, x, rows = (A.sb(m, [P, 2, TILES, D]) for m in ("sums", "x", "rows"))
        s = A.sems(("in0", "in1", "added", "indexed", "out0", "out1", "free", "gate"))
        with nc.Block() as block:
            @block.sync
            def _(eng):
                for i, both in batches(eng, n, 1):
                    for g, u in both:
                        m = tiles_of(g, n)
                        eng.wait_ge(s.added, freed(g))
                        eng.dma_start(sums[:, u, 0:m, :], slot_rows(K, K.sums, 0, g)).then_inc((s.in0, s.in1)[u], 16)
                        eng.dma_start(x[:, u, 0:m, :], slot_rows(K, K.resid, 0, g)).then_inc((s.in0, s.in1)[u], 16)

            @block.vector
            def _(eng):
                eng.sem_inc(s.added, 2)
                for i, both in batches(eng, n, 1):
                    for g, u in both:
                        m = tiles_of(g, n)
                        eng.wait_ge((s.in0, s.in1)[u], (i + 1) * 32)
                        eng.wait_ge(s.free, freed(g))
                        eng.tensor_tensor(rows[:, u, 0:m, :], sums[:, u, 0:m, :], x[:, u, 0:m, :], ALU.add).then_inc(s.added, 1)

            @block.gpsimd
            def _(eng):
                eng.sem_inc(s.free, 2)
                for i, both in batches(eng, n, 1):
                    for g, u in both:
                        m = tiles_of(g, n)
                        eng.wait_ge(s.free, freed(g))
                        eng.sem_inc(s.gate, 1)
                        eng.tensor_copy(at[:, u, 0:m], K.node_of[:, slot_cols(g, n)]).then_inc(s.indexed, 1)
                        eng.wait_ge(s.indexed, g + 1)
                        eng.wait_ge(s.added, done(g))
                        eng.sem_inc(s.gate, 1)
                        for t in range(m):
                            eng.indirect_dma_start(out, bass.IndirectOffsetOnAxis(ap=at[:, u, t:t + 1], axis=0),
                                                   rows[:, u, t, :], None, bounds_check=K.rows - 1,
                                                   oob_is_err=False).then_inc((s.out0, s.out1)[u], 16)
                    for g, u in both:
                        eng.wait_ge((s.out0, s.out1)[u], i * 16 * TILES + 16 * tiles_of(g, n))
                        eng.sem_inc(s.free, 1)


def gnn_stack(nc, I, out, rows, cols):
    L, C = GAT_LAYERS, cols
    with ExitStack() as ctx:
        A = Buffers(nc, ctx, "k")
        K = Kept(rows, cols)

        def dram(name, shape, dt=F32):
            return nc.dram_tensor(name, shape, dt, kind="Internal").ap()

        K.tables = [dram(f"table{l}", (rows + K.slots, ROWW if l < L else D)) for l in range(L + 3)]
        K.gat_out = dram("gat_out", (K.slots, D))
        K.hgt_q = dram("hgt_q", (K.slots, D))
        K.cat_si = dram("cat_si", (K.slots, CAT_TYPES * CAT_S))
        K.resid = dram("resid", (K.slots, D))
        K.sums = dram("sums", (K.slots, D))
        K.row_of = dram("row_of", (rows, 1), I32)

        sb = A.sb
        K.ones, K.ident, K.carry = (sb(n, [P, P]) for n in ("ones", "ident", "carry"))
        K.gat_wh = sb("gat_wh", [P, L, GAT_HEADS, D])
        K.gat_v, K.gat_u = sb("gat_v", [P, L, 4]), sb("gat_u", [P, L * GAT_HEADS, EDGE_F + 1])
        K.gat_bias, K.gat_bias_rep = sb("gat_bias", [P, L]), sb("gat_bias_rep", [P, L, D])
        K.gat_ewT = sb("gat_ewT", [GAT_HEADS * EDGE_F, L, D])
        K.hgt_wq, K.hgt_wa, K.hgt_ba = sb("hgt_wq", [P, D]), sb("hgt_wa", [P, D]), sb("hgt_ba", [P, D])
        K.hgt_gate = sb("hgt_gate", [P, 2])
        K.hgt_kv, K.hgt_kvb = sb("hgt_kv", [P, HGT_RELS, 2 * D]), sb("hgt_kvb", [P, HGT_RELS, 2 * D])
        K.gcn_w = sb("gcn_w", [P, D])
        K.by_feature = sb("by_feature", [P, 4])
        K.cat_wu, K.cat_ui = sb("cat_wu", [P, CAT_TYPES, D + CAT_S]), sb("cat_ui", [P, CAT_TYPES, CAT_S])
        K.cat_imp, K.cat_pk = sb("cat_imp", [P, CAT_TYPES]), sb("cat_pk", [P, CAT_CONF])
        K.minus_half = sb("minus_half", [P, TILES])
        K.slot_no, K.own, K.dinv = sb("slot_no", [P, C + 1]), sb("own", [P, C + 1]), sb("dinv", [P, C + 1])
        K.cont, K.goes_on, K.ends, K.restart, K.in_head, K.in_tail, K.inner = (
            sb(n, [P, C]) for n in ("cont", "goes_on", "ends", "restart", "in_head", "in_tail", "inner"))
        K.many = sb("many", [P, 1])
        K.seq_cont, K.seq_goes_on, K.seq_ends, K.seq_restart = (
            sb(n, [16, 2 * P]) for n in ("seq_cont", "seq_goes_on", "seq_ends", "seq_restart"))
        K.rel_mask, K.type_mask = sb("rel_mask", [P, HGT_RELS, C]), sb("type_mask", [P, CAT_TYPES, C])
        K.node_of, K.gather_dst = sb("node_of", [P, C + 1], I32), sb("gather_dst", [P, C + 1], I32)
        K.src_row, K.dst_slot = (sb(n, [P, C], I32) for n in ("src_row", "dst_slot"))
        K.part_slot, K.part_row = sb("part_slot", [P, 1], I32), sb("part_row", [P, 1], I32)
        K.sc, K.sc_next = sb("sc_a", [P, 4, C + 1]), sb("sc_b", [P, 4, C + 1])
        with ExitStack() as first_ctx:
            F = Buffers(nc, first_ctx, "first")
            K.from_prev, K.from_next, K.upper = (F.sb(n, [P, P]) for n in ("from_prev", "from_next", "upper"))
            K.gat_wm = F.sb("gat_wm", [P, L, D])
            K.slot_row = F.sb("slot_row", [P, C + 1], I32)
            K.src_node = F.sb("src_node", [P, C], I32)
            prepare_weights(nc, K, I)
            describe_slots(nc, K, I)
            map_rows(nc, K)
            node_pass(nc, K, I, out)
            enter_slots(nc, K)
        with ExitStack() as rows_ctx:
            G = rows_ctx.enter_context(nc.sbuf_tensor("source_rows", [P, C + 1, D], F32))
            with ExitStack() as gat_ctx:
                B = Buffers(nc, gat_ctx, "gat")
                src_score, alpha = B.sb("src_score", [P, GAT_HEADS, C]), B.sb("alpha", [P, GAT_HEADS, C])
                alpha_self = B.sb("alpha_self", [P, GAT_HEADS, C + 1])
                for l in range(L):
                    gather_rows(nc, K, l, K.tables[l], ROWW, G, src_score)
                    gat_weights(nc, K, I, l, src_score, alpha, alpha_self)
                    gat_slots(nc, K, I, l, G, alpha, alpha_self)
                    gat_extra(nc, K, l, alpha_self)
                    K.sc, K.sc_next = K.sc_next, K.sc
            gat_to_hgt(nc, K, I)
            with ExitStack() as hgt_ctx:
                score = Buffers(nc, hgt_ctx, "hgt_s").sb("score", [P, HGT_HEADS, C])
                typed_edges(nc, K, "hgt", G, score)
                typed_weights(nc, K, "hgt", score)
                run_sums(nc, K, "hgt_sums", G, score, HGT_HEADS)
            hgt_to_gcn(nc, K)
            gather_rows(nc, K, 6, K.tables[6], D, G)
            run_sums(nc, K, "gcn_sums", G, None, 1)
            gcn_to_cat(nc, K)
            with ExitStack() as cat_ctx:
                score = Buffers(nc, cat_ctx, "cat_s").sb("score", [P, CAT_HEADS, C])
                typed_edges(nc, K, "cat", G, score)
                typed_weights(nc, K, "cat", score)
                run_sums(nc, K, "cat_sums", G, score, CAT_HEADS)
        leave_slots(nc, K, out)


_NAMES = dict(
    x="x", gat_w="L0_gnn_weights", gat_att="L0_gnn_atts", gat_b="L0_gnn_biases", gat_ew="L0_gnn_edge_ws",
    gat_eb="L0_gnn_edge_bs", hgt_wk="L1_gnn_Wk", hgt_bk="L1_gnn_bk", hgt_wq="L1_gnn_Wq", hgt_bq="L1_gnn_bq",
    hgt_wv="L1_gnn_Wv", hgt_bv="L1_gnn_bv", hgt_a="L1_gnn_a_rel", hgt_m="L1_gnn_m_rel", hgt_p="L1_gnn_p_rel",
    hgt_wa="L1_gnn_Wa", hgt_ba="L1_gnn_ba", hgt_skip="L1_gnn_skip", gcn_w="L2_gnn_W", gcn_b="L2_gnn_b",
    cat_w="L3_gnn_W", cat_att="L3_gnn_att_vectors", cat_conf="L3_gnn_confounder_probs",
    cat_imp="L3_gnn_edge_importance", cat_b="L3_gnn_bias")


def kernel(**inputs):
    import numpy as np
    import concourse.bacc as bacc
    from concourse.bass_utils import run_bass_kernel_spmd as run

    n_nodes, n_edges = inputs["x"].shape[0], inputs["src"].shape[0]
    block = BLOCKS * BLOCK
    rows = (n_nodes + 1 + block - 1) // block * block
    cols = (n_edges + P * TILES - 1) // (P * TILES) * TILES
    fill = P * cols - n_edges

    def edges(a, value=0):
        a = np.asarray(a)
        tail = np.full((fill,) + a.shape[1:], value, a.dtype)
        return np.concatenate([a, tail]).reshape((P, cols) + a.shape[1:])

    arrays = {k: np.ascontiguousarray(np.asarray(inputs[v])) for k, v in _NAMES.items()}
    arrays["x"] = np.concatenate([arrays["x"], np.zeros((rows - n_nodes, D), arrays["x"].dtype)])
    arrays["hgt_skip"] = arrays["hgt_skip"].reshape(1, 1)
    arrays["src"], arrays["dst"] = edges(inputs["src"]), edges(inputs["dst"], n_nodes)
    arrays["type2"], arrays["type4"] = edges(inputs["edge_type_2"]), edges(inputs["edge_type_4"])
    arrays["edge_x"] = edges(inputs["edge_attr_16"])

    nc = bacc.Bacc("TRN2", target_bir_lowering=False, num_devices=1)
    I = named({k: nc.dram_tensor(f"in_{k}", a.shape, mybir.dt.from_np(a.dtype), kind="ExternalInput").ap()
                           for k, a in arrays.items()})
    out = nc.dram_tensor("out", (rows, D), F32, kind="ExternalOutput").ap()
    gnn_stack(nc, I, out, rows, cols)
    got = run(nc, [{f"in_{k}": a for k, a in arrays.items()}], core_ids=[0])
    return got.results[0]["out"][:n_nodes]
```
